# Optimizing a Trainium2 kernel written in Bass

```python
import numpy as np
import jax
import jax.numpy as jnp

def _softmax(x, axis=-1):
    return jax.nn.softmax(x, axis=axis)

def _gelu(x):
    return jax.nn.gelu(x, approximate=True)

def _silu(x):
    return jax.nn.silu(x)

def _sigmoid(x):
    return jax.nn.sigmoid(x)

def _layernorm(x, axis=-1, eps=1e-05):
    m = jnp.mean(x, axis=axis, keepdims=True)
    v = jnp.var(x, axis=axis, keepdims=True)
    return (x - m) / jnp.sqrt(v + eps)

def _scatter_add(tgt, idx, src, axis=0):
    return tgt.at[idx].add(src)

def _segment_sum(src, seg, n):
    return jax.ops.segment_sum(src, seg, n)
kernel_name = 'mk_decoder_preln_d2_seqx_r8_676126'

def setup_inputs(seed: int=0):
    np.random.seed(seed)
    _w = jnp.asarray

    def _rec_inputs():
        import jax
        import jax.numpy as jnp
        _rk = jax.random.key(seed)
        x = 7.22e-05 + 1 * jax.random.normal(jax.random.fold_in(_rk, 1), (4, 256, 256), jnp.float32)
        _lenS = 256 - jax.random.randint(jax.random.fold_in(_rk, 7), (4,), 0, max(1, 256 // 4) + 1, jnp.int32)
        _lenS2 = 256 - jax.random.randint(jax.random.fold_in(_rk, 8), (4,), 0, max(1, 256 // 4) + 1, jnp.int32)
        _ctx_1024P = jax.random.normal(jax.random.fold_in(_rk, 11), (4, 16, 128), jnp.float32)
        _ctx_1024c = jax.random.dirichlet(jax.random.fold_in(_rk, 511), 0.3 * jnp.ones((16,), jnp.float32), (4, 256))
        _ctx_1024t = jnp.einsum('bsk,bkd->bsd', _ctx_1024c, _ctx_1024P)
        _ctx_1024t = _ctx_1024t * jax.lax.rsqrt(jnp.mean(jnp.square(_ctx_1024t)) + 1e-12) * 0.953939
        ctx_1024 = 2.81802e-05 + 1.00001 * (_ctx_1024t + 0.3 * jax.random.normal(jax.random.fold_in(_rk, 611), (4, 256, 128), jnp.float32))
        _validS = jnp.arange(256)[None, :] < _lenS[:, None]
        _validS2 = jnp.arange(256)[None, :] < _lenS2[:, None]
        _causal = jnp.tril(jnp.ones((256, 256), dtype=bool))
        mask_BxS2_bf1 = jnp.ones((4, 256), dtype=bool)
        return (x, ctx_1024, mask_BxS2_bf1)
    x, ctx_1024, mask_BxS2_bf1 = _rec_inputs()

    def _L0_attn_setup():
        import jax, jax.numpy as jnp
        import numpy as np
        NUM_HEADS = 16
        LN_EPS = 1e-05

        def _rope(x):
            S, D = (x.shape[-2], x.shape[-1])
            rot = D // 2
            inv_freq = 1.0 / 10000.0 ** (jnp.arange(0, rot, 2, dtype=jnp.float32) / rot)
            ang = jnp.arange(S, dtype=jnp.float32)[:, None] * inv_freq[None, :]
            ang = jnp.repeat(ang, 2, axis=-1)
            cos, sin = (jnp.cos(ang), jnp.sin(ang))
            xr, xp = (x[..., :rot], x[..., rot:])
            x1, x2 = (xr[..., 0::2], xr[..., 1::2])
            rot_half = jnp.stack((-x2, x1), axis=-1).reshape(xr.shape)
            xr = xr * cos + rot_half * sin
            return jnp.concatenate([xr, xp], axis=-1)
        key = jax.random.key(seed)
        k1, k2, k3 = jax.random.split(key, 3)
        B, S, D = (4, 256, 256)
        X = jax.random.normal(k1, (B, S, D), dtype=jnp.float32)
        ln_w = jnp.ones((D,), dtype=jnp.float32)
        ln_b = jnp.zeros((D,), dtype=jnp.float32)
        W_in = jax.random.normal(k2, (D, 3 * D), dtype=jnp.float32) * 0.02
        W_out = jax.random.normal(k3, (D, D), dtype=jnp.float32) * 0.02
        return {'X': X, 'ln_w': ln_w, 'ln_b': ln_b, 'W_in': W_in, 'W_out': W_out}
    _L0_attn_all = _L0_attn_setup()
    _L0_attn_in = {k: v for k, v in _L0_attn_all.items() if k in ('ln_w', 'ln_b', 'W_in', 'W_out')}
    del _L0_attn_all

    def _L0_xattn_setup():
        import jax, jax.numpy as jnp
        import numpy as np
        key = jax.random.key(seed)
        ks = jax.random.split(key, 6)
        B, L, N, C, D = (8, 64, 256, 128, 128)
        return {'teacher_logits': jax.random.normal(ks[0], (B, L, N), dtype=jnp.float32), 'teacher_features': jax.random.normal(ks[1], (B, N, C), dtype=jnp.float32), 'Wq': jax.random.normal(ks[2], (D, C), dtype=jnp.float32) * (1.0 / np.sqrt(C)), 'bq': jnp.zeros((D,), dtype=jnp.float32), 'Wk': jax.random.normal(ks[3], (D, C), dtype=jnp.float32) * (1.0 / np.sqrt(C)), 'bk': jnp.zeros((D,), dtype=jnp.float32)}
    _L0_xattn_all = _L0_xattn_setup()
    _L0_xattn_in = {k: v for k, v in _L0_xattn_all.items() if k in ('Wq', 'bq', 'Wk', 'bk')}
    del _L0_xattn_all

    def _L0_ffn_setup():
        import jax, jax.numpy as jnp
        import numpy as np
        H = 256
        I = 128
        E = 32
        K = 4
        N_SHARED = 1
        EPS = 1e-06

        def _rmsnorm(x, w, eps=EPS):
            var = jnp.mean(jnp.square(x), axis=-1, keepdims=True)
            return x * jax.lax.rsqrt(var + eps) * w

        def _moe_core(x, gate_w, w13, w2):
            T = x.shape[0]
            N = T * K
            C = 2 * N // E
            logits = jnp.einsum('th,eh->te', x.astype(jnp.float32), gate_w.astype(jnp.float32))
            scores = jax.nn.softmax(logits, axis=-1)
            topk_w, topk_ids = jax.lax.top_k(scores, K)
            topk_w = topk_w / jnp.sum(topk_w, axis=-1, keepdims=True)
            flat_ids = topk_ids.reshape(-1)
            flat_w = topk_w.reshape(-1)
            order = jnp.argsort(flat_ids)
            sorted_eid = flat_ids[order]
            tok = order // K
            counts = jnp.zeros((E,), jnp.int32).at[flat_ids].add(1)
            starts = jnp.cumsum(counts) - counts
            pos = jnp.arange(N) - starts[sorted_eid]
            buf = jnp.zeros((E, C, x.shape[1]), x.dtype).at[sorted_eid, pos].set(x[tok], mode='drop')
            gu = jnp.einsum('ech,ehf->ecf', buf, w13)
            g, u = jnp.split(gu, 2, axis=-1)
            act = jax.nn.silu(g) * u
            eo = jnp.einsum('eci,eih->ech', act, w2)
            out_slots = eo[sorted_eid, pos]
            routed = jnp.zeros_like(x).at[tok].add(out_slots * flat_w[order][:, None])
            return routed
        key = jax.random.key(seed)
        ks = jax.random.split(key, 8)
        s = 1.0 / np.sqrt(H)
        si = 1.0 / np.sqrt(I)
        return {'hidden_states': jax.random.normal(ks[0], (1, 512, H), jnp.float32), 'norm_w': jnp.ones((H,), jnp.float32), 'gate_w': jax.random.normal(ks[1], (E, H), jnp.float32) * s, 'w13': jax.random.normal(ks[2], (E, H, 2 * I), jnp.float32) * s, 'w2': jax.random.normal(ks[3], (E, I, H), jnp.float32) * si, 'shared_gate_w': jax.random.normal(ks[4], (H, I * N_SHARED), jnp.float32) * s, 'shared_up_w': jax.random.normal(ks[5], (H, I * N_SHARED), jnp.float32) * s, 'shared_down_w': jax.random.normal(ks[6], (I * N_SHARED, H), jnp.float32) * si}
    _L0_ffn_all = _L0_ffn_setup()
    _L0_ffn_in = {k: v for k, v in _L0_ffn_all.items() if k in ('norm_w', 'gate_w', 'w13', 'w2', 'shared_gate_w', 'shared_up_w', 'shared_down_w')}
    del _L0_ffn_all

    def _L1_attn_setup():
        import jax, jax.numpy as jnp
        import numpy as np
        D_MODEL = 256
        STATE = 16
        KCONV = 4
        EXPAND = 2
        D_INNER = D_MODEL * EXPAND
        EPS = 1e-05

        def _silu(v):
            return v * jax.nn.sigmoid(v)
        key = jax.random.key(seed)
        ks = jax.random.split(key, 10)
        s = 0.02
        x = jax.random.normal(ks[0], (2, 256, D_MODEL), dtype=jnp.float32)
        norm_w = jnp.ones((D_MODEL,), jnp.float32)
        in_proj_w = jax.random.normal(ks[1], (D_INNER * 2, D_MODEL), jnp.float32) * s
        conv_w = jax.random.normal(ks[2], (D_INNER, 1, KCONV), jnp.float32) * s
        conv_b = jnp.zeros((D_INNER,), jnp.float32)
        x_proj_w = jax.random.normal(ks[3], (STATE * 2 + 1, D_INNER), jnp.float32) * s
        dt_w = jax.random.normal(ks[4], (D_INNER, 1), jnp.float32) * s
        dt_b = jnp.zeros((D_INNER,), jnp.float32)
        A_log = jnp.log(jnp.broadcast_to(jnp.arange(1, STATE + 1, dtype=jnp.float32)[None, :], (D_INNER, STATE)))
        D_param = jnp.ones((D_INNER,), jnp.float32)
        out_proj_w = jax.random.normal(ks[5], (D_MODEL, D_INNER), jnp.float32) * s
        return {'x': x, 'norm_w': norm_w, 'in_proj_w': in_proj_w, 'conv_w': conv_w, 'conv_b': conv_b, 'x_proj_w': x_proj_w, 'dt_w': dt_w, 'dt_b': dt_b, 'A_log': A_log, 'D_param': D_param, 'out_proj_w': out_proj_w}
    _L1_attn_all = _L1_attn_setup()
    _L1_attn_in = {k: v for k, v in _L1_attn_all.items() if k in ('norm_w', 'in_proj_w', 'conv_w', 'conv_b', 'x_proj_w', 'dt_w', 'dt_b', 'A_log', 'D_param', 'out_proj_w')}
    del _L1_attn_all

    def _L1_xattn_setup():
        import jax, jax.numpy as jnp
        import numpy as np
        N_HEADS = 16
        N_KV_HEADS = 8
        HEAD_DIM = 128
        D_TEXT = 256
        D_VISION = 128
        GROUPS = N_HEADS // N_KV_HEADS
        key = jax.random.key(seed)
        ks = jax.random.split(key, 6)
        B, T_text, T_vis = (4, 256, 72)
        text_hidden = jax.random.normal(ks[0], (B, T_text, D_TEXT), dtype=jnp.float32)
        vision_tokens = jax.random.normal(ks[1], (B, T_vis, D_VISION), dtype=jnp.float32)
        vision_mask = jnp.ones((B, T_vis), dtype=bool)
        s = 0.02
        Wq = jax.random.normal(ks[2], (D_TEXT, N_HEADS * HEAD_DIM), dtype=jnp.float32) * s
        Wk = jax.random.normal(ks[3], (D_VISION, N_KV_HEADS * HEAD_DIM), dtype=jnp.float32) * s
        Wv = jax.random.normal(ks[4], (D_VISION, N_KV_HEADS * HEAD_DIM), dtype=jnp.float32) * s
        Wo = jax.random.normal(ks[5], (N_HEADS * HEAD_DIM, D_TEXT), dtype=jnp.float32) * s
        return {'text_hidden': text_hidden, 'vision_tokens': vision_tokens, 'vision_mask': vision_mask, 'Wq': Wq, 'Wk': Wk, 'Wv': Wv, 'Wo': Wo}
    _L1_xattn_all = _L1_xattn_setup()
    _L1_xattn_in = {k: v for k, v in _L1_xattn_all.items() if k in ('Wq', 'Wk', 'Wv', 'Wo')}
    del _L1_xattn_all

    def _L1_ffn_setup():
        import jax, jax.numpy as jnp
        import numpy as np
        B, S, H = (2, 128, 256)
        E, K = (8, 2)
        F = 176
        FS = 704
        NORM_TOPK = False

        def _swiglu(x, wg, wu, wd):
            return jax.nn.silu(x @ wg) * (x @ wu) @ wd
        key = jax.random.key(seed)
        ks = jax.random.split(key, 9)
        s = 0.02
        return {'hidden_states': jax.random.normal(ks[0], (B, S, H), dtype=jnp.float32), 'Wr': jax.random.normal(ks[1], (H, E), dtype=jnp.float32) * s, 'Wg': jax.random.normal(ks[2], (E, H, F), dtype=jnp.float32) * s, 'Wu': jax.random.normal(ks[3], (E, H, F), dtype=jnp.float32) * s, 'Wd': jax.random.normal(ks[4], (E, F, H), dtype=jnp.float32) * s, 'Sg': jax.random.normal(ks[5], (H, FS), dtype=jnp.float32) * s, 'Su': jax.random.normal(ks[6], (H, FS), dtype=jnp.float32) * s, 'Sd': jax.random.normal(ks[7], (FS, H), dtype=jnp.float32) * s, 'Wsg': jax.random.normal(ks[8], (H, 1), dtype=jnp.float32) * s}
    _L1_ffn_all = _L1_ffn_setup()
    _L1_ffn_in = {k: v for k, v in _L1_ffn_all.items() if k in ('Wr', 'Wg', 'Wu', 'Wd', 'Sg', 'Su', 'Sd', 'Wsg')}
    del _L1_ffn_all
    return {'x': x, 'ctx_1024': ctx_1024, 'mask_BxS2_bf1': mask_BxS2_bf1, 'L0_attn_ln_w': _L0_attn_in['ln_w'], 'L0_attn_ln_b': _L0_attn_in['ln_b'], 'L0_attn_W_in': _L0_attn_in['W_in'], 'L0_attn_W_out': _L0_attn_in['W_out'], 'L0_xattn_Wq': _L0_xattn_in['Wq'], 'L0_xattn_bq': _L0_xattn_in['bq'], 'L0_xattn_Wk': _L0_xattn_in['Wk'], 'L0_xattn_bk': _L0_xattn_in['bk'], 'L0_ffn_norm_w': _L0_ffn_in['norm_w'], 'L0_ffn_gate_w': _L0_ffn_in['gate_w'], 'L0_ffn_w13': _L0_ffn_in['w13'], 'L0_ffn_w2': _L0_ffn_in['w2'], 'L0_ffn_shared_gate_w': _L0_ffn_in['shared_gate_w'], 'L0_ffn_shared_up_w': _L0_ffn_in['shared_up_w'], 'L0_ffn_shared_down_w': _L0_ffn_in['shared_down_w'], 'L1_attn_norm_w': _L1_attn_in['norm_w'], 'L1_attn_in_proj_w': _L1_attn_in['in_proj_w'], 'L1_attn_conv_w': _L1_attn_in['conv_w'], 'L1_attn_conv_b': _L1_attn_in['conv_b'], 'L1_attn_x_proj_w': _L1_attn_in['x_proj_w'], 'L1_attn_dt_w': _L1_attn_in['dt_w'], 'L1_attn_dt_b': _L1_attn_in['dt_b'], 'L1_attn_A_log': _L1_attn_in['A_log'], 'L1_attn_D_param': _L1_attn_in['D_param'], 'L1_attn_out_proj_w': _L1_attn_in['out_proj_w'], 'L1_xattn_Wq': _L1_xattn_in['Wq'], 'L1_xattn_Wk': _L1_xattn_in['Wk'], 'L1_xattn_Wv': _L1_xattn_in['Wv'], 'L1_xattn_Wo': _L1_xattn_in['Wo'], 'L1_ffn_Wr': _L1_ffn_in['Wr'], 'L1_ffn_Wg': _L1_ffn_in['Wg'], 'L1_ffn_Wu': _L1_ffn_in['Wu'], 'L1_ffn_Wd': _L1_ffn_in['Wd'], 'L1_ffn_Sg': _L1_ffn_in['Sg'], 'L1_ffn_Su': _L1_ffn_in['Su'], 'L1_ffn_Sd': _L1_ffn_in['Sd'], 'L1_ffn_Wsg': _L1_ffn_in['Wsg']}

def reference(x, ctx_1024, mask_BxS2_bf1, L0_attn_ln_w, L0_attn_ln_b, L0_attn_W_in, L0_attn_W_out, L0_xattn_Wq, L0_xattn_bq, L0_xattn_Wk, L0_xattn_bk, L0_ffn_norm_w, L0_ffn_gate_w, L0_ffn_w13, L0_ffn_w2, L0_ffn_shared_gate_w, L0_ffn_shared_up_w, L0_ffn_shared_down_w, L1_attn_norm_w, L1_attn_in_proj_w, L1_attn_conv_w, L1_attn_conv_b, L1_attn_x_proj_w, L1_attn_dt_w, L1_attn_dt_b, L1_attn_A_log, L1_attn_D_param, L1_attn_out_proj_w, L1_xattn_Wq, L1_xattn_Wk, L1_xattn_Wv, L1_xattn_Wo, L1_ffn_Wr, L1_ffn_Wg, L1_ffn_Wu, L1_ffn_Wd, L1_ffn_Sg, L1_ffn_Su, L1_ffn_Sd, L1_ffn_Wsg):
    import jax
    import jax.numpy as jnp

    def _L0_attn_ref(X, ln_w, ln_b, W_in, W_out):
        import jax, jax.numpy as jnp
        import numpy as np
        NUM_HEADS = 16
        LN_EPS = 1e-05

        def _rope(x):
            S, D = (x.shape[-2], x.shape[-1])
            rot = D // 2
            inv_freq = 1.0 / 10000.0 ** (jnp.arange(0, rot, 2, dtype=jnp.float32) / rot)
            ang = jnp.arange(S, dtype=jnp.float32)[:, None] * inv_freq[None, :]
            ang = jnp.repeat(ang, 2, axis=-1)
            cos, sin = (jnp.cos(ang), jnp.sin(ang))
            xr, xp = (x[..., :rot], x[..., rot:])
            x1, x2 = (xr[..., 0::2], xr[..., 1::2])
            rot_half = jnp.stack((-x2, x1), axis=-1).reshape(xr.shape)
            xr = xr * cos + rot_half * sin
            return jnp.concatenate([xr, xp], axis=-1)
        B, S, D = X.shape
        H = NUM_HEADS
        Dh = D // H
        mu = jnp.mean(X, axis=-1, keepdims=True)
        var = jnp.mean(jnp.square(X - mu), axis=-1, keepdims=True)
        Xn = (X - mu) * jax.lax.rsqrt(var + LN_EPS) * ln_w + ln_b
        qkv = jnp.einsum('bsd,df->bsf', Xn, W_in)
        Q, K, V = jnp.split(qkv, 3, axis=-1)
        Q = Q.reshape(B, S, H, Dh).transpose(0, 2, 1, 3)
        K = K.reshape(B, S, H, Dh).transpose(0, 2, 1, 3)
        V = V.reshape(B, S, H, Dh).transpose(0, 2, 1, 3)
        Q, K = (_rope(Q), _rope(K))
        scores = jnp.einsum('bhqd,bhkd->bhqk', Q, K) / jnp.sqrt(jnp.float32(Dh))
        probs = jax.nn.softmax(scores, axis=-1)
        ctx = jnp.einsum('bhqk,bhkd->bhqd', probs, V)
        ctx = ctx.transpose(0, 2, 1, 3).reshape(B, S, D)
        out = jnp.einsum('bsd,df->bsf', ctx, W_out)
        return out + X

    def _L0_xattn_ref(teacher_logits, teacher_features, Wq, bq, Wk, bk):
        import jax, jax.numpy as jnp
        import numpy as np
        query = jnp.einsum('bnc,dc->bnd', teacher_features, Wq) + bq
        key = jnp.einsum('bnc,dc->bnd', teacher_features, Wk) + bk
        energy = jnp.einsum('bnd,bmd->bnm', query, key)
        attention = jax.nn.softmax(energy, axis=-1)
        x_m = jnp.einsum('bln,bmn->blm', teacher_logits, attention)
        return x_m

    def _L0_ffn_ref(hidden_states, norm_w, gate_w, w13, w2, shared_gate_w, shared_up_w, shared_down_w):
        import jax, jax.numpy as jnp
        import numpy as np
        H = 256
        I = 128
        E = 32
        K = 4
        N_SHARED = 1
        EPS = 1e-06

        def _rmsnorm(x, w, eps=EPS):
            var = jnp.mean(jnp.square(x), axis=-1, keepdims=True)
            return x * jax.lax.rsqrt(var + eps) * w

        def _moe_core(x, gate_w, w13, w2):
            T = x.shape[0]
            N = T * K
            C = 2 * N // E
            logits = jnp.einsum('th,eh->te', x.astype(jnp.float32), gate_w.astype(jnp.float32))
            scores = jax.nn.softmax(logits, axis=-1)
            topk_w, topk_ids = jax.lax.top_k(scores, K)
            topk_w = topk_w / jnp.sum(topk_w, axis=-1, keepdims=True)
            flat_ids = topk_ids.reshape(-1)
            flat_w = topk_w.reshape(-1)
            order = jnp.argsort(flat_ids)
            sorted_eid = flat_ids[order]
            tok = order // K
            counts = jnp.zeros((E,), jnp.int32).at[flat_ids].add(1)
            starts = jnp.cumsum(counts) - counts
            pos = jnp.arange(N) - starts[sorted_eid]
            buf = jnp.zeros((E, C, x.shape[1]), x.dtype).at[sorted_eid, pos].set(x[tok], mode='drop')
            gu = jnp.einsum('ech,ehf->ecf', buf, w13)
            g, u = jnp.split(gu, 2, axis=-1)
            act = jax.nn.silu(g) * u
            eo = jnp.einsum('eci,eih->ech', act, w2)
            out_slots = eo[sorted_eid, pos]
            routed = jnp.zeros_like(x).at[tok].add(out_slots * flat_w[order][:, None])
            return routed
        B, S, Hd = hidden_states.shape
        residual = hidden_states
        h = _rmsnorm(hidden_states, norm_w)
        x = h.reshape(-1, Hd)
        routed = _moe_core(x, gate_w, w13, w2)
        shared = jax.nn.silu(x @ shared_gate_w) * (x @ shared_up_w) @ shared_down_w
        out = residual + (routed + shared).reshape(B, S, Hd)
        return out

    def _L1_attn_ref(x, norm_w, in_proj_w, conv_w, conv_b, x_proj_w, dt_w, dt_b, A_log, D_param, out_proj_w):
        import jax, jax.numpy as jnp
        import numpy as np
        D_MODEL = 256
        STATE = 16
        KCONV = 4
        EXPAND = 2
        D_INNER = D_MODEL * EXPAND
        EPS = 1e-05

        def _silu(v):
            return v * jax.nn.sigmoid(v)
        residual = x
        xn = x * jax.lax.rsqrt(jnp.mean(x * x, axis=-1, keepdims=True) + EPS) * norm_w
        xz = jnp.einsum('bld,ed->ble', xn, in_proj_w)
        x_inner, z = jnp.split(xz, 2, axis=-1)
        xc = jnp.transpose(x_inner, (0, 2, 1))
        xc = jax.lax.conv_general_dilated(xc, conv_w, window_strides=(1,), padding=[(KCONV - 1, 0)], dimension_numbers=('NCH', 'OIH', 'NCH'), feature_group_count=D_INNER)
        xc = xc + conv_b[None, :, None]
        xc = _silu(jnp.transpose(xc, (0, 2, 1)))
        x_ssm = jnp.einsum('bld,ed->ble', xc, x_proj_w)
        dt = jax.nn.softplus(x_ssm[..., -1:] * dt_w[:, 0] + dt_b)
        B_p = x_ssm[..., :STATE]
        C_p = x_ssm[..., STATE:2 * STATE]
        A = -jnp.exp(A_log)
        batch = x.shape[0]
        h0 = jnp.zeros((batch, D_INNER, STATE), x.dtype)

        def step(h, inp):
            dt_t, B_t, C_t, u_t = inp
            dA = jnp.exp(dt_t[..., None] * A)
            h = dA * h + (dt_t * u_t)[..., None] * B_t[:, None, :]
            y_t = jnp.sum(h * C_t[:, None, :], axis=-1) + D_param * u_t
            return (h, y_t)
        seq_first = lambda a: jnp.swapaxes(a, 0, 1)
        _, ys = jax.lax.scan(step, h0, (seq_first(dt), seq_first(B_p), seq_first(C_p), seq_first(xc)))
        y = jnp.swapaxes(ys, 0, 1)
        y = y * _silu(z)
        return jnp.einsum('ble,de->bld', y, out_proj_w) + residual

    def _L1_xattn_ref(text_hidden, vision_tokens, vision_mask, Wq, Wk, Wv, Wo):
        import jax, jax.numpy as jnp
        import numpy as np
        N_HEADS = 16
        N_KV_HEADS = 8
        HEAD_DIM = 128
        D_TEXT = 256
        D_VISION = 128
        GROUPS = N_HEADS // N_KV_HEADS
        B, T_text, _ = text_hidden.shape
        T_vis = vision_tokens.shape[1]
        scale = jnp.float32(np.sqrt(HEAD_DIM))
        q = (text_hidden @ Wq).reshape(B, T_text, N_HEADS, HEAD_DIM).transpose(0, 2, 1, 3)
        k = (vision_tokens @ Wk).reshape(B, T_vis, N_KV_HEADS, HEAD_DIM).transpose(0, 2, 1, 3)
        v = (vision_tokens @ Wv).reshape(B, T_vis, N_KV_HEADS, HEAD_DIM).transpose(0, 2, 1, 3)
        k = jnp.repeat(k, GROUPS, axis=1)
        v = jnp.repeat(v, GROUPS, axis=1)
        scores = jnp.einsum('bhtd,bhsd->bhts', q, k) / scale
        mask = vision_mask[:, None, None, :]
        scores = jnp.where(mask, scores, -jnp.inf)
        attn = jax.nn.softmax(scores, axis=-1)
        attn = jnp.nan_to_num(attn, nan=0.0)
        out = jnp.einsum('bhts,bhsd->bhtd', attn, v)
        out = out.transpose(0, 2, 1, 3).reshape(B, T_text, N_HEADS * HEAD_DIM)
        return out @ Wo

    def _L1_ffn_ref(hidden_states, Wr, Wg, Wu, Wd, Sg, Su, Sd, Wsg):
        import jax, jax.numpy as jnp
        import numpy as np
        B, S, H = (2, 128, 256)
        E, K = (8, 2)
        F = 176
        FS = 704
        NORM_TOPK = False

        def _swiglu(x, wg, wu, wd):
            return jax.nn.silu(x @ wg) * (x @ wu) @ wd
        b, s, h = hidden_states.shape
        x = hidden_states.reshape(-1, h)
        router_logits = x @ Wr
        probs = jax.nn.softmax(router_logits.astype(jnp.float32), axis=-1)
        routing_weights, selected = jax.lax.top_k(probs, K)
        if NORM_TOPK:
            routing_weights = routing_weights / routing_weights.sum(-1, keepdims=True)
        routing_weights = routing_weights.astype(x.dtype)
        C = jnp.einsum('tk,tke->te', routing_weights, jax.nn.one_hot(selected, E, dtype=x.dtype))
        expert_out = jax.vmap(lambda wg, wu, wd: _swiglu(x, wg, wu, wd))(Wg, Wu, Wd)
        moe_out = jnp.einsum('te,eth->th', C, expert_out)
        shared = _swiglu(x, Sg, Su, Sd)
        shared = jax.nn.sigmoid(x @ Wsg) * shared
        out = (moe_out + shared).reshape(b, s, h)
        return out
    x = x + _L0_attn_ref(_layernorm(x, axis=-1), L0_attn_ln_w, L0_attn_ln_b, L0_attn_W_in, L0_attn_W_out)
    x = x + _L0_xattn_ref(_layernorm(x, axis=-1), ctx_1024, L0_xattn_Wq, L0_xattn_bq, L0_xattn_Wk, L0_xattn_bk)
    x = x + _L0_ffn_ref(_layernorm(x, axis=-1), L0_ffn_norm_w, L0_ffn_gate_w, L0_ffn_w13, L0_ffn_w2, L0_ffn_shared_gate_w, L0_ffn_shared_up_w, L0_ffn_shared_down_w)
    x = x + _L1_attn_ref(_layernorm(x, axis=-1), L1_attn_norm_w, L1_attn_in_proj_w, L1_attn_conv_w, L1_attn_conv_b, L1_attn_x_proj_w, L1_attn_dt_w, L1_attn_dt_b, L1_attn_A_log, L1_attn_D_param, L1_attn_out_proj_w)
    x = x + _L1_xattn_ref(_layernorm(x, axis=-1), ctx_1024, mask_BxS2_bf1, L1_xattn_Wq, L1_xattn_Wk, L1_xattn_Wv, L1_xattn_Wo)
    x = x + _L1_ffn_ref(_layernorm(x, axis=-1), L1_ffn_Wr, L1_ffn_Wg, L1_ffn_Wu, L1_ffn_Wd, L1_ffn_Sg, L1_ffn_Su, L1_ffn_Sd, L1_ffn_Wsg)
    return x

_drawn_inputs = setup_inputs


def setup_inputs(seed=0):
    import zlib

    import numpy as np

    out = dict(_drawn_inputs(seed))
    spreads = {'L0_attn_ln_w': (1.0, 0.6),
     'L0_attn_ln_b': (0.0, 0.8),
     'L0_xattn_bq': (0.0, 0.1),
     'L0_xattn_bk': (0.0, 2.0),
     'L0_ffn_norm_w': (1.0, 0.2),
     'L1_attn_norm_w': (1.0, 0.6),
     'L1_attn_conv_b': (0.0, 0.8),
     'L1_attn_dt_b': (0.0, 0.8),
     'L1_attn_D_param': (1.0, 0.6)}
    factors = {'L0_attn_W_in': 6.647,
     'L0_attn_W_out': 6.338,
     'L1_attn_in_proj_w': 8.0,
     'L1_attn_conv_w': 8.0,
     'L1_attn_x_proj_w': 8.0,
     'L1_attn_dt_w': 8.0,
     'L1_attn_A_log': 8.0,
     'L1_attn_out_proj_w': 8.0,
     'L1_xattn_Wq': 64.0,
     'L1_xattn_Wk': 64.0,
     'L1_ffn_Wr': 36.801,
     'L1_ffn_Wg': 35.498,
     'L1_ffn_Wu': 31.155,
     'L1_ffn_Wd': 31.135,
     'L1_ffn_Sg': 22.963,
     'L1_ffn_Su': 8.0,
     'L1_ffn_Sd': 8.0,
     'L1_ffn_Wsg': 32.764,
     'L1_xattn_Wv': 8.0,
     'L1_xattn_Wo': 8.0}
    for name, (base, spread) in spreads.items():
        noise = np.random.default_rng([zlib.crc32(name.encode()), seed]).standard_normal(out[name].shape)
        drawn = base * np.exp(spread * noise) if base else spread * noise
        out[name] = jnp.asarray(drawn.astype(out[name].dtype))
    for name, factor in factors.items():
        out[name] = (out[name] * factor).astype(out[name].dtype)
    return out
```

```python
from contextlib import ExitStack

import numpy as np

import concourse.bass as bass
from concourse import mybir

F32 = mybir.dt.float32
BF16 = mybir.dt.bfloat16
U32 = mybir.dt.uint32
U8 = mybir.dt.uint8
ALU = mybir.AluOpType
ACT = mybir.ActivationFunctionType
AX = mybir.AxisListType
EXP_LN = "natural_log_exp_and_others"

P = 128
B, S, D = 4, 256, 256
T = B * S
TILES = T // P
TPB = S // P
DB = D // P
C = 128
LN_EPS = 1e-5
H0, DH0 = 16, D // 16
E0, K0, I0 = 32, 4, 128
CAP = 2 * T * K0 // E0
ROT = DH0 // 2
DI, NST, KC = 512, 16, 4
IB = DI // P
HALF = 512
NHALF = T // HALF
BPH = HALF // S
H1, HKV = 16, 8
GR = H1 // HKV
E1, F1, FS = 8, 176, 704
FT = E1 * F1 + FS
FB = -(-FT // P)
NEG = -1e30


def prev(n, k=0):
    n -= k
    return n // (4 * TPB), n // 4 % TPB, n % 4


def prev1(n):
    return n // (4 * TPB), n // TPB % 4, n % TPB


def head0(j, i):
    g, r = 2 * (j // 2) + i % 2, 2 * (j % 2) + i // 2
    return 4 * g + r


class Steps:

    def __init__(self, engine, book):
        self.engine, self.book, self.n = engine, book, 0

    def __call__(self, instruction, *step):
        self.n += 1
        if step:
            self.book[(self.engine, *step)] = self.n
        return instruction


def decoder(nc, ins, out, known):
    book = {}

    def at(*step):
        return known[step] if known is not None else 1

    ctx = ExitStack()
    with ctx:
        def sb(name, shape, dt=F32):
            return ctx.enter_context(nc.sbuf_tensor(name, shape, dt))

        def sem(name):
            return ctx.enter_context(nc.semaphore(name))

        X = sb("X", [P, TILES, D])
        XS = sb("XS", [P, 2 * TPB, D])
        XN = sb("XN", [P, TPB, D])
        stats = sb("stats", [P, TILES, 6])
        mv = sb("mv", [P, TILES, 2])
        lnv = sb("lnv", [P, 2, TILES])
        rstd = sb("rstd", [P, 2, TILES])
        ident = sb("ident", [P, P])
        lnw = sb("lnw", [P, 4, DB])
        ctxT = sb("ctxT", [P, T])
        iota_e = sb("iota_e", [P, E0])
        iota32 = iota_e[:, :]
        attT = sb("attT", [P, B, 2, S])

        def arena(name, size):
            whole = sb(name, [P, size])
            used = {}

            def phase(tag):
                used[tag] = 0

                def take(shape, dt=F32):
                    n = int(np.prod(shape))
                    words = n if dt in (F32, U32) else -(-n // (2 if dt == BF16 else 4))
                    a = used[tag]
                    used[tag] += words
                    assert used[tag] <= size, (name, tag, used[tag])
                    v = whole[:, a:a + words]
                    if dt != F32:
                        v = v.bitcast(dt)
                    if len(shape) == 1:
                        return v
                    names = "abcd"[:len(shape)]
                    return v.rearrange(f"p ({' '.join(names)}) -> p {' '.join(names)}",
                                       **dict(zip(names, shape)))
                return take
            return phase

        ping, pong = arena("ping", 26000), arena("pong", 19900)

        take = ping("A")
        w_in, w_out = take([DB, 3 * D]), take([DB, D])
        rope = take([TPB, 2, 2, ROT])
        xTa = take([2, DB, S])
        t1, t2 = take([2, H0, ROT]), take([2, H0, ROT])
        QP = take([TPB, 2, H0, 32])
        QT = take([2, 4, S])
        Va = take([2, TPB, D])
        Pa = take([2, 4, S])
        PTa = take([2, 4, 2, P])
        mxa, rsa, ria = take([2, 4]), take([2, H0]), take([H0])
        Ca = take([D])
        CTa = take([DB, P])
        wq0, wk0, bqk = take([P]), take([P]), take([2])
        cx = take([TILES, C])
        q0, k0 = take([T]), take([T])
        en = take([2, S])
        m0, s0 = take([TILES]), take([TILES])
        xTb = take([2, DB, S])

        take = pong("C")
        nwb = take([D])
        gw = take([DB, E0])
        sgu, sdn = take([DB, 2 * I0]), take([D])
        NW = 6
        w13, w2 = take([NW, DB, 2 * I0]), take([NW, D])
        hT = take([DB, T])
        tokid = take([TILES], U32)
        tri, ones = take([P], BF16), take([P], BF16)
        top8, idx8 = take([TILES, 8]), take([TILES, 8], U32)
        negm, ex4, sm4 = take([TILES]), take([TILES, K0]), take([TILES])
        w4 = take([TILES, K0])
        idf = take([K0])
        oh, ohp = take([K0, E0]), take([K0, E0])
        sel_tile = take([TILES, E0], BF16)
        posk, over, base = take([K0]), take([K0]), take([K0])
        rowf, slotf = take([K0]), take([K0])
        row, slot = take([TILES, K0], U32), take([TILES, K0], U32)
        tab, tabf = take([P], U32), take([P])
        slot_tok = take([2 * E0], U32)
        G = take([4, 2, D])
        XTc = take([2, DB, CAP])
        sg, ac = take([2, CAP]), take([2, CAP])
        EO = take([2, 2, D])
        Y = take([2, K0, D])
        sgs, acs = take([HALF]), take([HALF])
        zero1 = take([64], U32)

        take = ping("D")
        wip, wxp, wop = take([DB, 2 * DI]), take([IB, 33]), take([IB, D])
        cw, cb, dtw, dtb, dpar, alog, Aneg = (take([IB, KC]), take([IB]), take([IB]), take([IB]), take([IB]),
                                              take([IB, NST]), take([IB, NST]))
        selbc = take([2 * NST * P], BF16).rearrange("p (n m) -> p n m", m=P)
        xTd = take([DB, HALF])
        xi_words = take([IB * BPH * (S + KC - 1)])
        xi = xi_words.rearrange("p (m b s) -> p m b s", m=IB, b=BPH)
        dtu = xi_words[:, 0:IB * HALF].rearrange("p (m n) -> p m n", m=IB)
        u, sz, dt = take([IB, HALF]), take([IB, HALF]), take([IB, HALF])
        xs3f, xs3, xs3m = take([HALF]), take([HALF], BF16), take([HALF], BF16)
        wdt = take([IB, P])
        NB = 2
        Bb = take([NB, HALF])
        dA = take([2, IB, HALF])
        NHB = 2
        hb_ = take([NHB, IB, HALF])
        e1 = dA[:, 1]
        a1 = dA[:, 0]

        take = pong("E")
        wq1, wk1, wv1, wo1 = take([DB, H1 * P]), take([HKV * P]), take([HKV * P]), take([H1, D])
        xTe = take([DB, S])
        QE = take([2, 4, S])
        Pe = take([2, 4, S])
        mxe, rse, rie = take([2, 4]), take([2, 4]), take([2, 4])
        mrow, mrowb, one1 = take([B, S], U8), take([B * S], BF16), take([P], BF16)
        vfl, mflag = take([B, S], U8), take([B])
        take = ping("F")
        wg, wu, wd = take([DB, FT]), take([DB, FT]), take([FB, D])
        wr = take([DB, E1 + 1])
        sel27 = take([FB * P], BF16)
        kT, V1 = take([HKV, S]), take([2, HKV * P])
        PTe = take([2, 4, 2, P])
        OT = take([H1, S])
        take = pong("F")
        xTf = take([NHALF, DB, HALF])
        lg, pr, sp1, rp = take([TILES, E1 + 1]), take([TILES, E1]), take([TILES]), take([TILES])
        np8, tp8, ti8, tif = take([TILES]), take([TILES, 8]), take([TILES, 8], U32), take([TILES, 2])
        cc, c2 = take([TILES, E1 + 1]), take([TILES, E1])
        chb, cmb = take([E1 + 1 + 1], BF16), take([E1 + 1 + 1], BF16)
        c27 = take([TILES, 27])
        r1c = take([E1 + 1])
        cT = take([T], BF16)
        iota8 = iota_e[:, 0:E1]
        sgf, tf, acf = take([2, HALF]), take([2, HALF]), take([3, HALF])

        PS = ctx.enter_context(nc.psum_tensor("PS", [P, 8, 512], F32))

        def bank(i, n=1):
            return PS[:, i:i + n, :]

        h_dram = nc.dram_tensor("h_dram", (T, D), F32, kind="Internal").ap()
        eo_dram = nc.dram_tensor("eo_dram", (E0 * CAP, D), F32, kind="Internal").ap()
        slots_dram = nc.dram_tensor("slots_dram", (E0 * CAP, 1), U32, kind="Internal").ap()

        pe_done, act_done = sem("pe_done"), sem("act_done")
        dve_done, pool_done = sem("dve_done"), sem("pool_done")
        PEs, ACs, VEs, POs = Steps("pe", book), Steps("act", book), Steps("dve", book), Steps("pool", book)
        x_in, ctx_in, attn_w_in, xattn_w_in = sem("x_in"), sem("ctx_in"), sem("attn_w_in"), sem("xattn_w_in")
        moe_w_in, const_in, mamba_w_in, xattn1_w_in = sem("moe_w_in"), sem("const_in"), sem("mamba_w_in"), sem("xattn1_w_in")
        ffn1_w_in = sem("ffn1_w_in")
        expert_in = [sem(f"expert_in{i}") for i in range(NW)]
        h_stored = [sem(f"h_stored{i}") for i in range(2 * TPB)]
        table_clear, scattered, table_in = sem("table_clear"), sem("scattered"), sem("table_in")
        gathered = [sem(f"gathered{i}") for i in range(4)]
        eo_stored = [sem(f"eo_stored{i}") for i in range(2)]
        y_in = [sem(f"y_in{i}") for i in range(2)]
        out_stored = sem("out_stored")

        N_X, N_CONST, N_ATTN, N_XATTN, N_MOE, N_MAMBA, N_XATTN1, N_FFN1 = 4, 7, 2, 3, 4, 10, 6, 5

        block = ctx.enter_context(nc.Block())

        @block.sync
        def _(sp):
            xv = ins["x"].rearrange("b (t p) d -> p (b t) d", p=P)
            for b in range(B):
                sp.dma_start(X[:, TPB * b:TPB * b + TPB, :], xv[:, TPB * b:TPB * b + TPB, :]).then_inc(x_in, 16)
            sp.dma_start(cx, ins["ctx"].rearrange("b (t p) d -> p (b t) d", p=P)).then_inc(ctx_in, 16)
            sp.dma_start(ident[:, :], ins["ident"]).then_inc(const_in, 16)
            sp.dma_start(lnw[:, :, :], ins["lnw"]).then_inc(const_in, 16)
            sp.dma_start(wq0, ins["wq0T"]).then_inc(xattn_w_in, 16)
            sp.dma_start(wk0, ins["wk0T"]).then_inc(xattn_w_in, 16)
            sp.dma_start(bqk, ins["bqk"]).then_inc(xattn_w_in, 16)
            sp.dma_start(w_in, ins["w_in"].rearrange("(k p) n -> p k n", p=P)).then_inc(attn_w_in, 16)
            sp.dma_start(w_out, ins["w_out"].rearrange("(k p) n -> p k n", p=P)).then_inc(attn_w_in, 16)
            sp.dma_start(rope, ins["rope"]).then_inc(const_in, 16)
            sp.dma_start(iota32, ins["iota32"]).then_inc(const_in, 16)
            sp.dma_start(tri, ins["tri"]).then_inc(const_in, 16)
            sp.dma_start(tokid, ins["tokid"]).then_inc(const_in, 16)
            sp.dma_start(nwb, ins["norm_w"].partition_broadcast(P)).then_inc(const_in, 16)
            sp.dma_start(gw, ins["gate_wT"].rearrange("(k p) n -> p k n", p=P)).then_inc(moe_w_in, 16)
            sp.dma_start(sgu[:, :, 0:I0], ins["sgate"].rearrange("(k p) n -> p k n", p=P)).then_inc(moe_w_in, 16)
            sp.dma_start(sgu[:, :, I0:2 * I0], ins["sup"].rearrange("(k p) n -> p k n", p=P)).then_inc(moe_w_in, 16)
            sp.dma_start(sdn, ins["sdown"]).then_inc(moe_w_in, 16)
            sp.wait_ge(pool_done, at("pool", "zeros"))
            sp.dma_start(slots_dram.rearrange("(p n) o -> p (n o)", p=P), zero1).then_inc(table_clear, 16)

            def load_expert(e):
                sp.dma_start(w13[:, e % NW], ins["w13"][e].rearrange("(k p) n -> p k n", p=P)).then_inc(expert_in[e % NW], 16)
                sp.dma_start(w2[:, e % NW], ins["w2"][e]).then_inc(expert_in[e % NW], 16)

            for e in range(NW):
                load_expert(e)
            for t in range(TILES):
                sp.wait_ge(dve_done, at("dve", "C.h", t))
                sp.dma_start(h_dram[t * P:(t + 1) * P, :], XS[:, t % (2 * TPB), :]).then_inc(h_stored[t % 4], 16)
            sp.wait_ge(pe_done, at("pe", "B.end"))
            sp.wait_ge(act_done, at("act", "B.end"))
            sp.wait_ge(dve_done, at("dve", "B.end"))
            sp.dma_start(wip, ins["in_projT"].rearrange("(k p) n -> p k n", p=P)).then_inc(mamba_w_in, 16)
            for dst, name in ((wxp, "x_projT"), (wop, "out_projT"), (cw, "conv_w"), (cb, "conv_b"), (dtw, "dt_w"),
                              (dtb, "dt_b"), (dpar, "D_param"), (alog, "A_log")):
                src = ins[name]
                if src.shape[0] == DI:
                    src = src.rearrange("(k p) n -> p k n", p=P)
                sp.dma_start(dst, src).then_inc(mamba_w_in, 16)
            sp.dma_start(selbc[0:96], ins["selbc"]).then_inc(mamba_w_in, 16)
            sp.wait_ge(scattered, 16 * TILES * K0)
            sp.dma_start(tab[0:2 * E0, :], slots_dram.rearrange("(j p) o -> j (p o)", p=P)).then_inc(table_in, 16)
            for e in range(E0):
                sp.wait_ge(act_done, at("act", "C.eo", e))
                sp.dma_start(eo_dram[e * CAP:(e + 1) * CAP, :].rearrange("(s p) d -> p s d", p=P),
                             EO[:, e % 2]).then_inc(eo_stored[e % 2], 16)
                if e + NW < E0:
                    sp.wait_ge(pe_done, at("pe", "C.down", e))
                    load_expert(e + NW)
            sp.wait_ge(dve_done, at("dve", "C.end"))
            for i in range(2):
                sp.wait_ge(eo_stored[i], 16 * E0 // 2)
            sp.dma_start(wq1, ins["wq1"].rearrange("(k p) n -> p k n", p=P)).then_inc(xattn1_w_in, 16)
            sp.dma_start(wk1, ins["wk1"]).then_inc(xattn1_w_in, 16)
            sp.dma_start(wv1, ins["wv1"]).then_inc(xattn1_w_in, 16)
            sp.dma_start(wo1, ins["wo1"].rearrange("(h p) n -> p h n", p=P)).then_inc(xattn1_w_in, 16)
            sp.dma_start(mrow[0:1], ins["mask"].rearrange("(o b) s -> o b s", o=1)).then_inc(xattn1_w_in, 16)
            sp.dma_start(vfl, ins["mask"].partition_broadcast(P)).then_inc(xattn1_w_in, 16)
            sp.wait_ge(pe_done, at("pe", "D.end"))
            sp.wait_ge(act_done, at("act", "D.end"))
            sp.wait_ge(dve_done, at("dve", "D.end"))
            sp.wait_ge(pool_done, at("pool", "D.end"))
            sp.dma_start(wg, ins["wg"].rearrange("(k p) n -> p k n", p=P)).then_inc(ffn1_w_in, 16)
            sp.dma_start(wu, ins["wu"].rearrange("(k p) n -> p k n", p=P)).then_inc(ffn1_w_in, 16)
            sp.dma_start(wd, ins["wd"]).then_inc(ffn1_w_in, 16)
            sp.dma_start(wr, ins["wr"].rearrange("(k p) n -> p k n", p=P)).then_inc(ffn1_w_in, 16)
            sp.dma_start(sel27[0:27], ins["sel27"]).then_inc(ffn1_w_in, 16)
            ov = out.rearrange("b (t p) d -> p (b t) d", p=P)
            for t in range(0, TILES, 4):
                sp.wait_ge(dve_done, at("dve", "F.x", t + 3))
                sp.dma_start(ov[:, t:t + 4, :], X[:, t:t + 4, :]).then_inc(out_stored, 16)
            sp.wait_ge(out_stored, 16 * 2)

        @block.gpsimd
        def _(pool):
            POs(nc.gpsimd.memset(zero1, 0).then_inc(pool_done, 1), "zeros")
            POs(nc.gpsimd.memset(QP, 0.0).then_inc(pool_done, 1), "QP")
            POs(nc.gpsimd.memset(ones, 1.0).then_inc(pool_done, 1), "ones")

            pool.wait_ge(table_clear, 16)
            pool.wait_ge(const_in, 16 * N_CONST)
            for t in range(TILES):
                pool.wait_ge(dve_done, at("dve", "C.slot", t))
                for k in range(K0):
                    nc.gpsimd.indirect_dma_start(
                        out=slots_dram, out_offset=bass.IndirectOffsetOnAxis(ap=slot[:, t, k:k + 1], axis=0),
                        in_=tokid[:, t:t + 1], in_offset=None,
                        bounds_check=E0 * CAP - 1, oob_is_err=False).then_inc(scattered, 16)
            for i in range(4):
                pool.wait_ge(h_stored[i], 16 * TILES // 4)
            pool.wait_ge(dve_done, at("dve", "C.slot_tok"))
            for j in range(2 * E0):
                if j >= 8:
                    pool.wait_ge(pe_done, at("pe", "C.xT", j // 2 - 4))
                nc.gpsimd.indirect_dma_start(
                    out=G[:, (j // 2) % 4, j % 2, :], out_offset=None, in_=h_dram,
                    in_offset=bass.IndirectOffsetOnAxis(ap=slot_tok[:, j:j + 1], axis=0),
                    bounds_check=T - 1, oob_is_err=False).then_inc(gathered[(j // 2) % 4], 16)
            for i in range(2):
                pool.wait_ge(eo_stored[i], 16 * E0 // 2)
            for t in range(TILES):
                if t >= 2:
                    pool.wait_ge(dve_done, at("dve", "C.comb", t - 2))
                for k in range(K0):
                    nc.gpsimd.indirect_dma_start(
                        out=Y[:, t % 2, k, :], out_offset=None, in_=eo_dram,
                        in_offset=bass.IndirectOffsetOnAxis(ap=row[:, t, k:k + 1], axis=0),
                        bounds_check=E0 * CAP - 1, oob_is_err=False).then_inc(y_in[t % 2], 16)

            pool.wait_ge(pe_done, at("pe", "B.end"))
            pool.wait_ge(dve_done, at("dve", "B.end"))
            pool.wait_ge(act_done, at("act", "B.end"))
            for hf in range(NHALF):
                if hf:
                    pool.wait_ge(pool_done, POs.n)
                POs(nc.gpsimd.memset(xi[:, :, :, 0:KC - 1], 0.0).then_inc(pool_done, 1), "D.pad", hf)
                pool.wait_ge(dve_done, at("dve", "D.dtu", hf))
                for r in range(2):
                    POs(nc.gpsimd.memset(dA[:, r, :, 0:HALF:S], 0.0).then_inc(pool_done, 1), "D.zero", hf, r)
                for n in range(NST):
                    s = hf * NST + n
                    pool.wait_ge(act_done, at("act", "D.Bb", s))
                    if s >= NHB:
                        pool.wait_ge(pe_done, at("pe", "D.sum", s - NHB))
                    bn = Bb[:, s % NB, :]
                    POs(nc.gpsimd.tensor_tensor(
                        hb_[:, s % NHB], dtu, bn.rearrange("p (o n) -> p o n", o=1).broadcast_to((P, IB, HALF)),
                        ALU.mult).then_inc(pool_done, 1), "D.Bu", s)
            book[("pool", "D.end")] = POs.n

        @block.scalar
        def _(act):
            a = nc.scalar

            def ln(name, b, second):
                act.wait_ge(dve_done, at("dve", name + ".mv", b))
                t0 = TPB * b
                var = mv[:, t0:t0 + TPB, 1]
                ACs(a.activation(lnv[:, 0, t0:t0 + TPB], var, ACT.Ln, bias=LN_EPS).then_inc(act_done, 1))
                if second:
                    ACs(a.activation(lnv[:, 1, t0:t0 + TPB], var, ACT.Ln, bias=LN_EPS * second, scale=1.0 + second).then_inc(act_done, 1))
                act.wait_ge(act_done, ACs.n)
                k = 2 if second else 1
                ACs(a.activation(rstd[:, 0:k, t0:t0 + TPB], lnv[:, 0:k, t0:t0 + TPB], ACT.Exp, scale=-0.5).then_inc(act_done, 1),
                    name + ".rstd", b)

            a.preload_act_table_set(EXP_LN)
            act.wait_ge(xattn_w_in, 16 * N_XATTN)
            for i in range(2):
                act.wait_ge(pe_done, at("pe", "ctxT", i))
                ACs(a.activation(ctxT[:, 512 * i:512 * i + 512], bank(i)[:, 0, :], ACT.Copy).then_inc(act_done, 1), "ctxT", i)
            for i in range(4):
                act.wait_ge(pe_done, at("pe", "qk0", i))
                dst = (q0, k0)[i // 2][:, 512 * (i % 2):512 * (i % 2) + 512]
                ACs(a.activation(dst, bank(2 + i)[:, 0, :], ACT.Identity, bias=bqk[:, i // 2:i // 2 + 1]).then_inc(act_done, 1), "qk0", i)
            for t in range(TILES):
                act.wait_ge(dve_done, at("dve", "m0", t))
                if t >= 2:
                    act.wait_ge(pe_done, at("pe", "attT", t - 2))
                ACs(a.activation(en[:, t % 2, :], bank(t % 2)[:, 0, 0:S], ACT.Exp, bias=m0[:, t:t + 1],
                                 accum_out=s0[:, t:t + 1]).then_inc(act_done, 1), "en", t)

            for b in range(B):
                ln("A", b, LN_EPS)
                act.wait_ge(pe_done, at("pe", "A.xT", b))
                act.wait_ge(const_in, 16 * N_CONST)
                for k in range(DB):
                    ACs(a.activation(xTa[:, b % 2, k, :], bank(7)[:, 0, k * S:k * S + S], ACT.Identity, scale=lnw[:, 0, k:k + 1],
                                     bias=lnw[:, 1, k:k + 1]).then_inc(act_done, 1), "A.xT", b)
                for tt in range(TPB):
                    act.wait_ge(pe_done, at("pe", "A.qkv", b, tt))
                    if b >= 2 and tt == 0:
                        act.wait_ge(pe_done, at("pe", "A.av", b - 2, TPB - 1, 3))
                    ACs(a.activation(Va[:, b % 2, tt, :], bank(7)[:, 0, 0:D], ACT.Copy).then_inc(act_done, 1), "A.V", b, tt)
                for tt in range(TPB):
                    act.wait_ge(pe_done, at("pe", "A.qkT", b, tt))
                    if b > 0 and tt == 0:
                        act.wait_ge(pe_done, at("pe", "A.S", b - 1, TPB - 1, 3))
                    ACs(a.activation(QT[:, :, :, tt * P:tt * P + P],
                                     bank(4, 2).rearrange("p w (g n) -> p w g n", g=4), ACT.Copy).then_inc(act_done, 1), "A.QT", b, tt)
                for tt in range(TPB):
                    for j in range(4):
                        n = (b * TPB + tt) * 4 + j
                        act.wait_ge(dve_done, at("dve", "A.max", b, tt, j))
                        if n >= 2:
                            act.wait_ge(pe_done, at("pe", "A.PT", *prev(n, 2)))
                        if j == 0 and b * TPB + tt >= 2:
                            act.wait_ge(dve_done, at("dve", "A.ctx", (b * TPB + tt - 2) // TPB, tt))
                        Sb = bank(2 * (n % 2), 2).rearrange("p w (g k) -> p (w g) k", g=2)
                        for i in range(4):
                            h = head0(j, i)
                            ACs(a.activation(Pa[:, n % 2, i, :], Sb[:, i, :], ACT.Exp, bias=mxa[:, n % 2, i:i + 1],
                                             accum_out=rsa[:, tt, h:h + 1]).then_inc(act_done, 1), "A.P", b, tt, j)
                        act.wait_ge(pe_done, at("pe", "A.PT", b, tt, j))
                        if n >= 2:
                            act.wait_ge(pe_done, at("pe", "A.av", *prev(n, 2)))
                        ACs(a.activation(PTa[:, n % 2, 0:2], bank(4)[:, 0, :].rearrange("p (i k q) -> p i k q", i=2, k=2),
                                         ACT.Copy).then_inc(act_done, 1), "A.PT", b, tt, j)
                    act.wait_ge(pe_done, at("pe", "A.cT", b, tt))
                    ACs(a.activation(CTa, bank(7)[:, 0, 0:2 * P].rearrange("p (k q) -> p k q", k=2), ACT.Copy).then_inc(act_done, 1), "A.cT", b, tt)

            for b in range(B):
                ln("B", b, None)
                act.wait_ge(pe_done, at("pe", "B.xT", b))
                if b >= 2:
                    act.wait_ge(pe_done, at("pe", "B.out", b - 2))
                ACs(a.activation(xTb[:, b % 2], bank(b % 2)[:, 0, :].rearrange("p (k n) -> p k n", k=DB), ACT.Copy).then_inc(act_done, 1), "B.xT", b)
            book[("act", "B.end")] = ACs.n

            for b in range(B):
                ln("C", b, 1e-6)
            for t in range(TILES):
                act.wait_ge(pe_done, at("pe", "C.hT", t))
                ACs(a.activation(hT[:, :, t * P:t * P + P], bank(t % 2)[:, 0, 0:2 * P].rearrange("p (k n) -> p k n", k=DB),
                                 ACT.Copy).then_inc(act_done, 1), "C.hT", t)
                act.wait_ge(dve_done, at("dve", "C.top", t))
                ACs(a.activation(ex4[:, t, :], top8[:, t, 0:K0], ACT.Exp, bias=negm[:, t:t + 1],
                                 accum_out=sm4[:, t:t + 1]).then_inc(act_done, 1), "C.ex4", t)
            for hf in range(NHALF):
                act.wait_ge(pe_done, at("pe", "C.sgu", hf))
                if hf:
                    act.wait_ge(dve_done, at("dve", "C.sact", hf - 1))
                ACs(a.activation(sgs, bank(4)[:, 0, :], ACT.Silu).then_inc(act_done, 1), "C.sgs", hf)
            for e in range(E0):
                act.wait_ge(pe_done, at("pe", "C.gu", e))
                if e >= 2:
                    act.wait_ge(dve_done, at("dve", "C.act", e - 2))
                ACs(a.activation(sg[:, e % 2, :], bank(2 + e % 2)[:, 0, 0:CAP], ACT.Silu).then_inc(act_done, 1), "C.sg", e)
                act.wait_ge(pe_done, at("pe", "C.down", e))
                if e >= 2:
                    act.wait_ge(eo_stored[e % 2], 16 * (e // 2))
                ACs(a.activation(EO[:, e % 2], bank(4 + e % 2)[:, 0, :].rearrange("p (s d) -> p s d", s=2), ACT.Copy).then_inc(act_done, 1), "C.eo", e)

            a.preload_act_table_set(EXP_LN)
            act.wait_ge(mamba_w_in, 16 * N_MAMBA)
            ACs(a.activation(Aneg, alog, ACT.Exp).then_inc(act_done, 1), "D.A")
            for b in range(B):
                ln("D", b, LN_EPS)
            for hf in range(NHALF):
                act.wait_ge(pe_done, at("pe", "D.xT", hf))
                if hf:
                    act.wait_ge(pe_done, at("pe", "D.z", hf - 1, IB - 1))
                for k in range(DB):
                    ACs(a.activation(xTd[:, k, :], bank(6 + k)[:, 0, :], ACT.Copy, scale=lnw[:, 3, k:k + 1]).then_inc(act_done, 1), "D.xT", hf)
                for m in range(IB):
                    act.wait_ge(pe_done, at("pe", "D.xi", hf, m))
                    act.wait_ge(pool_done, at("pool", "D.pad", hf))
                    if hf:
                        act.wait_ge(dve_done, at("dve", "D.conv", hf - 1, m))
                    ACs(a.activation(xi[:, m, :, KC - 1:], bank(m)[:, 0, :].rearrange("p (b s) -> p b s", b=BPH), ACT.Copy).then_inc(act_done, 1), "D.xi", hf, m)
                for m in range(IB):
                    act.wait_ge(pe_done, at("pe", "D.z", hf, m))
                    if hf and m == 0:
                        act.wait_ge(dve_done, at("dve", "D.yz", hf - 1, IB - 1))
                    ACs(a.activation(sz[:, m, :], bank(4 + m % 2)[:, 0, :], ACT.Silu).then_inc(act_done, 1), "D.sz", hf, m)
                for m in range(IB):
                    act.wait_ge(dve_done, at("dve", "D.conv", hf, m))
                    ACs(a.activation(u[:, m, :], u[:, m, :], ACT.Silu).then_inc(act_done, 1), "D.u", hf, m)
                a.preload_act_table_set(EXP_LN)
                for m in range(IB):
                    act.wait_ge(dve_done, at("dve", "D.v", hf, m))
                    ACs(a.activation(a1[:, m, :], dt[:, m, :], ACT.Abs).then_inc(act_done, 1))
                act.wait_ge(act_done, ACs.n)
                ACs(a.activation(e1, a1, ACT.Exp, scale=-1.0).then_inc(act_done, 1))
                act.wait_ge(act_done, ACs.n)
                ACs(a.activation(e1, e1, ACT.Ln, bias=1.0).then_inc(act_done, 1), "D.sp", hf)
                for n in range(NST):
                    s = hf * NST + n
                    act.wait_ge(pe_done, at("pe", "D.B", s))
                    if s >= NB:
                        act.wait_ge(pool_done, at("pool", "D.Bu", s - NB))
                    ACs(a.activation(Bb[:, s % NB, :], bank(6)[:, 0, :], ACT.Copy).then_inc(act_done, 1), "D.Bb", s)
                    act.wait_ge(dve_done, at("dve", "D.dtu", hf) if n < 2 else at("dve", "D.scan", s - 2))
                    for m in range(IB):
                        step = dA[:, s % 2, m, :].rearrange("p (b s) -> p b s", b=BPH)[:, :, 1:]
                        ACs(a.activation(step, dt[:, m, :].rearrange("p (b s) -> p b s", b=BPH)[:, :, 1:], ACT.Exp,
                                         scale=Aneg[:, m, n:n + 1]).then_inc(act_done, 1), "D.dA", s)
            book[("act", "D.end")] = ACs.n

            for b in range(B):
                ln("E", b, None)
                act.wait_ge(pe_done, at("pe", "E.xT", b))
                if b:
                    act.wait_ge(pe_done, at("pe", "E.q", b - 1, 3, 1))
                ACs(a.activation(xTe, bank(7)[:, 0, :].rearrange("p (k n) -> p k n", k=DB), ACT.Copy).then_inc(act_done, 1), "E.xT", b)
                for i in range(4):
                    act.wait_ge(pe_done, at("pe", "E.k", b, i))
                    if b and i == 0:
                        act.wait_ge(pe_done, at("pe", "E.av", b - 1, 3, 1))
                    ACs(a.activation(kT[:, 2 * i:2 * i + 2, :], bank(4 + i % 2)[:, 0, :].rearrange("p (h s) -> p h s", h=2),
                                     ACT.Copy).then_inc(act_done, 1), "E.k", b, i)

                def q_copies(hg):
                    for i in range(2):
                        act.wait_ge(pe_done, at("pe", "E.q", b, hg, i))
                        n0 = (b * 4 + hg) * 2
                        if n0 >= 4 and i == 0:
                            act.wait_ge(pe_done, at("pe", "E.S", *prev1(n0 - 3)))
                        ACs(a.activation(QE[:, hg % 2, 2 * i:2 * i + 2, :], bank(7)[:, 0, :].rearrange("p (h s) -> p h s", h=2),
                                         ACT.Copy, scale=float(P) ** -0.5).then_inc(act_done, 1), "E.q", b, hg, i)

                q_copies(0)
                for hg in range(4):
                    n0 = (b * 4 + hg) * 2
                    for qt in range(TPB):
                        n = n0 + qt
                        act.wait_ge(dve_done, at("dve", "E.max", b, hg, qt))
                        if n >= 2:
                            act.wait_ge(pe_done, at("pe", "E.PT", *prev1(n - 2)))
                            act.wait_ge(dve_done, at("dve", "E.PT", *prev1(n - 2)))
                        Sb = bank(2 * (n % 2), 2).rearrange("p w (g k) -> p (w g) k", g=2)
                        for i in range(4):
                            ACs(a.activation(Pe[:, n % 2, i, :], Sb[:, i, :], ACT.Exp, bias=mxe[:, n % 2, i:i + 1],
                                             accum_out=rse[:, n % 2, i:i + 1]).then_inc(act_done, 1), "E.P", b, hg, qt)
                        act.wait_ge(pe_done, at("pe", "E.PT", b, hg, qt))
                        if n >= 2:
                            act.wait_ge(pe_done, at("pe", "E.av", *prev1(n - 2)))
                        ACs(a.activation(PTe[:, n % 2, 0:2], bank(4)[:, 0, :].rearrange("p (i k q) -> p i k q", i=2, k=2),
                                         ACT.Copy).then_inc(act_done, 1), "E.PT", b, hg, qt)
                        act.wait_ge(pe_done, at("pe", "E.av", b, hg, qt))
                        if b and n % 8 < 2:
                            act.wait_ge(pe_done, at("pe", "E.o", b - 1, TPB - 1))
                        ACs(a.activation(OT[:, 4 * hg:4 * hg + 4, qt * P:qt * P + P],
                                         bank(6)[:, 0, :].rearrange("p (h q) -> p h q", h=4), ACT.Copy).then_inc(act_done, 1), "E.OT", b, hg, qt)
                        if qt == 0 and hg + 1 < 4:
                            q_copies(hg + 1)

            for b in range(B):
                ln("F", b, None)
            for b in range(B):
                act.wait_ge(pe_done, at("pe", "F.xT", b))
                ACs(a.activation(xTf[:, b // BPH, :, (b % BPH) * S:(b % BPH) * S + S],
                                 bank(b % 2)[:, 0, :].rearrange("p (k n) -> p k n", k=DB), ACT.Copy).then_inc(act_done, 1), "F.xT", b)
            for t in range(TILES):
                act.wait_ge(dve_done, at("dve", "F.max", t))
                ACs(a.activation(pr[:, t, :], lg[:, t, 0:E1], ACT.Exp, bias=np8[:, t:t + 1], accum_out=sp1[:, t:t + 1]).then_inc(act_done, 1))
                ACs(a.activation(lg[:, t, E1:], lg[:, t, E1:], ACT.Exp, scale=-1.0).then_inc(act_done, 1), "F.pr", t)
                act.wait_ge(pe_done, at("pe", "F.cT", t))
                ACs(a.activation(cT[0:27, t * P:t * P + P], bank(4 + t % 2)[0:27, 0, 0:P], ACT.Copy).then_inc(act_done, 1), "F.cT", t)
            for hf in range(NHALF):
                for f in range(FB):
                    n = hf * FB + f
                    act.wait_ge(pe_done, at("pe", "F.gu", n))
                    if n >= 2:
                        act.wait_ge(dve_done, at("dve", "F.act", n - 2))
                    m = min(P, FT - f * P)
                    ACs(a.activation(sgf[0:m, n % 2, :], bank(n % 2)[0:m, 0, :], ACT.Silu).then_inc(act_done, 1), "F.sg", n)

        @block.vector
        def _(dve):
            v = nc.vector

            def ln(name, b, second, residual):
                t0 = TPB * b
                for t in range(t0, t0 + TPB):
                    VEs(v.bn_stats(stats[:, t, :], X[:, t, :]).then_inc(dve_done, 1))
                dve.wait_ge(dve_done, VEs.n)
                for t in range(t0, t0 + TPB):
                    VEs(v.bn_aggr(mv[:, t, :], stats[:, t, :]).then_inc(dve_done, 1), name + ".mv", b)

            def ln_apply(name, b, second, residual, free):
                t0 = TPB * b
                dve.wait_ge(act_done, at("act", name + ".rstd", b))
                dve.wait_ge(dve_done, VEs.n)
                free()
                for t in range(t0, t0 + TPB):
                    VEs(v.tensor_scalar(XS[:, t % 4, :], X[:, t, :], mv[:, t, 0:1], rstd[:, 1 if second else 0, t:t + 1],
                                        ALU.subtract, ALU.mult).then_inc(dve_done, 1), name + ".xs", b)
                if residual:
                    for t in range(t0, t0 + TPB):
                        VEs(v.tensor_scalar(XN[:, t % TPB, :], X[:, t, :], mv[:, t, 0:1], rstd[:, 0, t:t + 1],
                                            ALU.subtract, ALU.mult).then_inc(dve_done, 1))
                    dve.wait_ge(dve_done, VEs.n)
                    for t in range(t0, t0 + TPB):
                        VEs(v.tensor_tensor(X[:, t, :], X[:, t, :], XN[:, t % TPB, :], ALU.add).then_inc(dve_done, 1), name + ".res", b)

            def add_to_x(t, psum, *step):
                VEs(v.tensor_tensor(X[:, t, :], X[:, t, :], psum, ALU.add).then_inc(dve_done, 1), *step)

            for t in range(TILES):
                dve.wait_ge(pe_done, at("pe", "en", t))
                VEs(v.tensor_reduce(m0[:, t:t + 1], bank(t % 2)[:, 0, 0:S], AX.X, ALU.max, negate=True).then_inc(dve_done, 1), "m0", t)
                dve.wait_ge(act_done, at("act", "en", t))
                VEs(v.reciprocal(s0[:, t:t + 1], s0[:, t:t + 1]).then_inc(dve_done, 1))
                dve.wait_ge(dve_done, VEs.n)
                VEs(v.tensor_scalar(en[:, t % 2, :], en[:, t % 2, :], s0[:, t:t + 1], None, ALU.mult).then_inc(dve_done, 1), "enn", t)
                dve.wait_ge(pe_done, at("pe", "attT", t))
                b, nt = t // 2, t % 2
                VEs(v.tensor_copy(attT[:, b, :, nt * P:nt * P + P],
                                  bank(2 + t % 2)[:, 0, 0:2 * P].rearrange("p (m n) -> p m n", m=2)).then_inc(dve_done, 1), "attT", t)

            def stats_a(b):
                dve.wait_ge(x_in, 16 * N_X)
                ln("A", b, True, True)

            stats_a(0)
            for b in range(B):
                def free(b=b):
                    if b >= 2:
                        dve.wait_ge(pe_done, at("pe", "A.xT", b - 2))
                ln_apply("A", b, True, True, free)
                for tt in range(TPB):
                    t = TPB * b + tt
                    dve.wait_ge(pe_done, at("pe", "A.qkv", b, tt))
                    dve.wait_ge(const_in, 16 * N_CONST)
                    qk = bank(6)[:, 0, :].rearrange("p (w h d) -> p w h d", w=2, h=H0)

                    def tab_(i, a0):
                        v_ = rope[:, tt, :, i, a0:ROT:1 if i == 0 else 2]
                        n = ROT if i == 0 else ROT // 2
                        return v_.rearrange("p w (o d) -> p w o d", o=1).broadcast_to((P, 2, H0, n))
                    VEs(v.tensor_tensor(t1, qk[:, :, :, 0:ROT], tab_(0, 0), ALU.mult).then_inc(dve_done, 1))
                    VEs(v.tensor_tensor(t2[:, :, :, 0:ROT:2], qk[:, :, :, 1:ROT:2], tab_(1, 0), ALU.mult).then_inc(dve_done, 1))
                    VEs(v.tensor_tensor(t2[:, :, :, 1:ROT:2], qk[:, :, :, 0:ROT:2], tab_(1, 1), ALU.mult).then_inc(dve_done, 1))
                    dve.wait_ge(dve_done, VEs.n)
                    dve.wait_ge(pool_done, at("pool", "QP"))
                    if b:
                        dve.wait_ge(pe_done, at("pe", "A.qkT", b - 1, tt))
                    VEs(v.tensor_scalar(QP[:, tt, 0, :, ROT:DH0], qk[:, 0, :, ROT:DH0], DH0 ** -0.5, None, ALU.mult).then_inc(dve_done, 1))
                    VEs(v.tensor_copy(QP[:, tt, 1, :, ROT:DH0], qk[:, 1, :, ROT:DH0]).then_inc(dve_done, 1), "A.qk", b, tt)
                    VEs(v.tensor_tensor(QP[:, tt, :, :, 0:ROT], t1, t2, ALU.add).then_inc(dve_done, 1), "A.rope", b, tt)
                    if tt + 1 < TPB:
                        dve.wait_ge(dve_done, VEs.n)
                if b + 1 < B:
                    stats_a(b + 1)
                for tt in range(TPB):
                    for j in range(4):
                        n = (b * TPB + tt) * 4 + j
                        def maxes(n):
                            dve.wait_ge(pe_done, at("pe", "A.S", *prev(n)))
                            if n >= 2:
                                dve.wait_ge(act_done, at("act", "A.P", *prev(n, 2)))
                            VEs(v.tensor_reduce(mxa[:, n % 2, :], bank(2 * (n % 2), 2).rearrange("p w (g k) -> p (w g) k", g=2),
                                                AX.X, ALU.max, negate=True).then_inc(dve_done, 1), "A.max", *prev(n))
                        if tt == 0 and j == 0:
                            maxes(n)
                        if not (tt == TPB - 1 and j == 3):
                            maxes(n + 1)
                        dve.wait_ge(pe_done, at("pe", "A.PT", b, tt, j))
                        if n >= 2:
                            dve.wait_ge(pe_done, at("pe", "A.av", *prev(n, 2)))
                        VEs(v.tensor_copy(PTa[:, n % 2, 2:4], bank(5)[:, 0, :].rearrange("p (i k q) -> p i k q", i=2, k=2))
                            .then_inc(dve_done, 1), "A.PT", b, tt, j)
                    dve.wait_ge(act_done, at("act", "A.P", b, tt, 3))
                    VEs(v.reciprocal(ria, rsa[:, tt, :]).then_inc(dve_done, 1))
                    dve.wait_ge(dve_done, VEs.n)
                    dve.wait_ge(pe_done, at("pe", "A.av", b, tt, 3))
                    if n >= 4:
                        dve.wait_ge(pe_done, at("pe", "A.cT", (b * TPB + tt - 1) // TPB, (tt - 1) % TPB))
                    VEs(v.tensor_tensor(Ca.rearrange("p (h d) -> p h d", h=H0), bank(6)[:, 0, 0:D].rearrange("p (h d) -> p h d", h=H0),
                                        ria.rearrange("p (h o) -> p h o", o=1).broadcast_to((P, H0, DH0)), ALU.mult).then_inc(dve_done, 1), "A.ctx", b, tt)
                    dve.wait_ge(pe_done, at("pe", "A.out", b, tt))
                    add_to_x(TPB * b + tt, bank(7)[:, 0, D:2 * D], "A.x", b, tt)

            dve.wait_ge(dve_done, VEs.n)
            ln("B", 0, False, False)
            for b in range(B):
                if b + 1 < B:
                    ln("B", b + 1, False, False)

                def free(b=b):
                    dve.wait_ge(pe_done, at("pe", "B.xT", b - 2) if b >= 2 else at("pe", "A.xT", B - 1))
                ln_apply("B", b, False, False, free)
                for tt in range(TPB):
                    dve.wait_ge(pe_done, at("pe", "B.out", b))
                    add_to_x(TPB * b + tt, bank(2 + b % 2)[:, 0, tt * D:tt * D + D], "B.x", b, tt)
            book[("dve", "B.end")] = VEs.n

            dve.wait_ge(dve_done, VEs.n)
            dve.wait_ge(const_in, 16 * N_CONST)
            for b in range(B):
                ln("C", b, True, True)
            for b in range(B):
                def free(b=b):
                    if b < 2:
                        dve.wait_ge(pe_done, at("pe", "B.xT", b + 2))
                    else:
                        dve.wait_ge(pe_done, at("pe", "C.hT", TPB * (b - 2) + 1))
                        for i in range(TPB):
                            dve.wait_ge(h_stored[(TPB * b + i) % 4], 16)
                ln_apply("C", b, True, True, free)
                for t in range(TPB * b, TPB * b + TPB):
                    VEs(v.tensor_tensor(XS[:, t % 4, :], XS[:, t % 4, :], nwb, ALU.mult).then_inc(dve_done, 1), "C.h", t)
                for t in range(TPB * b, TPB * b + TPB):
                    dve.wait_ge(pe_done, at("pe", "C.logits", t))
                    L = bank(2 + t % 2)[:, 0, 0:E0]
                    VEs(v.max(top8[:, t, :], L).then_inc(dve_done, 1))
                    dve.wait_ge(dve_done, VEs.n)
                    VEs(v.max_index(idx8[:, t, :], top8[:, t, :], L).then_inc(dve_done, 1))
                    VEs(v.tensor_scalar(negm[:, t:t + 1], top8[:, t, 0:1], -1.0, None, ALU.mult).then_inc(dve_done, 1), "C.top", t)
                    dve.wait_ge(dve_done, VEs.n)
                    VEs(v.tensor_copy(idf, idx8[:, t, 0:K0]).then_inc(dve_done, 1))
                    dve.wait_ge(dve_done, VEs.n)
                    VEs(v.tensor_tensor(oh, iota32.rearrange("p (o e) -> p o e", o=1).broadcast_to((P, K0, E0)),
                                        idf.rearrange("p (k o) -> p k o", o=1).broadcast_to((P, K0, E0)), ALU.is_equal).then_inc(dve_done, 1))
                    VEs(v.tensor_scalar(base, idf, float(CAP), None, ALU.mult).then_inc(dve_done, 1))
                    dve.wait_ge(dve_done, VEs.n)
                    with nc.allow_low_precision(reason="0 and 1"):
                        VEs(v.tensor_reduce(sel_tile[:, t, :], oh.rearrange("p k e -> p e k"), AX.X, ALU.add).then_inc(dve_done, 1), "C.sel", t)
                    dve.wait_ge(pe_done, at("pe", "C.pos", t))
                    VEs(v.tensor_tensor(ohp, oh, bank(4 + t % 2)[:, 0, 0:E0].rearrange("p (o e) -> p o e", o=1).broadcast_to((P, K0, E0)),
                                        ALU.mult).then_inc(dve_done, 1), "C.ohp", t)
                    dve.wait_ge(dve_done, VEs.n)
                    VEs(v.tensor_reduce(posk, ohp, AX.X, ALU.add).then_inc(dve_done, 1))
                    dve.wait_ge(dve_done, VEs.n)
                    VEs(v.tensor_scalar(over, posk, float(CAP - 1), float(E0 * CAP), ALU.is_gt, ALU.mult).then_inc(dve_done, 1))
                    VEs(v.scalar_tensor_tensor(out=rowf, in0=posk, scalar=float(CAP - 1), in1=base, op0=ALU.min, op1=ALU.add).then_inc(dve_done, 1))
                    dve.wait_ge(dve_done, VEs.n)
                    VEs(v.tensor_tensor(slotf, rowf, over, ALU.add).then_inc(dve_done, 1))
                    VEs(v.tensor_copy(row[:, t, :], rowf).then_inc(dve_done, 1))
                    dve.wait_ge(dve_done, VEs.n)
                    VEs(v.tensor_copy(slot[:, t, :], slotf).then_inc(dve_done, 1), "C.slot", t)
                    dve.wait_ge(act_done, at("act", "C.ex4", t))
                    VEs(v.reciprocal(sm4[:, t:t + 1], sm4[:, t:t + 1]).then_inc(dve_done, 1))
                    dve.wait_ge(dve_done, VEs.n)
                    VEs(v.tensor_scalar(w4[:, t, :], ex4[:, t, :], sm4[:, t:t + 1], None, ALU.mult).then_inc(dve_done, 1), "C.w4", t)
            for hf in range(NHALF):
                dve.wait_ge(act_done, at("act", "C.sgs", hf))
                if hf:
                    dve.wait_ge(pe_done, at("pe", "C.sout", hf - 1))
                VEs(v.tensor_tensor(acs, sgs, bank(5)[:, 0, :], ALU.mult).then_inc(dve_done, 1), "C.sact", hf)
                dve.wait_ge(pe_done, at("pe", "C.sout", hf))
                for tt in range(HALF // P):
                    add_to_x(hf * 4 + tt, bank(6 + tt // 2)[:, 0, (tt % 2) * D:(tt % 2) * D + D], "C.xs", hf)
                dve.wait_ge(dve_done, VEs.n)
            dve.wait_ge(table_in, 16)
            VEs(v.tensor_copy(tabf[0:2 * E0, :], tab[0:2 * E0, :]).then_inc(dve_done, 1), "C.tabf")
            dve.wait_ge(pe_done, at("pe", "C.tabT"))
            VEs(v.tensor_copy(slot_tok, bank(6)[:, 0, 0:2 * E0]).then_inc(dve_done, 1), "C.slot_tok")

            def gated(e):
                dve.wait_ge(act_done, at("act", "C.sg", e))
                if e >= 2:
                    dve.wait_ge(pe_done, at("pe", "C.down", e - 2))
                VEs(v.tensor_tensor(ac[:, e % 2, :], sg[:, e % 2, :], bank(2 + e % 2)[:, 0, CAP:2 * CAP], ALU.mult).then_inc(dve_done, 1),
                    "C.act", e)

            for e in range(E0):
                dve.wait_ge(pe_done, at("pe", "C.xT", e))
                if e >= 2:
                    dve.wait_ge(pe_done, at("pe", "C.gu", e - 2))
                VEs(v.tensor_copy(XTc[:, e % 2], bank(e % 2)[:, 0, :].rearrange("p (k n) -> p k n", k=DB)).then_inc(dve_done, 1), "C.xT", e)
                if e:
                    gated(e - 1)
            gated(E0 - 1)
            for t in range(TILES):
                dve.wait_ge(y_in[t % 2], 16 * K0 * (t // 2 + 1))
                for k in range(K0):
                    VEs(v.scalar_tensor_tensor(out=X[:, t, :], in0=Y[:, t % 2, k, :], scalar=w4[:, t, k:k + 1], in1=X[:, t, :],
                                               op0=ALU.mult, op1=ALU.add).then_inc(dve_done, 1), "C.comb", t)
                    dve.wait_ge(dve_done, VEs.n)
            book[("dve", "C.end")] = VEs.n

            dve.wait_ge(act_done, at("act", "D.A"))
            VEs(v.tensor_scalar(Aneg, Aneg, -1.0, None, ALU.mult).then_inc(dve_done, 1), "D.A")
            dve.wait_ge(mamba_w_in, 16 * N_MAMBA)
            VEs(v.tensor_copy(wdt, wxp[:, :, 32:33].broadcast_to((P, IB, P))).then_inc(dve_done, 1), "D.wdt")
            for b in range(B):
                ln("D", b, True, True)
            for hf in range(NHALF):
                for b in range(BPH * hf, BPH * hf + BPH):
                    def free(b=b):
                        if b < 2:
                            dve.wait_ge(pe_done, at("pe", "C.hT", TILES - 1))
                            for i in range(4):
                                dve.wait_ge(h_stored[i], 16 * TILES // 4)
                        else:
                            dve.wait_ge(pe_done, at("pe", "D.xT", 0))
                    ln_apply("D", b, True, True, free)
                for m in range(IB):
                    dve.wait_ge(act_done, at("act", "D.xi", hf, m))
                    if hf:
                        dve.wait_ge(dve_done, VEs.n)
                        dve.wait_ge(pe_done, at("pe", "D.xs", hf - 1))
                    um = u[:, m, :].rearrange("p (b s) -> p b s", b=BPH)
                    VEs(v.tensor_scalar(um, xi[:, m, :, 0:S], cw[:, m, 0:1], cb[:, m:m + 1], ALU.mult, ALU.add).then_inc(dve_done, 1))
                    for k in range(1, KC):
                        dve.wait_ge(dve_done, VEs.n)
                        VEs(v.scalar_tensor_tensor(out=um, in0=xi[:, m, :, k:k + S], scalar=cw[:, m, k:k + 1], in1=um,
                                                   op0=ALU.mult, op1=ALU.add).then_inc(dve_done, 1), "D.conv", hf, m)
                dve.wait_ge(pe_done, at("pe", "D.xs", hf))
                R = 2 * NST
                if hf:
                    dve.wait_ge(pe_done, at("pe", "D.C", hf * NST - 1))
                VEs(v.tensor_copy(xs3f[0:R, :], bank(7)[0:R, 0, :]).then_inc(dve_done, 1), "D.xsf", hf)
                dve.wait_ge(dve_done, VEs.n)
                VEs(v.tensor_copy(xs3[0:R, :], xs3f[0:R, :]).then_inc(dve_done, 1))
                for i in range(1, 3):
                    dve.wait_ge(dve_done, VEs.n)
                    VEs(v.tensor_tensor(xs3f[0:R, :], xs3f[0:R, :], xs3[0:R, :] if i == 1 else xs3m[0:R, :], ALU.subtract).then_inc(dve_done, 1))
                    dve.wait_ge(dve_done, VEs.n)
                    if i == 1:
                        VEs(v.tensor_copy(xs3m[0:R, :], xs3f[0:R, :]).then_inc(dve_done, 1))
                        dve.wait_ge(dve_done, VEs.n)
                    VEs(v.tensor_copy(xs3[R * i:R * i + R, :], xs3f[0:R, :]).then_inc(dve_done, 1), "D.xs3", hf)
                dve.wait_ge(pe_done, at("pe", "D.dt", hf))
                for m in range(IB):
                    if hf and m == 0:
                        dve.wait_ge(act_done, at("act", "D.dA", hf * NST - 1))
                    VEs(v.tensor_scalar(dt[:, m, :], bank(6)[:, 0, :], dtw[:, m:m + 1], dtb[:, m:m + 1], ALU.mult, ALU.add).then_inc(dve_done, 1), "D.v", hf, m)
                dve.wait_ge(act_done, at("act", "D.sp", hf))
                VEs(v.scalar_tensor_tensor(out=dt, in0=dt, scalar=0.0, in1=e1, op0=ALU.max, op1=ALU.add).then_inc(dve_done, 1))
                dve.wait_ge(dve_done, VEs.n)
                VEs(v.tensor_tensor(dtu, dt, u, ALU.mult).then_inc(dve_done, 1), "D.dtu", hf)
                flat = "p m n -> p (m n)"
                for n in range(NST):
                    s = hf * NST + n
                    dve.wait_ge(pool_done, at("pool", "D.Bu", s))
                    dve.wait_ge(act_done, at("act", "D.dA", s))
                    h = hb_[:, s % NHB]
                    VEs(v.tensor_tensor_scan(h.rearrange(flat), dA[:, s % 2].rearrange(flat), h.rearrange(flat), 0.0,
                                             ALU.mult, ALU.add).then_inc(dve_done, 1), "D.scan", s)
                    dve.wait_ge(dve_done, VEs.n)
                    dve.wait_ge(pe_done, at("pe", "D.C", s))
                    VEs(v.tensor_tensor(h, h, bank(4 + s % 2).broadcast_to((P, IB, HALF)), ALU.mult).then_inc(dve_done, 1), "D.hC", s)
                dve.wait_ge(pe_done, at("pe", "D.sum", hf * NST + NST - 1))
                for m in range(IB):
                    VEs(v.scalar_tensor_tensor(out=u[:, m, :], in0=u[:, m, :], scalar=dpar[:, m:m + 1], in1=bank(m)[:, 0, :],
                                               op0=ALU.mult, op1=ALU.add).then_inc(dve_done, 1), "D.yu", hf)
                dve.wait_ge(dve_done, VEs.n)
                for m in range(IB):
                    dve.wait_ge(act_done, at("act", "D.sz", hf, m))
                    VEs(v.tensor_tensor(sz[:, m, :], sz[:, m, :], u[:, m, :], ALU.mult).then_inc(dve_done, 1), "D.yz", hf, m)
                dve.wait_ge(pe_done, at("pe", "D.out", hf))
                for tt in range(HALF // P):
                    add_to_x(hf * 4 + tt, bank(4 + tt // 2)[:, 0, (tt % 2) * D:(tt % 2) * D + D], "D.x", hf)
            book[("dve", "D.end")] = VEs.n

            dve.wait_ge(xattn1_w_in, 16 * N_XATTN1)
            VEs(v.tensor_scalar(mrowb[0:1, :], mrow[0:1].rearrange("p b s -> p (b s)"), 1.0, -NEG, ALU.subtract, ALU.mult).then_inc(dve_done, 1), "E.mrow")
            VEs(v.tensor_reduce(mflag, vfl, AX.X, ALU.max).then_inc(dve_done, 1))
            VEs(v.memset(one1, 1.0).then_inc(dve_done, 1), "E.one")
            dve.wait_ge(dve_done, VEs.n)
            for b in range(B):
                ln("E", b, False, False)

                def free(b=b):
                    dve.wait_ge(pe_done, at("pe", "E.xT", b - 1) if b else at("pe", "D.xT", NHALF - 1))
                ln_apply("E", b, False, False, free)
                for i in range(4):
                    dve.wait_ge(pe_done, at("pe", "E.v", b, i))
                    if b and i == 0:
                        dve.wait_ge(pe_done, at("pe", "E.av", b - 1, 3, 1))
                    VEs(v.tensor_copy(V1[:, i // 2, 512 * (i % 2):512 * (i % 2) + 512], bank(i)[:, 0, :]).then_inc(dve_done, 1), "E.v", b, i)
                for hg in range(4):
                    for qt in range(TPB):
                        n = (b * 4 + hg) * 2 + qt
                        dve.wait_ge(pe_done, at("pe", "E.S", b, hg, qt))
                        if n >= 2:
                            dve.wait_ge(act_done, at("act", "E.P", *prev1(n - 2)))
                        VEs(v.tensor_reduce(mxe[:, n % 2, :], bank(2 * (n % 2), 2).rearrange("p w (g k) -> p (w g) k", g=2),
                                            AX.X, ALU.max, negate=True).then_inc(dve_done, 1), "E.max", b, hg, qt)
                        dve.wait_ge(act_done, at("act", "E.P", b, hg, qt))
                        VEs(v.reciprocal(rie[:, n % 2, :], rse[:, n % 2, :]).then_inc(dve_done, 1))
                        dve.wait_ge(dve_done, VEs.n)
                        for i in range(4):
                            VEs(v.tensor_scalar(Pe[:, n % 2, i, :], Pe[:, n % 2, i, :], rie[:, n % 2, i:i + 1], mflag[:, b:b + 1],
                                                ALU.mult, ALU.mult).then_inc(dve_done, 1), "E.Pn", b, hg, qt)
                        dve.wait_ge(pe_done, at("pe", "E.PT", b, hg, qt))
                        if n >= 2:
                            dve.wait_ge(pe_done, at("pe", "E.av", *prev1(n - 2)))
                        VEs(v.tensor_copy(PTe[:, n % 2, 2:4], bank(5)[:, 0, :].rearrange("p (i k q) -> p i k q", i=2, k=2))
                            .then_inc(dve_done, 1), "E.PT", b, hg, qt)
                for qt in range(TPB):
                    dve.wait_ge(pe_done, at("pe", "E.o", b, TPB - 1))
                    add_to_x(TPB * b + qt, bank(7)[:, 0, qt * D:qt * D + D], "E.x", b, qt)
                dve.wait_ge(dve_done, VEs.n)

            for b in range(B):
                ln("F", b, False, False)
            for b in range(B):
                def free(b=b):
                    dve.wait_ge(pe_done, at("pe", "F.xT", b - 2) if b >= 2 else at("pe", "E.xT", B - 1))
                ln_apply("F", b, False, False, free)
            dve.wait_ge(const_in, 16 * N_CONST)
            dve.wait_ge(ffn1_w_in, 16 * N_FFN1)
            for t in range(TILES):
                dve.wait_ge(pe_done, at("pe", "F.logits", t))
                VEs(v.tensor_copy(lg[:, t, :], bank(2 + t % 2)[:, 0, 0:E1 + 1]).then_inc(dve_done, 1), "F.lg", t)
                dve.wait_ge(dve_done, VEs.n)
                VEs(v.tensor_reduce(np8[:, t:t + 1], lg[:, t, 0:E1], AX.X, ALU.max, negate=True).then_inc(dve_done, 1), "F.max", t)
                dve.wait_ge(act_done, at("act", "F.pr", t))
                VEs(v.reciprocal(rp[:, t:t + 1], sp1[:, t:t + 1]).then_inc(dve_done, 1))
                VEs(v.tensor_scalar(cc[:, t, E1:], lg[:, t, E1:], 1.0, None, ALU.add).then_inc(dve_done, 1))
                dve.wait_ge(dve_done, VEs.n)
                VEs(v.tensor_scalar(pr[:, t, :], pr[:, t, :], rp[:, t:t + 1], None, ALU.mult).then_inc(dve_done, 1))
                VEs(v.reciprocal(cc[:, t, E1:], cc[:, t, E1:]).then_inc(dve_done, 1))
                dve.wait_ge(dve_done, VEs.n)
                VEs(v.max(tp8[:, t, :], pr[:, t, :]).then_inc(dve_done, 1))
                dve.wait_ge(dve_done, VEs.n)
                VEs(v.max_index(ti8[:, t, :], tp8[:, t, :], pr[:, t, :]).then_inc(dve_done, 1))
                dve.wait_ge(dve_done, VEs.n)
                VEs(v.tensor_copy(tif[:, t, :], ti8[:, t, 0:2]).then_inc(dve_done, 1))
                dve.wait_ge(dve_done, VEs.n)
                VEs(v.tensor_scalar(cc[:, t, 0:E1], iota8, tif[:, t, 0:1], tp8[:, t, 0:1], ALU.is_equal, ALU.mult).then_inc(dve_done, 1))
                VEs(v.tensor_scalar(c2[:, t, :], iota8, tif[:, t, 1:2], tp8[:, t, 1:2], ALU.is_equal, ALU.mult).then_inc(dve_done, 1))
                dve.wait_ge(dve_done, VEs.n)
                VEs(v.tensor_tensor(cc[:, t, 0:E1], cc[:, t, 0:E1], c2[:, t, :], ALU.add).then_inc(dve_done, 1))
                dve.wait_ge(dve_done, VEs.n)
                W = E1 + 1
                VEs(v.tensor_copy(chb[:, 0:W], cc[:, t, :]).then_inc(dve_done, 1))
                dve.wait_ge(dve_done, VEs.n)
                VEs(v.tensor_copy(c27[:, t, 0:W], chb[:, 0:W]).then_inc(dve_done, 1))
                VEs(v.tensor_tensor(r1c, cc[:, t, :], chb[:, 0:W], ALU.subtract).then_inc(dve_done, 1))
                dve.wait_ge(dve_done, VEs.n)
                VEs(v.tensor_copy(cmb[:, 0:W], r1c).then_inc(dve_done, 1))
                dve.wait_ge(dve_done, VEs.n)
                VEs(v.tensor_copy(c27[:, t, W:2 * W], cmb[:, 0:W]).then_inc(dve_done, 1))
                VEs(v.tensor_tensor(c27[:, t, 2 * W:], r1c, cmb[:, 0:W], ALU.subtract).then_inc(dve_done, 1), "F.c27", t)
                dve.wait_ge(dve_done, VEs.n)
            for hf in range(NHALF):
                for f in range(FB):
                    n = hf * FB + f
                    m = min(P, FT - f * P)
                    dve.wait_ge(act_done, at("act", "F.sg", n))
                    VEs(v.tensor_tensor(tf[0:m, n % 2, :], sgf[0:m, n % 2, :], bank(2 + n % 2)[0:m, 0, :], ALU.mult).then_inc(dve_done, 1))
                    dve.wait_ge(dve_done, VEs.n)
                    if n >= 3:
                        dve.wait_ge(pe_done, at("pe", "F.down", n - 3))
                    VEs(v.tensor_tensor(acf[0:m, n % 3, :], tf[0:m, n % 2, :], bank(4 + n % 2)[0:m, 0, :], ALU.mult).then_inc(dve_done, 1), "F.act", n)
                dve.wait_ge(pe_done, at("pe", "F.down", hf * FB + FB - 1))
                for tt in range(HALF // P):
                    add_to_x(hf * 4 + tt, bank(6 + tt // 2)[:, 0, (tt % 2) * D:(tt % 2) * D + D], "F.x", hf * 4 + tt)

        @block.tensor
        def _(pe):
            te = nc.tensor

            def mm(dst, lhsT, rhs, start=True, stop=True, **kw):
                return te.matmul(dst, lhsT, rhs, start=start, stop=stop, **kw)

            def transposes(dst, name, b, step):
                pe.wait_ge(dve_done, at("dve", name + ".xs", b))
                for tt in range(TPB):
                    for k in range(DB):
                        last = te.transpose(dst[:, k, tt * P:tt * P + P], XS[:, (TPB * b + tt) % 4, k * P:k * P + P], ident[:, :])
                PEs(last.then_inc(pe_done, 1), *step)

            pe.wait_ge(const_in, 16 * N_CONST)
            pe.wait_ge(ctx_in, 16)
            pe.wait_ge(xattn_w_in, 16 * N_XATTN)
            for i in range(2):
                for t in range(4):
                    last = te.transpose(bank(i)[:, 0, t * P:t * P + P], cx[:, 4 * i + t, :], ident[:, :])
                PEs(last.then_inc(pe_done, 1), "ctxT", i)
            for i in range(4):
                pe.wait_ge(act_done, at("act", "ctxT", i % 2))
                PEs(mm(bank(2 + i)[:, 0, :], (wq0, wk0)[i // 2], ctxT[:, 512 * (i % 2):512 * (i % 2) + 512]).then_inc(pe_done, 1), "qk0", i)

            def energy(t):
                if t == 0:
                    pe.wait_ge(act_done, at("act", "qk0", 3))
                if t >= 2:
                    pe.wait_ge(act_done, at("act", "en", t - 2))
                b = t // 2
                PEs(mm(bank(t % 2)[:, 0, 0:S], q0[:, t * P:t * P + P], k0[:, b * S:b * S + S]).then_inc(pe_done, 1), "en", t)

            energy(0)
            for t in range(TILES):
                if t + 1 < TILES:
                    energy(t + 1)
                pe.wait_ge(dve_done, at("dve", "enn", t))
                if t >= 2:
                    pe.wait_ge(dve_done, at("dve", "attT", t - 2))
                for m in range(2):
                    last = te.transpose(bank(2 + t % 2)[:, 0, m * P:m * P + P], en[:, t % 2, m * P:m * P + P], ident[:, :])
                PEs(last.then_inc(pe_done, 1), "attT", t)

            pe.wait_ge(attn_w_in, 16 * N_ATTN)
            for b in range(B):
                if b:
                    pe.wait_ge(dve_done, at("dve", "A.x", b - 1, TPB - 1))
                transposes(bank(7)[:, 0, :].rearrange("p (k n) -> p k n", k=DB), "A", b, ("A.xT", b))
                pe.wait_ge(act_done, at("act", "A.xT", b))
                for tt in range(TPB):
                    if tt:
                        pe.wait_ge(act_done, at("act", "A.V", b, tt - 1))
                        pe.wait_ge(dve_done, at("dve", "A.qk", b, tt - 1))
                    elif b:
                        pe.wait_ge(dve_done, at("dve", "A.ctx", b - 1, TPB - 1))
                    for k in range(DB):
                        mm(bank(6)[:, 0, :], xTa[:, b % 2, k, tt * P:tt * P + P], w_in[:, k, 0:512], k == 0, k == DB - 1)
                    for k in range(DB):
                        last = mm(bank(7)[:, 0, 0:D], xTa[:, b % 2, k, tt * P:tt * P + P], w_in[:, k, 512:768], k == 0, k == DB - 1)
                    PEs(last.then_inc(pe_done, 1), "A.qkv", b, tt)
                for tt in range(TPB):
                    pe.wait_ge(dve_done, at("dve", "A.rope", b, tt))
                    if tt:
                        pe.wait_ge(act_done, at("act", "A.QT", b, tt - 1))
                    elif b:
                        pe.wait_ge(act_done, at("act", "A.PT", b - 1, TPB - 1, 3))
                        pe.wait_ge(dve_done, at("dve", "A.PT", b - 1, TPB - 1, 3))
                    for w in range(2):
                        for g in range(4):
                            last = te.transpose(bank(4 + w)[:, 0, g * P:g * P + P],
                                                QP[:, tt, w, 4 * g:4 * g + 4, :].rearrange("p h d -> p (h d)"), ident[:, :])
                    PEs(last.then_inc(pe_done, 1), "A.qkT", b, tt)

                def scores(n):
                    bb, tt, j = prev(n)
                    pe.wait_ge(act_done, at("act", "A.QT", bb, TPB - 1))
                    if n >= 2:
                        pe.wait_ge(act_done, at("act", "A.P", *prev(n, 2)))
                    elif n == 0:
                        pe.wait_ge(dve_done, at("dve", "attT", TILES - 1))
                    for gg in range(2):
                        for jj in range(2):
                            h = head0(j, 2 * jj + gg)
                            g, r = h // 4, 32 * (h % 4)
                            last = mm(bank(2 * (n % 2) + jj)[:, 0, gg * S:gg * S + S], QT[r:r + DH0, 0, g, tt * P:tt * P + P],
                                      QT[r:r + DH0, 1, g, :])
                    PEs(last.then_inc(pe_done, 1), "A.S", bb, tt, j)

                n0 = b * TPB * 4
                scores(n0)
                for n in range(n0, n0 + TPB * 4):
                    _, tt, j = prev(n)
                    if n + 1 < n0 + TPB * 4:
                        scores(n + 1)
                    pe.wait_ge(act_done, at("act", "A.P", b, tt, j))
                    if n % (TPB * 4):
                        pe.wait_ge(act_done, at("act", "A.PT", *prev(n, 1)))
                        pe.wait_ge(dve_done, at("dve", "A.PT", *prev(n, 1)))
                    for i in range(4):
                        for k in range(2):
                            o = (i % 2) * 2 + k
                            last = te.transpose(bank(4 + i // 2)[:, 0, o * P:o * P + P], Pa[:, n % 2, i, k * P:k * P + P], ident[:, :])
                    PEs(last.then_inc(pe_done, 1), "A.PT", b, tt, j)
                    pe.wait_ge(act_done, at("act", "A.PT", b, tt, j))
                    pe.wait_ge(dve_done, at("dve", "A.PT", b, tt, j))
                    if tt and j == 0:
                        pe.wait_ge(dve_done, at("dve", "A.ctx", b, tt - 1))
                    for i in range(4):
                        h = head0(j, i)
                        for k in range(2):
                            last = mm(bank(6)[:, 0, h * DH0:h * DH0 + DH0], PTa[:, n % 2, i, k, :], Va[:, b % 2, k, h * DH0:h * DH0 + DH0],
                                      k == 0, k == 1)
                    PEs(last.then_inc(pe_done, 1), "A.av", b, tt, j)
                    if j == 3:
                        pe.wait_ge(dve_done, at("dve", "A.ctx", b, tt))
                        if tt:
                            pe.wait_ge(dve_done, at("dve", "A.x", b, tt - 1))
                        for k in range(DB):
                            last = te.transpose(bank(7)[:, 0, k * P:k * P + P], Ca[:, k * P:k * P + P], ident[:, :])
                        PEs(last.then_inc(pe_done, 1), "A.cT", b, tt)
                        pe.wait_ge(act_done, at("act", "A.cT", b, tt))
                        for k in range(DB):
                            last = mm(bank(7)[:, 0, D:2 * D], CTa[:, k, :], w_out[:, k, :], k == 0, k == DB - 1)
                        PEs(last.then_inc(pe_done, 1), "A.out", b, tt)

            for b in range(B):
                if b >= 2:
                    pe.wait_ge(act_done, at("act", "B.xT", b - 2))
                transposes(bank(b % 2)[:, 0, :].rearrange("p (k n) -> p k n", k=DB), "B", b, ("B.xT", b))
                pe.wait_ge(act_done, at("act", "B.xT", b))
                if b >= 2:
                    pe.wait_ge(dve_done, at("dve", "B.x", b - 2, 1))
                for tt in range(TPB):
                    for k in range(DB):
                        last = mm(bank(2 + b % 2)[:, 0, tt * D:tt * D + D], xTb[:, b % 2, k, tt * P:tt * P + P], attT[:, b, k, :], k == 0, k == DB - 1)
                PEs(last.then_inc(pe_done, 1), "B.out", b)
            book[("pe", "B.end")] = PEs.n

            pe.wait_ge(moe_w_in, 16 * N_MOE)
            pe.wait_ge(pool_done, at("pool", "ones"))
            pe.wait_ge(dve_done, at("dve", "B.end"))
            for t in range(TILES):
                pe.wait_ge(dve_done, at("dve", "C.h", t))
                if t >= 2:
                    pe.wait_ge(act_done, at("act", "C.hT", t - 2))
                for k in range(DB):
                    last = te.transpose(bank(t % 2)[:, 0, k * P:k * P + P], XS[:, t % 4, k * P:k * P + P], ident[:, :])
                PEs(last.then_inc(pe_done, 1), "C.hT", t)
                pe.wait_ge(act_done, at("act", "C.hT", t))
                if t >= 2:
                    pe.wait_ge(dve_done, at("dve", "C.top", t - 2))
                for k in range(DB):
                    last = mm(bank(2 + t % 2)[:, 0, 0:E0], hT[:, k, t * P:t * P + P], gw[:, k, :], k == 0, k == DB - 1)
                PEs(last.then_inc(pe_done, 1), "C.logits", t)
                pe.wait_ge(dve_done, at("dve", "C.sel", t))
                if t >= 2:
                    pe.wait_ge(dve_done, at("dve", "C.ohp", t - 2))
                for i in range(t):
                    mm(bank(4 + t % 2)[:, 0, 0:E0], ones, sel_tile[:, i, :], i == 0, False)
                PEs(mm(bank(4 + t % 2)[:, 0, 0:E0], tri, sel_tile[:, t, :], t == 0, True).then_inc(pe_done, 1), "C.pos", t)
            pe.wait_ge(dve_done, at("dve", "C.slot", TILES - 1))
            for hf in range(NHALF):
                if hf:
                    pe.wait_ge(dve_done, at("dve", "C.xs", hf - 1))
                for w in range(2):
                    for k in range(DB):
                        last = mm(bank(4 + w)[:, 0, :], sgu[:, k, w * I0:w * I0 + I0], hT[:, k, hf * HALF:hf * HALF + HALF], k == 0, k == DB - 1)
                PEs(last.then_inc(pe_done, 1), "C.sgu", hf)
                pe.wait_ge(dve_done, at("dve", "C.sact", hf))
                for tt in range(HALF // P):
                    last = mm(bank(6 + tt // 2)[:, 0, (tt % 2) * D:(tt % 2) * D + D], acs[:, tt * P:tt * P + P], sdn)
                PEs(last.then_inc(pe_done, 1), "C.sout", hf)
            pe.wait_ge(dve_done, at("dve", "C.tabf"))
            PEs(te.transpose(bank(6)[:, 0, 0:2 * E0], tabf[0:2 * E0, :], ident[0:2 * E0, 0:2 * E0]).then_inc(pe_done, 1), "C.tabT")

            def expert_rows(e):
                pe.wait_ge(gathered[e % 4], 16 * 2 * (e // 4 + 1))
                if e >= 2:
                    pe.wait_ge(dve_done, at("dve", "C.xT", e - 2))
                for s in range(2):
                    for k in range(DB):
                        last = te.transpose(bank(e % 2)[:, 0, k * CAP + s * P:k * CAP + s * P + P], G[:, e % 4, s, k * P:k * P + P], ident[:, :])
                PEs(last.then_inc(pe_done, 1), "C.xT", e)

            def expert_up(e):
                pe.wait_ge(dve_done, at("dve", "C.xT", e))
                pe.wait_ge(expert_in[e % NW], 32 * (e // NW + 1))
                if e >= 2:
                    pe.wait_ge(dve_done, at("dve", "C.act", e - 2))
                for w in range(2):
                    for k in range(DB):
                        last = mm(bank(2 + e % 2)[:, 0, w * CAP:w * CAP + CAP], w13[:, e % NW, k, w * I0:w * I0 + I0], XTc[:, e % 2, k, :],
                                  k == 0, k == DB - 1)
                PEs(last.then_inc(pe_done, 1), "C.gu", e)

            def expert_down(e):
                pe.wait_ge(dve_done, at("dve", "C.act", e))
                if e >= 2:
                    pe.wait_ge(act_done, at("act", "C.eo", e - 2))
                for s in range(2):
                    last = mm(bank(4 + e % 2)[:, 0, s * D:s * D + D], ac[:, e % 2, s * P:s * P + P], w2[:, e % NW, :])
                PEs(last.then_inc(pe_done, 1), "C.down", e)

            expert_rows(0)
            expert_up(0)
            for e in range(E0):
                if e + 1 < E0:
                    expert_rows(e + 1)
                    expert_up(e + 1)
                expert_down(e)

            pe.wait_ge(mamba_w_in, 16 * N_MAMBA)
            pe.wait_ge(act_done, at("act", "C.eo", E0 - 1))
            pe.wait_ge(dve_done, at("dve", "D.wdt"))
            for hf in range(NHALF):
                if hf:
                    pe.wait_ge(act_done, at("act", "D.Bb", hf * NST - 1))
                    pe.wait_ge(dve_done, at("dve", "D.yu", hf - 1))
                for b in range(BPH * hf, BPH * hf + BPH):
                    pe.wait_ge(dve_done, at("dve", "D.xs", b))
                    for tt in range(TPB):
                        for k in range(DB):
                            o = (b % BPH) * S + tt * P
                            last = te.transpose(bank(6 + k)[:, 0, o:o + P], XS[:, (TPB * b + tt) % 4, k * P:k * P + P], ident[:, :])
                PEs(last.then_inc(pe_done, 1), "D.xT", hf)
                pe.wait_ge(act_done, at("act", "D.xT", hf))
                for m in range(2 * IB):
                    if m >= IB + 2:
                        pe.wait_ge(act_done, at("act", "D.sz", hf, m - IB - 2))
                    elif m >= IB and hf:
                        pe.wait_ge(dve_done, at("dve", "D.x", hf - 1))
                    dst = bank(m if m < IB else 4 + m % 2)[:, 0, :]
                    for k in range(DB):
                        last = mm(dst, wip[:, k, m * P:m * P + P], xTd[:, k, :], k == 0, k == DB - 1)
                    PEs(last.then_inc(pe_done, 1), *(("D.xi", hf, m) if m < IB else ("D.z", hf, m - IB)))
                pe.wait_ge(act_done, at("act", "D.u", hf, IB - 1))
                for m in range(IB):
                    last = mm(bank(7)[0:33, 0, :], wxp[:, m, :], u[:, m, :], m == 0, m == IB - 1)
                for m in range(IB):
                    last = mm(bank(6)[:, 0, :], wdt[:, m, :], u[:, m, :], m == 0, m == IB - 1)
                    if m == IB - 1:
                        PEs(last.then_inc(pe_done, 1), "D.xs", hf)
                        book[("pe", "D.dt", hf)] = PEs.n
                pe.wait_ge(dve_done, at("dve", "D.v", hf, IB - 1))
                pe.wait_ge(dve_done, at("dve", "D.xs3", hf))
                pe.wait_ge(act_done, at("act", "D.sz", hf, IB - 1))

                def spread(s):
                    n = s % NST
                    if n:
                        pe.wait_ge(act_done, at("act", "D.Bb", s - 1))
                    PEs(mm(bank(6)[:, 0, :], selbc[0:96, n, :], xs3[0:96, :]).then_inc(pe_done, 1), "D.B", s)
                    if n >= 2:
                        pe.wait_ge(dve_done, at("dve", "D.hC", s - 2))
                    PEs(mm(bank(4 + s % 2)[:, 0, :], selbc[0:96, NST + n, :], xs3[0:96, :]).then_inc(pe_done, 1), "D.C", s)

                s0_ = hf * NST
                spread(s0_)
                spread(s0_ + 1)
                for s in range(s0_, s0_ + NST):
                    pe.wait_ge(dve_done, at("dve", "D.hC", s))
                    for m in range(IB):
                        last = mm(bank(m)[:, 0, :], ident[:, :], hb_[:, s % NHB, m, :], s == s0_, s == s0_ + NST - 1)
                    PEs(last.then_inc(pe_done, 1), "D.sum", s)
                    if s + 2 < s0_ + NST:
                        spread(s + 2)
                for tt in range(HALF // P):
                    for m in range(IB):
                        pe.wait_ge(dve_done, at("dve", "D.yz", hf, m))
                        last = mm(bank(4 + tt // 2)[:, 0, (tt % 2) * D:(tt % 2) * D + D], sz[:, m, tt * P:tt * P + P], wop[:, m, :], m == 0, m == IB - 1)
                PEs(last.then_inc(pe_done, 1), "D.out", hf)
            book[("pe", "D.end")] = PEs.n

            pe.wait_ge(xattn1_w_in, 16 * N_XATTN1)
            pe.wait_ge(dve_done, at("dve", "E.one"))
            pe.wait_ge(dve_done, at("dve", "D.x", NHALF - 1))
            for b in range(B):
                if b:
                    pe.wait_ge(dve_done, at("dve", "E.x", b - 1, TPB - 1))
                transposes(bank(7)[:, 0, :].rearrange("p (k n) -> p k n", k=DB), "E", b, ("E.xT", b))
                for i in range(4):
                    if i >= 2:
                        pe.wait_ge(act_done, at("act", "E.k", b, i - 2))
                    elif b:
                        pe.wait_ge(act_done, at("act", "E.PT", b - 1, 3, 1))
                        pe.wait_ge(dve_done, at("dve", "E.PT", b - 1, 3, 1))
                    for j in range(2):
                        last = mm(bank(4 + i % 2)[:, 0, j * S:j * S + S], wk1[:, (2 * i + j) * P:(2 * i + j + 1) * P], ctxT[:, b * S:b * S + S])
                    PEs(last.then_inc(pe_done, 1), "E.k", b, i)
                for i in range(4):
                    if b:
                        pe.wait_ge(act_done, at("act", "E.P", b - 1, 3, 1))
                    PEs(mm(bank(i)[:, 0, :], ctxT[:, b * S + (i // 2) * P:b * S + (i // 2) * P + P], wv1[:, (i % 2) * 512:(i % 2) * 512 + 512])
                        .then_inc(pe_done, 1), "E.v", b, i)
                pe.wait_ge(act_done, at("act", "E.xT", b))

                def queries(hg):
                    for i in range(2):
                        if i:
                            pe.wait_ge(act_done, at("act", "E.q", b, hg, 0))
                        elif hg:
                            pe.wait_ge(act_done, at("act", "E.q", b, hg - 1, 1))
                        for j in range(2):
                            h = 4 * hg + 2 * i + j
                            for k in range(DB):
                                last = mm(bank(7)[:, 0, j * S:j * S + S], wq1[:, k, h * P:h * P + P], xTe[:, k, :], k == 0, k == DB - 1)
                        PEs(last.then_inc(pe_done, 1), "E.q", b, hg, i)

                def scores1(n):
                    _, hg, qt = prev1(n)
                    pe.wait_ge(act_done, at("act", "E.q", b, hg, 1))
                    if n % 8 == 0:
                        pe.wait_ge(act_done, at("act", "E.k", b, 3))
                        pe.wait_ge(dve_done, at("dve", "E.v", b, 3))
                    if n >= 2:
                        pe.wait_ge(act_done, at("act", "E.P", *prev1(n - 2)))
                    for w in range(2):
                        dst = bank(2 * (n % 2) + w)[:, 0, :]
                        for j in range(2):
                            mm(dst[:, j * S:j * S + S], QE[:, hg % 2, 2 * w + j, qt * P:qt * P + P], kT[:, 2 * hg + w, :], j == 0, False,
                               skip_group_check=True)
                        mr = mrowb[0:1, b * S:b * S + S].rearrange("p (o s) -> p o s", o=1).broadcast_to((1, 2, S))
                        last = mm(dst.rearrange("p (o s) -> p o s", o=2), one1[0:1, :], mr, False, True, skip_group_check=True)
                    PEs(last.then_inc(pe_done, 1), "E.S", b, hg, qt)

                n0 = b * 8
                queries(0)
                scores1(n0)
                for n in range(n0, n0 + 8):
                    _, hg, qt = prev1(n)
                    if n + 1 < n0 + 8:
                        scores1(n + 1)
                    pe.wait_ge(dve_done, at("dve", "E.Pn", b, hg, qt))
                    if n % 8:
                        pe.wait_ge(act_done, at("act", "E.PT", *prev1(n - 1)))
                        pe.wait_ge(dve_done, at("dve", "E.PT", *prev1(n - 1)))
                    for i in range(4):
                        for k in range(2):
                            o = (i % 2) * 2 + k
                            last = te.transpose(bank(4 + i // 2)[:, 0, o * P:o * P + P], Pe[:, n % 2, i, k * P:k * P + P], ident[:, :])
                    PEs(last.then_inc(pe_done, 1), "E.PT", b, hg, qt)
                    pe.wait_ge(act_done, at("act", "E.PT", b, hg, qt))
                    pe.wait_ge(dve_done, at("dve", "E.PT", b, hg, qt))
                    if n:
                        pe.wait_ge(act_done, at("act", "E.OT", *prev1(n - 1)))
                    for w in range(2):
                        for k in range(2):
                            kv = 2 * hg + w
                            last = mm(bank(6)[:, 0, w * 2 * P:w * 2 * P + 2 * P].rearrange("p (i q) -> p i q", i=2), V1[:, k, kv * P:kv * P + P],
                                      PTe[:, n % 2, 2 * w:2 * w + 2, k, :], k == 0, k == 1)
                    PEs(last.then_inc(pe_done, 1), "E.av", b, hg, qt)
                    if qt == 0 and hg + 1 < 4:
                        queries(hg + 1)
                for qt in range(TPB):
                    pe.wait_ge(act_done, at("act", "E.OT", b, 3, qt))
                    for h in range(H1):
                        last = mm(bank(7)[:, 0, qt * D:qt * D + D], OT[:, h, qt * P:qt * P + P], wo1[:, h, :], h == 0, h == H1 - 1)
                    PEs(last.then_inc(pe_done, 1), "E.o", b, qt)

            pe.wait_ge(ffn1_w_in, 16 * N_FFN1)
            pe.wait_ge(dve_done, at("dve", "E.x", B - 1, TPB - 1))
            for b in range(B):
                if b >= 2:
                    pe.wait_ge(act_done, at("act", "F.xT", b - 2))
                transposes(bank(b % 2)[:, 0, :].rearrange("p (k n) -> p k n", k=DB), "F", b, ("F.xT", b))

            def weights_turned(t):
                pe.wait_ge(dve_done, at("dve", "F.c27", t))
                if t >= 2:
                    pe.wait_ge(act_done, at("act", "F.cT", t - 2))
                PEs(te.transpose(bank(4 + t % 2)[0:27, 0, 0:P], c27[:, t, :], ident[:, :]).then_inc(pe_done, 1), "F.cT", t)

            for t in range(TILES):
                pe.wait_ge(act_done, at("act", "F.xT", t // TPB))
                if t >= 2:
                    pe.wait_ge(dve_done, at("dve", "F.lg", t - 2))
                o = (t % 4) * P
                for k in range(DB):
                    last = mm(bank(2 + t % 2)[:, 0, 0:E1 + 1], xTf[:, t // 4, k, o:o + P], wr[:, k, :], k == 0, k == DB - 1)
                PEs(last.then_inc(pe_done, 1), "F.logits", t)
                if t:
                    weights_turned(t - 1)
            weights_turned(TILES - 1)
            pe.wait_ge(act_done, at("act", "F.cT", TILES - 1))

            def up(n):
                hf, f = n // FB, n % FB
                m = min(P, FT - f * P)
                if n >= 2:
                    pe.wait_ge(dve_done, at("dve", "F.act", n - 2))
                for w_, bk in ((wg, n % 2), (wu, 2 + n % 2)):
                    for k in range(DB):
                        mm(bank(bk)[0:m, 0, :], w_[:, k, f * P:f * P + m], xTf[:, hf, k, :], k == 0, k == DB - 1)
                PEs(mm(bank(4 + n % 2)[0:m, 0, :], sel27[0:27, f * P:f * P + m], cT[0:27, hf * HALF:hf * HALF + HALF]).then_inc(pe_done, 1), "F.gu", n)

            up(0)
            for n in range(NHALF * FB):
                hf, f = n // FB, n % FB
                m = min(P, FT - f * P)
                if n + 1 < NHALF * FB:
                    up(n + 1)
                pe.wait_ge(dve_done, at("dve", "F.act", n))
                if f == 0 and hf:
                    pe.wait_ge(dve_done, at("dve", "F.x", hf * 4 - 1))
                for tt in range(HALF // P):
                    last = mm(bank(6 + tt // 2)[:, 0, (tt % 2) * D:(tt % 2) * D + D], acf[0:m, n % 3, tt * P:tt * P + P], wd[0:m, f, :],
                              f == 0 and tt % 2 == 0, f == FB - 1, skip_group_check=True)
                PEs(last.then_inc(pe_done, 1), "F.down", n)
    return book


def kernel(**inputs):
    import ml_dtypes
    from concourse import bacc
    from concourse.bass_utils import run_bass_kernel_spmd

    f = {k: np.asarray(v) for k, v in inputs.items()}
    bf = ml_dtypes.bfloat16

    def turned(name):
        return np.ascontiguousarray(f[name].T)

    def by_row(name):
        return f[name].reshape(IB, P).T

    inv = (1.0 / 10000.0 ** (np.arange(0, ROT, 2, dtype=np.float32) / ROT)).astype(np.float32)
    ang = np.repeat(np.arange(S, dtype=np.float32)[:, None] * inv[None, :], 2, axis=1)
    cos, sin = np.cos(ang), np.sin(ang) * np.tile(np.array([-1.0, 1.0], np.float32), ROT // 2)
    rope = np.stack([cos, sin], 1).astype(np.float32).reshape(TPB, P, 1, 2, ROT)
    rope = np.concatenate([rope * np.float32(DH0 ** -0.5), rope], axis=2).transpose(1, 0, 2, 3, 4)
    r = np.arange(96)[:, None, None] % (2 * NST) == np.arange(2 * NST)[None, :, None]
    selbc = np.broadcast_to(r, (96, 2 * NST, P)).astype(bf)
    which = np.minimum(np.arange(FB * P) // F1, E1)
    sel27 = (np.arange(27)[:, None] % (E1 + 1) == which[None, :]).astype(bf)
    tri = (np.arange(P)[:, None] < np.arange(P)[None, :]).astype(bf)
    wd = np.concatenate([f["L1_ffn_Wd"].reshape(E1 * F1, D), f["L1_ffn_Sd"], np.zeros((FB * P - FT, D), np.float32)])

    def flat(e, shared):
        return np.concatenate([f[e].transpose(1, 0, 2).reshape(D, E1 * F1), f[shared]], axis=1)

    arrays = {
        "x": f["x"], "ctx": f["ctx_1024"], "mask": f["mask_BxS2_bf1"].view(np.uint8),
        "ident": np.eye(P, dtype=np.float32),
        "lnw": np.stack([f[n].reshape(DB, P).T for n in ("L0_attn_ln_w", "L0_attn_ln_b", "L0_ffn_norm_w", "L1_attn_norm_w")], 1),
        "wq0T": turned("L0_xattn_Wq"), "wk0T": turned("L0_xattn_Wk"),
        "bqk": np.stack([f["L0_xattn_bq"], f["L0_xattn_bk"]], 1),
        "w_in": f["L0_attn_W_in"], "w_out": f["L0_attn_W_out"], "rope": rope,
        "iota32": np.broadcast_to(np.arange(E0, dtype=np.float32), (P, E0)), "tri": tri,
        "tokid": np.arange(T, dtype=np.uint32).reshape(TILES, P).T, "norm_w": f["L0_ffn_norm_w"],
        "gate_wT": turned("L0_ffn_gate_w"), "sgate": f["L0_ffn_shared_gate_w"], "sup": f["L0_ffn_shared_up_w"],
        "sdown": f["L0_ffn_shared_down_w"], "w13": f["L0_ffn_w13"], "w2": f["L0_ffn_w2"],
        "in_projT": turned("L1_attn_in_proj_w"), "x_projT": turned("L1_attn_x_proj_w"), "out_projT": turned("L1_attn_out_proj_w"),
        "conv_w": f["L1_attn_conv_w"].reshape(DI, KC), "conv_b": by_row("L1_attn_conv_b"), "dt_w": by_row("L1_attn_dt_w"),
        "dt_b": by_row("L1_attn_dt_b"), "D_param": by_row("L1_attn_D_param"), "A_log": f["L1_attn_A_log"], "selbc": selbc,
        "wq1": f["L1_xattn_Wq"], "wk1": f["L1_xattn_Wk"], "wv1": f["L1_xattn_Wv"], "wo1": f["L1_xattn_Wo"],
        "wg": flat("L1_ffn_Wg", "L1_ffn_Sg"), "wu": flat("L1_ffn_Wu", "L1_ffn_Su"),
        "wd": wd.reshape(FB, P, D).transpose(1, 0, 2), "wr": np.concatenate([f["L1_ffn_Wr"], f["L1_ffn_Wsg"]], axis=1),
        "sel27": sel27,
    }
    arrays = {k: np.ascontiguousarray(v) for k, v in arrays.items()}

    def emitted(known):
        nc = bacc.Bacc("TRN2", target_bir_lowering=False, num_devices=1)
        ins = {k: nc.dram_tensor("in_" + k, v.shape, mybir.dt.from_np(v.dtype), kind="ExternalInput").ap() for k, v in arrays.items()}
        out = nc.dram_tensor("out", (B, S, D), F32, kind="ExternalOutput").ap()
        return nc, decoder(nc, ins, out, known)

    _, steps = emitted(None)
    nc, again = emitted(steps)
    assert again == steps
    res = run_bass_kernel_spmd(nc, [{"in_" + k: v for k, v in arrays.items()}], core_ids=[0])
    return res.results[0]["out"]
```

```python
from contextlib import ExitStack

import numpy as np

import concourse.bass as bass
from concourse import mybir

F32 = mybir.dt.float32
BF16 = mybir.dt.bfloat16
U32 = mybir.dt.uint32
U8 = mybir.dt.uint8
ALU = mybir.AluOpType
ACT = mybir.ActivationFunctionType
AX = mybir.AxisListType
EXP_LN = "natural_log_exp_and_others"

P = 128
B, S, D = 4, 256, 256
T = B * S
TILES = T // P
TPB = S // P
DB = D // P
C = 128
LN_EPS = 1e-5
H0, DH0 = 16, D // 16
E0, K0, I0 = 32, 4, 128
CAP = 2 * T * K0 // E0
ROT = DH0 // 2
DI, NST, KC = 512, 16, 4
IB = DI // P
HALF = 512
NHALF = T // HALF
BPH = HALF // S
H1, HKV = 16, 8
GR = H1 // HKV
E1, F1, FS = 8, 176, 704
FT = E1 * F1 + FS
FB = -(-FT // P)
NEG = -1e30


PIECES = 6
KA = PIECES * DH0
UPT0 = H0 // 2
UNITS0 = TILES * UPT0
LAST0 = UNITS0 + 5


def unit0(n):
    return n // UPT0 // TPB, n // UPT0 % TPB, n % UPT0


def side_work0():
    items = {}
    for b in range(B):
        prep = [("rows", b)]
        for tt in range(TPB):
            prep += [("qk", b, tt), ("v", b, tt)]
        prep += [("turn", b, tt, w, half) for tt in range(TPB) for w in (1, 0) for half in range(2)]
        for n, item in enumerate(prep):
            items.setdefault((b - 1) * TPB * UPT0 + 1 + n if b else -1, []).append(item)
    for t in range(TILES):
        items.setdefault(UPT0 * t + UPT0 + 3, []).append(("out", t // TPB, t % TPB))
    return items


def map_work():
    items = {}
    for i in range(2):
        items.setdefault(i, []).append(("context", i))
    for i in range(4):
        items.setdefault(2 + i, []).append(("qk", i))
    for t in range(TILES):
        for n, kind in enumerate(("energy", "scale", "turn")):
            items.setdefault(6 + 4 * t + n, []).append((kind, t))
    return items


UPB = HKV * TPB
UNITS = B * UPB
LAST_STEP = UNITS + 3 + TPB


def unit(n):
    return n // UPB, n // TPB % HKV, n % TPB


def side_work():
    items = {}

    def put(step, *item):
        items.setdefault(max(step, -1), []).append(item)

    for b in range(B):
        u0 = b * UPB
        first = u0 - UPB + 2 if b else -1
        put(first, "rows", b)
        for i in range(4):
            put(first + 1 + i if b else -1, "keys", b, i)
            put(first + 5 + i if b else -1, "values", b, i)
        for h in range(HKV):
            put(u0 + TPB * h - 3, "queries", b, h)
        for q in range(TPB):
            put(u0 + UPB + 3 + q, "output", b, q)
    return items


def head0(j, i):
    g, r = 2 * (j // 2) + i % 2, 2 * (j % 2) + i // 2
    return 4 * g + r


class Steps:

    def __init__(self, engine, book):
        self.engine, self.book, self.n = engine, book, 0

    def __call__(self, instruction, *step):
        self.n += 1
        if step:
            self.book[(self.engine, *step)] = self.n
        return instruction


def decoder(nc, ins, out, known):
    book = {}

    def at(*step):
        return known[step] if known is not None else 1

    ctx = ExitStack()
    with ctx:
        def sb(name, shape, dt=F32):
            return ctx.enter_context(nc.sbuf_tensor(name, shape, dt))

        def sem(name):
            return ctx.enter_context(nc.semaphore(name))

        X = sb("X", [P, TILES, D])
        XS = sb("XS", [P, 2 * TPB, D])
        XN = sb("XN", [P, TPB, D])
        stats = sb("stats", [P, TILES, 6])
        mv = sb("mv", [P, TILES, 2])
        lnv = sb("lnv", [P, 2, TILES])
        rstd = sb("rstd", [P, 2, TILES])
        ident = sb("ident", [P, P])
        lnw = sb("lnw", [P, 4, DB])
        ctxT = sb("ctxT", [P, T])
        iota_e = sb("iota_e", [P, E0])
        iota32 = iota_e[:, :]
        attT = sb("attT", [P, B, 2, S])

        def arena(name, size):
            whole = sb(name, [P, size])
            used = {}

            def phase(tag, after=None):
                used[tag] = used[after] if after else 0

                def take(shape, dt=F32):
                    n = int(np.prod(shape))
                    words = n if dt in (F32, U32) else -(-n // (2 if dt == BF16 else 4))
                    a = used[tag]
                    used[tag] += words
                    assert used[tag] <= size, (name, tag, used[tag])
                    v = whole[:, a:a + words]
                    if dt != F32:
                        v = v.bitcast(dt)
                    if len(shape) == 1:
                        return v
                    names = "abcd"[:len(shape)]
                    return v.rearrange(f"p ({' '.join(names)}) -> p {' '.join(names)}",
                                       **dict(zip(names, shape)))
                return take
            return phase

        ping, pong = arena("ping", 26000), arena("pong", 19900)

        take = ping("A")
        w_in, w_out = take([DB, 3 * D]), take([4, D])
        rope = take([TPB, 2, 2, ROT])
        xTa = take([2, DB, S])
        t1, t2 = take([2, H0, ROT]), take([2, H0, ROT])
        R = take([2, H0, DH0])
        stack = take([TPB, 2 * H0 * KA], BF16).rearrange("p t (w h d) -> p t w h d", w=2, h=H0)
        QT = take([2, 2 * H0 * S], BF16).rearrange("p b (w h s) -> p b w h s", w=2, h=H0)
        Va = take([2, TPB, H0 * 32]).rearrange("p b t (h d) -> p b t h d", h=H0)
        Pa = take([3, 2, S])
        PTa = take([2, 2, 2, P])
        mxa, rsa, ria = take([3, 2]), take([3, 2]), take([3, 2])
        CTa = take([4, P])
        identb = take([P], BF16)
        wq0, wk0, bqk = take([P]), take([P]), take([2])
        cx = take([TILES, C])
        q0, k0 = take([T]), take([T])
        en = take([S])
        m0, s0 = take([TILES]), take([TILES])
        xTb = take([2, DB, S])

        take = pong("C")
        nwb = take([D])
        gw = take([DB, E0])
        sgu, sdn = take([DB, 2 * I0]), take([D])
        NW = 6
        w13, w2 = take([NW, DB, 2 * I0]), take([NW, D])
        hT = take([DB, T])
        tokid = take([TILES], U32)
        tri, ones = take([P], BF16), take([P], BF16)
        top8, idx8 = take([TILES, 8]), take([TILES, 8], U32)
        negm, ex4, sm4 = take([TILES]), take([TILES, K0]), take([TILES])
        w4 = take([TILES, K0])
        idf = take([K0])
        oh, ohp = take([K0, E0]), take([K0, E0])
        sel_tile = take([TILES, E0], BF16)
        posk, over, base = take([K0]), take([K0]), take([K0])
        rowf, slotf = take([K0]), take([K0])
        row, slot = take([TILES, K0], U32), take([TILES, K0], U32)
        tab, tabf = take([P], U32), take([P])
        slot_tok = take([2 * E0], U32)
        G = take([4, 2, D])
        XTc = take([2, DB, CAP])
        sg, ac = take([2, CAP]), take([2, CAP])
        EO = take([2, 2, D])
        Y = take([2, K0, D])
        sgs, acs = take([HALF]), take([HALF])
        zero1 = take([64], U32)

        take = ping("D")
        wip, wxp, wop = take([DB, 2 * DI]), take([IB, 33]), take([IB, D])
        cw, cb, dtw, dtb, dpar, alog, Aneg = (take([IB, KC]), take([IB]), take([IB]), take([IB]), take([IB]),
                                              take([IB, NST]), take([IB, NST]))
        selbc = take([2 * NST * P], BF16).rearrange("p (n m) -> p n m", m=P)
        xTd = take([DB, HALF])
        xi_words = take([IB * BPH * (S + KC - 1)])
        xi = xi_words.rearrange("p (m b s) -> p m b s", m=IB, b=BPH)
        dtu = xi_words[:, 0:IB * HALF].rearrange("p (m n) -> p m n", m=IB)
        u, sz, dt = take([IB, HALF]), take([IB, HALF]), take([IB, HALF])
        xs3f, xs3, xs3m = take([HALF]), take([HALF], BF16), take([HALF], BF16)
        wdt = take([IB, P])
        NB = 2
        Bb = take([NB, HALF])
        dA = take([2, IB, HALF])
        NHB = 4
        hb_ = take([2, IB, HALF])
        e1 = dA[:, 1]
        a1 = dA[:, 0]

        take = pong("E")
        wq1, wk1, wv1, wo1 = take([DB, H1 * P]), take([HKV * P]), take([HKV * P]), take([H1, D])
        mrow, mrowb, one1 = take([B, S], U8), take([B * S], BF16), take([P], BF16)
        vfl, mflag = take([B, S], U8), take([B])
        far = pong("D", after="E")
        hb_far = far([2, IB, HALF])
        xTe = take([2, DB, S])
        QE = take([3, GR, S])
        Pe = take([3, GR, S])
        mxe, rse, rie = take([3, GR]), take([3, GR]), take([3, GR])
        V1 = take([2, 2, HKV * P])

        def hbuf(s):
            return (hb_ if s % NHB < 2 else hb_far)[:, s % 2]

        take = ping("F")
        wg, wu, wd = take([DB, FT]), take([DB, FT]), take([FB, D])
        wr = take([DB, E1 + 1])
        sel27 = take([FB * P], BF16)
        kT = take([2, HKV, S])
        PTe = take([2, GR, 2, P])
        OT = take([TPB, H1, P])
        take = pong("F")
        xTf = take([NHALF, DB, HALF])
        lg, pr, sp1, rp = take([TILES, E1 + 1]), take([TILES, E1]), take([TILES]), take([TILES])
        np8, tp8, ti8, tif = take([TILES]), take([TILES, 8]), take([TILES, 8], U32), take([TILES, 2])
        cc, c2 = take([TILES, E1 + 1]), take([TILES, E1])
        chb, cmb = take([E1 + 1 + 1], BF16), take([E1 + 1 + 1], BF16)
        c27 = take([TILES, 27])
        r1c = take([E1 + 1])
        cT = take([T], BF16)
        iota8 = iota_e[:, 0:E1]
        sgf, tf, acf = take([2, HALF]), take([2, HALF]), take([3, HALF])

        PS = ctx.enter_context(nc.psum_tensor("PS", [P, 8, 512], F32))

        def bank(i, n=1):
            return PS[:, i:i + n, :]

        h_dram = nc.dram_tensor("h_dram", (T, D), F32, kind="Internal").ap()
        eo_dram = nc.dram_tensor("eo_dram", (E0 * CAP, D), F32, kind="Internal").ap()
        slots_dram = nc.dram_tensor("slots_dram", (E0 * CAP, 1), U32, kind="Internal").ap()

        pe_done, act_done = sem("pe_done"), sem("act_done")
        dve_done, pool_done = sem("dve_done"), sem("pool_done")
        PEs, ACs, VEs, POs = Steps("pe", book), Steps("act", book), Steps("dve", book), Steps("pool", book)
        x_in, ctx_in, attn_w_in, xattn_w_in = sem("x_in"), sem("ctx_in"), sem("attn_w_in"), sem("xattn_w_in")
        moe_w_in, const_in, mamba_w_in, xattn1_w_in = sem("moe_w_in"), sem("const_in"), sem("mamba_w_in"), sem("xattn1_w_in")
        ffn1_w_in = sem("ffn1_w_in")
        expert_in = [sem(f"expert_in{i}") for i in range(NW)]
        h_stored = [sem(f"h_stored{i}") for i in range(2 * TPB)]
        table_clear, scattered, table_in = sem("table_clear"), sem("scattered"), sem("table_in")
        gathered = [sem(f"gathered{i}") for i in range(4)]
        eo_stored = [sem(f"eo_stored{i}") for i in range(2)]
        y_in = [sem(f"y_in{i}") for i in range(2)]
        out_stored = sem("out_stored")

        N_X, N_CONST, N_ATTN, N_XATTN, N_MOE, N_MAMBA, N_XATTN1, N_FFN1 = 4, 7, 2, 3, 4, 10, 6, 5

        block = ctx.enter_context(nc.Block())

        @block.sync
        def _(sp):
            xv = ins["x"].rearrange("b (t p) d -> p (b t) d", p=P)
            for b in range(B):
                sp.dma_start(X[:, TPB * b:TPB * b + TPB, :], xv[:, TPB * b:TPB * b + TPB, :]).then_inc(x_in, 16)
            sp.dma_start(cx, ins["ctx"].rearrange("b (t p) d -> p (b t) d", p=P)).then_inc(ctx_in, 16)
            sp.dma_start(ident[:, :], ins["ident"]).then_inc(const_in, 16)
            sp.dma_start(lnw[:, :, :], ins["lnw"]).then_inc(const_in, 16)
            sp.dma_start(wq0, ins["wq0T"]).then_inc(xattn_w_in, 16)
            sp.dma_start(wk0, ins["wk0T"]).then_inc(xattn_w_in, 16)
            sp.dma_start(bqk, ins["bqk"]).then_inc(xattn_w_in, 16)
            sp.dma_start(w_in, ins["w_in"].rearrange("(k p) n -> p k n", p=P)).then_inc(attn_w_in, 16)
            sp.dma_start(w_out, ins["w_out"]).then_inc(attn_w_in, 16)
            sp.dma_start(rope, ins["rope"]).then_inc(const_in, 16)
            sp.dma_start(iota32, ins["iota32"]).then_inc(const_in, 16)
            sp.dma_start(tri, ins["tri"]).then_inc(const_in, 16)
            sp.dma_start(tokid, ins["tokid"]).then_inc(const_in, 16)
            sp.dma_start(nwb, ins["norm_w"].partition_broadcast(P)).then_inc(const_in, 16)
            sp.dma_start(gw, ins["gate_wT"].rearrange("(k p) n -> p k n", p=P)).then_inc(moe_w_in, 16)
            sp.dma_start(sgu[:, :, 0:I0], ins["sgate"].rearrange("(k p) n -> p k n", p=P)).then_inc(moe_w_in, 16)
            sp.dma_start(sgu[:, :, I0:2 * I0], ins["sup"].rearrange("(k p) n -> p k n", p=P)).then_inc(moe_w_in, 16)
            sp.dma_start(sdn, ins["sdown"]).then_inc(moe_w_in, 16)
            sp.wait_ge(pool_done, at("pool", "zeros"))
            sp.dma_start(slots_dram.rearrange("(p n) o -> p (n o)", p=P), zero1).then_inc(table_clear, 16)

            def load_expert(e):
                sp.dma_start(w13[:, e % NW], ins["w13"][e].rearrange("(k p) n -> p k n", p=P)).then_inc(expert_in[e % NW], 16)
                sp.dma_start(w2[:, e % NW], ins["w2"][e]).then_inc(expert_in[e % NW], 16)

            for e in range(NW):
                load_expert(e)
            for t in range(TILES):
                sp.wait_ge(dve_done, at("dve", "C.h", t))
                sp.dma_start(h_dram[t * P:(t + 1) * P, :], XS[:, t % (2 * TPB), :]).then_inc(h_stored[t % 4], 16)
            sp.wait_ge(pe_done, at("pe", "B.end"))
            sp.wait_ge(act_done, at("act", "B.end"))
            sp.wait_ge(dve_done, at("dve", "B.end"))
            sp.dma_start(wip, ins["in_projT"].rearrange("(k p) n -> p k n", p=P)).then_inc(mamba_w_in, 16)
            for dst, name in ((wxp, "x_projT"), (wop, "out_projT"), (cw, "conv_w"), (cb, "conv_b"), (dtw, "dt_w"),
                              (dtb, "dt_b"), (dpar, "D_param"), (alog, "A_log")):
                src = ins[name]
                if src.shape[0] == DI:
                    src = src.rearrange("(k p) n -> p k n", p=P)
                sp.dma_start(dst, src).then_inc(mamba_w_in, 16)
            sp.dma_start(selbc[0:96], ins["selbc"]).then_inc(mamba_w_in, 16)
            sp.wait_ge(scattered, 16 * TILES * K0)
            sp.dma_start(tab[0:2 * E0, :], slots_dram.rearrange("(j p) o -> j (p o)", p=P)).then_inc(table_in, 16)
            for e in range(E0):
                sp.wait_ge(act_done, at("act", "C.eo", e))
                sp.dma_start(eo_dram[e * CAP:(e + 1) * CAP, :].rearrange("(s p) d -> p s d", p=P),
                             EO[:, e % 2]).then_inc(eo_stored[e % 2], 16)
                if e + NW < E0:
                    sp.wait_ge(pe_done, at("pe", "C.down", e))
                    load_expert(e + NW)
            sp.wait_ge(dve_done, at("dve", "C.end"))
            for i in range(2):
                sp.wait_ge(eo_stored[i], 16 * E0 // 2)
            sp.dma_start(wq1, ins["wq1"].rearrange("(k p) n -> p k n", p=P)).then_inc(xattn1_w_in, 16)
            sp.dma_start(wk1, ins["wk1"]).then_inc(xattn1_w_in, 16)
            sp.dma_start(wv1, ins["wv1"]).then_inc(xattn1_w_in, 16)
            sp.dma_start(wo1, ins["wo1"].rearrange("(h p) n -> p h n", p=P)).then_inc(xattn1_w_in, 16)
            sp.dma_start(mrow[0:1], ins["mask"].rearrange("(o b) s -> o b s", o=1)).then_inc(xattn1_w_in, 16)
            sp.dma_start(vfl, ins["mask"].partition_broadcast(P)).then_inc(xattn1_w_in, 16)
            sp.wait_ge(pe_done, at("pe", "D.end"))
            sp.wait_ge(act_done, at("act", "D.end"))
            sp.wait_ge(dve_done, at("dve", "D.end"))
            sp.wait_ge(pool_done, at("pool", "D.end"))
            sp.dma_start(wg, ins["wg"].rearrange("(k p) n -> p k n", p=P)).then_inc(ffn1_w_in, 16)
            sp.dma_start(wu, ins["wu"].rearrange("(k p) n -> p k n", p=P)).then_inc(ffn1_w_in, 16)
            sp.dma_start(wd, ins["wd"]).then_inc(ffn1_w_in, 16)
            sp.dma_start(wr, ins["wr"].rearrange("(k p) n -> p k n", p=P)).then_inc(ffn1_w_in, 16)
            sp.dma_start(sel27[0:27], ins["sel27"]).then_inc(ffn1_w_in, 16)
            ov = out.rearrange("b (t p) d -> p (b t) d", p=P)
            for t in range(0, TILES, 4):
                sp.wait_ge(dve_done, at("dve", "F.x", t + 3))
                sp.dma_start(ov[:, t:t + 4, :], X[:, t:t + 4, :]).then_inc(out_stored, 16)
            sp.wait_ge(out_stored, 16 * 2)

        @block.gpsimd
        def _(pool):
            POs(nc.gpsimd.memset(zero1, 0).then_inc(pool_done, 1), "zeros")
            POs(nc.gpsimd.memset(Va, 0.0).then_inc(pool_done, 1), "A.V")
            POs(nc.gpsimd.memset(ones, 1.0).then_inc(pool_done, 1), "ones")

            for b in range(B):
                for tt in range(TPB):
                    pool.wait_ge(dve_done, at("dve", "A.pieces", b, tt))
                    st = stack[:, tt]
                    for w, to, frm, n in ((0, 3, 0, 2), (0, 5, 0, 1), (1, 4, 0, 2), (1, 2, 0, 1)):
                        POs(nc.gpsimd.tensor_copy(st[:, w, :, to * DH0:(to + n) * DH0], st[:, w, :, frm * DH0:(frm + n) * DH0])
                            .then_inc(pool_done, 1), "A.stack", b, tt)

            pool.wait_ge(table_clear, 16)
            pool.wait_ge(const_in, 16 * N_CONST)
            for t in range(TILES):
                pool.wait_ge(dve_done, at("dve", "C.slot", t))
                for k in range(K0):
                    nc.gpsimd.indirect_dma_start(
                        out=slots_dram, out_offset=bass.IndirectOffsetOnAxis(ap=slot[:, t, k:k + 1], axis=0),
                        in_=tokid[:, t:t + 1], in_offset=None,
                        bounds_check=E0 * CAP - 1, oob_is_err=False).then_inc(scattered, 16)
            for i in range(4):
                pool.wait_ge(h_stored[i], 16 * TILES // 4)
            pool.wait_ge(dve_done, at("dve", "C.slot_tok"))
            for j in range(2 * E0):
                if j >= 8:
                    pool.wait_ge(pe_done, at("pe", "C.xT", j // 2 - 4))
                nc.gpsimd.indirect_dma_start(
                    out=G[:, (j // 2) % 4, j % 2, :], out_offset=None, in_=h_dram,
                    in_offset=bass.IndirectOffsetOnAxis(ap=slot_tok[:, j:j + 1], axis=0),
                    bounds_check=T - 1, oob_is_err=False).then_inc(gathered[(j // 2) % 4], 16)
            for i in range(2):
                pool.wait_ge(eo_stored[i], 16 * E0 // 2)
            for t in range(TILES):
                if t >= 2:
                    pool.wait_ge(dve_done, at("dve", "C.comb", t - 2))
                for k in range(K0):
                    nc.gpsimd.indirect_dma_start(
                        out=Y[:, t % 2, k, :], out_offset=None, in_=eo_dram,
                        in_offset=bass.IndirectOffsetOnAxis(ap=row[:, t, k:k + 1], axis=0),
                        bounds_check=E0 * CAP - 1, oob_is_err=False).then_inc(y_in[t % 2], 16)

            pool.wait_ge(pe_done, at("pe", "B.end"))
            pool.wait_ge(dve_done, at("dve", "B.end"))
            pool.wait_ge(act_done, at("act", "B.end"))
            for hf in range(NHALF):
                if hf:
                    pool.wait_ge(pool_done, POs.n)
                POs(nc.gpsimd.memset(xi[:, :, :, 0:KC - 1], 0.0).then_inc(pool_done, 1), "D.pad", hf)
                pool.wait_ge(dve_done, at("dve", "D.dtu", hf))
                for r in range(2):
                    POs(nc.gpsimd.memset(dA[:, r, :, 0:HALF:S], 0.0).then_inc(pool_done, 1), "D.zero", hf, r)
                for n in range(NST):
                    s = hf * NST + n
                    pool.wait_ge(act_done, at("act", "D.Bb", s))
                    if s >= NHB:
                        pool.wait_ge(pe_done, at("pe", "D.sum", s - NHB))
                    bn = Bb[:, s % NB, :]
                    POs(nc.gpsimd.tensor_tensor(
                        hbuf(s), dtu, bn.rearrange("p (o n) -> p o n", o=1).broadcast_to((P, IB, HALF)),
                        ALU.mult).then_inc(pool_done, 1), "D.Bu", s)
            book[("pool", "D.end")] = POs.n

        @block.scalar
        def _(act):
            a = nc.scalar

            def ln(name, b, second):
                act.wait_ge(dve_done, at("dve", name + ".mv", b))
                t0 = TPB * b
                var = mv[:, t0:t0 + TPB, 1]
                ACs(a.activation(lnv[:, 0, t0:t0 + TPB], var, ACT.Ln, bias=LN_EPS).then_inc(act_done, 1))
                if second:
                    ACs(a.activation(lnv[:, 1, t0:t0 + TPB], var, ACT.Ln, bias=LN_EPS * second, scale=1.0 + second).then_inc(act_done, 1))
                act.wait_ge(act_done, ACs.n)
                k = 2 if second else 1
                ACs(a.activation(rstd[:, 0:k, t0:t0 + TPB], lnv[:, 0:k, t0:t0 + TPB], ACT.Exp, scale=-0.5).then_inc(act_done, 1),
                    name + ".rstd", b)

            a.preload_act_table_set(EXP_LN)
            side, maps = side_work0(), map_work()
            for b in range(B):
                ln("A", b, LN_EPS)
            act.wait_ge(const_in, 16 * N_CONST)
            act.wait_ge(xattn_w_in, 16 * N_XATTN)
            for i in range(-1, LAST0 + 1):
                if 0 <= i < UNITS0:
                    act.wait_ge(dve_done, at("dve", "A.max", i))
                    if i >= 3:
                        act.wait_ge(pe_done, at("pe", "A.PT", i - 3))
                    for j in range(2):
                        ACs(a.activation(Pa[:, i % 3, j, :], bank(i % 3)[:, 0, j * S:j * S + S], ACT.Exp, bias=mxa[:, i % 3, j:j + 1],
                                         accum_out=rsa[:, i % 3, j:j + 1]).then_inc(act_done, 1), "A.P", i)
                n = i - 2
                if 0 <= n < UNITS0:
                    act.wait_ge(pe_done, at("pe", "A.PT", n))
                    if n >= 2:
                        act.wait_ge(pe_done, at("pe", "A.av", n - 2))
                    ACs(a.activation(PTa[:, n % 2], bank(3 + n % 2)[:, 0, :].rearrange("p (i k q) -> p i k q", i=2, k=2), ACT.Copy)
                        .then_inc(act_done, 1), "A.PT", n)
                n = i - 3
                if 0 <= n < UNITS0 and n % UPT0 == UPT0 - 1:
                    t = n // UPT0
                    act.wait_ge(pe_done, at("pe", "A.av", n))
                    if t:
                        act.wait_ge(pe_done, at("pe", "A.out", (t - 1) // TPB, (t - 1) % TPB))
                    ACs(a.activation(CTa, bank(5)[:, 0, :].rearrange("p (g q) -> p g q", g=4), ACT.Copy).then_inc(act_done, 1), "A.cT", t)
                for kind, b, *w in side.get(i, []):
                    if kind == "rows":
                        act.wait_ge(pe_done, at("pe", "A.rows", b))
                        if b >= 2:
                            act.wait_ge(pe_done, at("pe", "A.v", b - 2, TPB - 1))
                        for k in range(DB):
                            ACs(a.activation(xTa[:, b % 2, k, :], bank(7)[:, 0, k * S:k * S + S], ACT.Identity, scale=lnw[:, 0, k:k + 1],
                                             bias=lnw[:, 1, k:k + 1]).then_inc(act_done, 1), "A.rows", b)
                    elif kind == "v":
                        act.wait_ge(pe_done, at("pe", "A.v", b, w[0]))
                        act.wait_ge(pool_done, at("pool", "A.V"))
                        if b >= 2 and w[0] == 0:
                            act.wait_ge(pe_done, at("pe", "A.av", (b - 1) * TPB * UPT0 - 1))
                        ACs(a.activation(Va[:, b % 2, w[0], :, 0:DH0], bank(7)[:, 0, 0:D].rearrange("p (h d) -> p h d", h=H0), ACT.Copy)
                            .then_inc(act_done, 1), "A.v", b, w[0])
                    elif kind == "turn":
                        tt, qk, half = w
                        act.wait_ge(pe_done, at("pe", "A.turn", b, *w))
                        if b >= 2 and (tt, qk, half) == (0, 1, 0):
                            act.wait_ge(pe_done, at("pe", "A.S", (b - 1) * TPB * UPT0 - 1))
                        ACs(a.activation(QT[0:KA, b % 2, qk, 8 * half:8 * half + 8, tt * P:tt * P + P],
                                         bank(7)[0:KA, 0, :].bitcast(BF16).rearrange("p (h s) -> p h s", h=8), ACT.Copy)
                            .then_inc(act_done, 1), "A.turn", b, *w)
                for kind, t in maps.get(i, []):
                    if kind == "context":
                        act.wait_ge(pe_done, at("pe", "context", t))
                        ACs(a.activation(ctxT[:, 512 * t:512 * t + 512], bank(6)[:, 0, :], ACT.Copy).then_inc(act_done, 1), "context", t)
                    elif kind == "qk":
                        act.wait_ge(pe_done, at("pe", "map.qk", t))
                        ACs(a.activation((q0, k0)[t // 2][:, 512 * (t % 2):512 * (t % 2) + 512], bank(6)[:, 0, :], ACT.Identity,
                                         bias=bqk[:, t // 2:t // 2 + 1]).then_inc(act_done, 1), "map.qk", t)
                    elif kind == "energy":
                        act.wait_ge(dve_done, at("dve", "m0", t))
                        if t:
                            act.wait_ge(pe_done, at("pe", "map", t - 1))
                        ACs(a.activation(en, bank(6)[:, 0, 0:S], ACT.Exp, bias=m0[:, t:t + 1], accum_out=s0[:, t:t + 1])
                            .then_inc(act_done, 1), "en", t)
                    elif kind == "turn":
                        act.wait_ge(pe_done, at("pe", "map", t))
                        ACs(a.activation(attT[:, t // 2, :, (t % 2) * P:(t % 2) * P + P],
                                         bank(6)[:, 0, 0:2 * P].rearrange("p (m n) -> p m n", m=2), ACT.Copy).then_inc(act_done, 1), "map", t)

            for b in range(B):
                ln("B", b, None)
                act.wait_ge(pe_done, at("pe", "B.xT", b))
                if b >= 2:
                    act.wait_ge(pe_done, at("pe", "B.out", b - 2))
                ACs(a.activation(xTb[:, b % 2], bank(b % 2)[:, 0, :].rearrange("p (k n) -> p k n", k=DB), ACT.Copy).then_inc(act_done, 1), "B.xT", b)
            book[("act", "B.end")] = ACs.n

            for b in range(B):
                ln("C", b, 1e-6)
            for t in range(TILES):
                act.wait_ge(pe_done, at("pe", "C.hT", t))
                ACs(a.activation(hT[:, :, t * P:t * P + P], bank(t % 2)[:, 0, 0:2 * P].rearrange("p (k n) -> p k n", k=DB),
                                 ACT.Copy).then_inc(act_done, 1), "C.hT", t)
                act.wait_ge(dve_done, at("dve", "C.top", t))
                ACs(a.activation(ex4[:, t, :], top8[:, t, 0:K0], ACT.Exp, bias=negm[:, t:t + 1],
                                 accum_out=sm4[:, t:t + 1]).then_inc(act_done, 1), "C.ex4", t)
            for hf in range(NHALF):
                act.wait_ge(pe_done, at("pe", "C.sgu", hf))
                if hf:
                    act.wait_ge(dve_done, at("dve", "C.sact", hf - 1))
                ACs(a.activation(sgs, bank(4)[:, 0, :], ACT.Silu).then_inc(act_done, 1), "C.sgs", hf)
            for e in range(E0):
                act.wait_ge(pe_done, at("pe", "C.gu", e))
                if e >= 2:
                    act.wait_ge(dve_done, at("dve", "C.act", e - 2))
                ACs(a.activation(sg[:, e % 2, :], bank(2 + e % 2)[:, 0, 0:CAP], ACT.Silu).then_inc(act_done, 1), "C.sg", e)
                act.wait_ge(pe_done, at("pe", "C.down", e))
                if e >= 2:
                    act.wait_ge(eo_stored[e % 2], 16 * (e // 2))
                ACs(a.activation(EO[:, e % 2], bank(4 + e % 2)[:, 0, :].rearrange("p (s d) -> p s d", s=2), ACT.Copy).then_inc(act_done, 1), "C.eo", e)

            a.preload_act_table_set(EXP_LN)
            act.wait_ge(mamba_w_in, 16 * N_MAMBA)
            ACs(a.activation(Aneg, alog, ACT.Exp).then_inc(act_done, 1), "D.A")
            for b in range(B):
                ln("D", b, LN_EPS)
            for hf in range(NHALF):
                act.wait_ge(pe_done, at("pe", "D.xT", hf))
                if hf:
                    act.wait_ge(pe_done, at("pe", "D.z", hf - 1, IB - 1))
                for k in range(DB):
                    ACs(a.activation(xTd[:, k, :], bank(6 + k)[:, 0, :], ACT.Copy, scale=lnw[:, 3, k:k + 1]).then_inc(act_done, 1), "D.xT", hf)
                for m in range(IB):
                    act.wait_ge(pe_done, at("pe", "D.xi", hf, m))
                    act.wait_ge(pool_done, at("pool", "D.pad", hf))
                    if hf:
                        act.wait_ge(dve_done, at("dve", "D.conv", hf - 1, m))
                    ACs(a.activation(xi[:, m, :, KC - 1:], bank(m)[:, 0, :].rearrange("p (b s) -> p b s", b=BPH), ACT.Copy).then_inc(act_done, 1), "D.xi", hf, m)
                for m in range(IB):
                    act.wait_ge(pe_done, at("pe", "D.z", hf, m))
                    if hf and m == 0:
                        act.wait_ge(dve_done, at("dve", "D.yz", hf - 1, IB - 1))
                    ACs(a.activation(sz[:, m, :], bank(4 + m % 2)[:, 0, :], ACT.Silu).then_inc(act_done, 1), "D.sz", hf, m)
                for m in range(IB):
                    act.wait_ge(dve_done, at("dve", "D.conv", hf, m))
                    ACs(a.activation(u[:, m, :], u[:, m, :], ACT.Silu).then_inc(act_done, 1), "D.u", hf, m)
                a.preload_act_table_set(EXP_LN)
                for m in range(IB):
                    act.wait_ge(dve_done, at("dve", "D.v", hf, m))
                    ACs(a.activation(a1[:, m, :], dt[:, m, :], ACT.Abs).then_inc(act_done, 1))
                act.wait_ge(act_done, ACs.n)
                ACs(a.activation(e1, a1, ACT.Exp, scale=-1.0).then_inc(act_done, 1))
                act.wait_ge(act_done, ACs.n)
                ACs(a.activation(e1, e1, ACT.Ln, bias=1.0).then_inc(act_done, 1), "D.sp", hf)
                for n in range(NST):
                    s = hf * NST + n
                    act.wait_ge(pe_done, at("pe", "D.B", s))
                    if s >= NB:
                        act.wait_ge(pool_done, at("pool", "D.Bu", s - NB))
                    ACs(a.activation(Bb[:, s % NB, :], bank(6)[:, 0, :], ACT.Copy).then_inc(act_done, 1), "D.Bb", s)
                    act.wait_ge(dve_done, at("dve", "D.dtu", hf) if n < 2 else at("dve", "D.scan", s - 2))
                    for m in range(IB):
                        step = dA[:, s % 2, m, :].rearrange("p (b s) -> p b s", b=BPH)[:, :, 1:]
                        ACs(a.activation(step, dt[:, m, :].rearrange("p (b s) -> p b s", b=BPH)[:, :, 1:], ACT.Exp,
                                         scale=Aneg[:, m, n:n + 1]).then_inc(act_done, 1), "D.dA", s)
            book[("act", "D.end")] = ACs.n

            side = side_work()
            for b in range(B):
                ln("E", b, None)
            for i in range(-1, LAST_STEP + 1):
                if 0 <= i < UNITS:
                    act.wait_ge(dve_done, at("dve", "E.max", i))
                    if i >= 3:
                        act.wait_ge(pe_done, at("pe", "E.PT", i - 3))
                    for j in range(GR):
                        ACs(a.activation(Pe[:, i % 3, j, :], bank(i % 3)[:, 0, j * S:j * S + S], ACT.Exp, bias=mxe[:, i % 3, j:j + 1],
                                         accum_out=rse[:, i % 3, j:j + 1]).then_inc(act_done, 1), "E.P", i)
                n = i - 3
                if 0 <= n < UNITS and n % 2 == 1:
                    b, h, _ = unit(n)
                    act.wait_ge(pe_done, at("pe", "E.av", n))
                    if b and h == 0:
                        act.wait_ge(pe_done, at("pe", "E.output", b - 1, TPB - 1))
                    ACs(a.activation(OT[:, :, GR * h:GR * h + GR, :], bank(5 + n // 2 % 2)[:, 0, :].rearrange("p (t g q) -> p t g q", t=TPB, g=GR),
                                     ACT.Copy).then_inc(act_done, 1), "E.OT", n // 2)
                for kind, b, *w in side.get(i, []):
                    if kind == "rows":
                        act.wait_ge(pe_done, at("pe", "E.rows", b))
                        if b >= 2:
                            act.wait_ge(pe_done, at("pe", "E.queries", b - 2, HKV - 1))
                        ACs(a.activation(xTe[:, b % 2], bank(7)[:, 0, :].rearrange("p (k n) -> p k n", k=DB), ACT.Copy).then_inc(act_done, 1),
                            "E.rows", b)
                    elif kind == "keys":
                        act.wait_ge(pe_done, at("pe", "E.keys", b, w[0]))
                        if b >= 2 and w[0] == 0:
                            act.wait_ge(pe_done, at("pe", "E.S", (b - 1) * UPB - 1))
                        ACs(a.activation(kT[:, b % 2, 2 * w[0]:2 * w[0] + 2, :], bank(7)[:, 0, :].rearrange("p (h s) -> p h s", h=2),
                                         ACT.Copy).then_inc(act_done, 1), "E.keys", b, w[0])
                    elif kind == "queries":
                        act.wait_ge(pe_done, at("pe", "E.queries", b, w[0]))
                        c = b * HKV + w[0]
                        if c >= 3:
                            act.wait_ge(pe_done, at("pe", "E.S", (c - 2) * TPB - 1))
                        ACs(a.activation(QE[:, c % 3], bank(7)[:, 0, :].rearrange("p (h s) -> p h s", h=GR), ACT.Copy,
                                         scale=float(P) ** -0.5).then_inc(act_done, 1), "E.queries", b, w[0])

            for b in range(B):
                ln("F", b, None)
            for b in range(B):
                act.wait_ge(pe_done, at("pe", "F.xT", b))
                ACs(a.activation(xTf[:, b // BPH, :, (b % BPH) * S:(b % BPH) * S + S],
                                 bank(b % 2)[:, 0, :].rearrange("p (k n) -> p k n", k=DB), ACT.Copy).then_inc(act_done, 1), "F.xT", b)
            for t in range(TILES):
                act.wait_ge(dve_done, at("dve", "F.max", t))
                ACs(a.activation(pr[:, t, :], lg[:, t, 0:E1], ACT.Exp, bias=np8[:, t:t + 1], accum_out=sp1[:, t:t + 1]).then_inc(act_done, 1))
                ACs(a.activation(lg[:, t, E1:], lg[:, t, E1:], ACT.Exp, scale=-1.0).then_inc(act_done, 1), "F.pr", t)
                act.wait_ge(pe_done, at("pe", "F.cT", t))
                ACs(a.activation(cT[0:27, t * P:t * P + P], bank(4 + t % 2)[0:27, 0, 0:P], ACT.Copy).then_inc(act_done, 1), "F.cT", t)
            for hf in range(NHALF):
                for f in range(FB):
                    n = hf * FB + f
                    act.wait_ge(pe_done, at("pe", "F.gu", n))
                    if n >= 2:
                        act.wait_ge(dve_done, at("dve", "F.act", n - 2))
                    m = min(P, FT - f * P)
                    ACs(a.activation(sgf[0:m, n % 2, :], bank(n % 2)[0:m, 0, :], ACT.Silu).then_inc(act_done, 1), "F.sg", n)

        @block.vector
        def _(dve):
            v = nc.vector

            def ln(name, b, second, residual):
                t0 = TPB * b
                for t in range(t0, t0 + TPB):
                    VEs(v.bn_stats(stats[:, t, :], X[:, t, :]).then_inc(dve_done, 1))
                dve.wait_ge(dve_done, VEs.n)
                for t in range(t0, t0 + TPB):
                    VEs(v.bn_aggr(mv[:, t, :], stats[:, t, :]).then_inc(dve_done, 1), name + ".mv", b)

            def ln_apply(name, b, second, residual, free):
                t0 = TPB * b
                dve.wait_ge(act_done, at("act", name + ".rstd", b))
                dve.wait_ge(dve_done, VEs.n)
                free()
                for t in range(t0, t0 + TPB):
                    VEs(v.tensor_scalar(XS[:, t % 4, :], X[:, t, :], mv[:, t, 0:1], rstd[:, 1 if second else 0, t:t + 1],
                                        ALU.subtract, ALU.mult).then_inc(dve_done, 1), name + ".xs", b)
                if residual:
                    for t in range(t0, t0 + TPB):
                        VEs(v.tensor_scalar(XN[:, t % TPB, :], X[:, t, :], mv[:, t, 0:1], rstd[:, 0, t:t + 1],
                                            ALU.subtract, ALU.mult).then_inc(dve_done, 1))
                    dve.wait_ge(dve_done, VEs.n)
                    for t in range(t0, t0 + TPB):
                        VEs(v.tensor_tensor(X[:, t, :], X[:, t, :], XN[:, t % TPB, :], ALU.add).then_inc(dve_done, 1), name + ".res", b)

            def add_to_x(t, psum, *step):
                VEs(v.tensor_tensor(X[:, t, :], X[:, t, :], psum, ALU.add).then_inc(dve_done, 1), *step)

            side, maps = side_work0(), map_work()
            dve.wait_ge(x_in, 16 * N_X)
            for b in range(B):
                ln("A", b, True, True)
            dve.wait_ge(const_in, 16 * N_CONST)
            VEs(v.tensor_copy(identb, ident[:, :]).then_inc(dve_done, 1), "identb")

            def rows0(b):
                def free():
                    if b >= 2:
                        dve.wait_ge(pe_done, at("pe", "A.rows", b - 2))
                ln_apply("A", b, True, True, free)

            def pieces(b, tt):
                dve.wait_ge(pe_done, at("pe", "A.qk", b, tt))
                dve.wait_ge(dve_done, VEs.n)
                qk = bank(7)[:, 0, :].rearrange("p (w h d) -> p w h d", w=2, h=H0)

                def table(i, a0, n):
                    return rope[:, tt, :, i, a0:ROT:ROT // n].rearrange("p w (o d) -> p w o d", o=1).broadcast_to((P, 2, H0, n))
                VEs(v.tensor_tensor(t1, qk[:, :, :, 0:ROT], table(0, 0, ROT), ALU.mult).then_inc(dve_done, 1))
                VEs(v.tensor_tensor(t2[:, :, :, 0:ROT:2], qk[:, :, :, 1:ROT:2], table(1, 0, ROT // 2), ALU.mult).then_inc(dve_done, 1))
                VEs(v.tensor_tensor(t2[:, :, :, 1:ROT:2], qk[:, :, :, 0:ROT:2], table(1, 1, ROT // 2), ALU.mult).then_inc(dve_done, 1))
                VEs(v.tensor_scalar(R[:, 0, :, ROT:], qk[:, 0, :, ROT:], DH0 ** -0.5, None, ALU.mult).then_inc(dve_done, 1))
                VEs(v.tensor_copy(R[:, 1, :, ROT:], qk[:, 1, :, ROT:]).then_inc(dve_done, 1), "A.qk", b, tt)
                dve.wait_ge(dve_done, VEs.n)
                VEs(v.tensor_tensor(R[:, :, :, 0:ROT], t1, t2, ALU.add).then_inc(dve_done, 1))
                st = stack[:, tt]
                if b:
                    dve.wait_ge(pe_done, at("pe", "A.turn", b - 1, tt, 0, 1))
                    dve.wait_ge(pool_done, at("pool", "A.stack", b - 1, tt))
                dve.wait_ge(dve_done, VEs.n)
                for p in range(2):
                    piece = st[:, :, :, p * DH0:(p + 1) * DH0]
                    VEs(v.tensor_copy(piece, R).then_inc(dve_done, 1))
                    dve.wait_ge(dve_done, VEs.n)
                    VEs(v.tensor_tensor(R, R, piece, ALU.subtract).then_inc(dve_done, 1))
                    dve.wait_ge(dve_done, VEs.n)
                VEs(v.tensor_copy(st[:, 0, :, 2 * DH0:3 * DH0], R[:, 0]).then_inc(dve_done, 1))
                VEs(v.tensor_copy(st[:, 1, :, 3 * DH0:4 * DH0], R[:, 1]).then_inc(dve_done, 1), "A.pieces", b, tt)

            rows0(0)
            for i in range(-1, LAST0 + 1):
                for kind, b, *w in side.get(i + 1, []):
                    if kind == "rows" and b:
                        rows0(b)
                if 0 <= i < UNITS0:
                    dve.wait_ge(pe_done, at("pe", "A.S", i))
                    if i >= 3:
                        dve.wait_ge(act_done, at("act", "A.P", i - 3))
                    VEs(v.tensor_reduce(mxa[:, i % 3, :], bank(i % 3)[:, 0, :].rearrange("p (h s) -> p h s", h=2), AX.X, ALU.max,
                                        negate=True).then_inc(dve_done, 1), "A.max", i)
                n = i - 1
                if 0 <= n < UNITS0:
                    dve.wait_ge(act_done, at("act", "A.P", n))
                    VEs(v.reciprocal(ria[:, n % 3, :], rsa[:, n % 3, :]).then_inc(dve_done, 1))
                    dve.wait_ge(dve_done, VEs.n)
                    for j in range(2):
                        VEs(v.tensor_scalar(Pa[:, n % 3, j, :], Pa[:, n % 3, j, :], ria[:, n % 3, j:j + 1], None, ALU.mult)
                            .then_inc(dve_done, 1), "A.Pn", n)
                for kind, b, *w in side.get(i, []):
                    if kind == "qk":
                        pieces(b, w[0])
                    elif kind == "out":
                        dve.wait_ge(pe_done, at("pe", "A.out", b, w[0]))
                        add_to_x(TPB * b + w[0], bank(7)[:, 0, 0:D], "A.out", b, w[0])
                for kind, t in maps.get(i, []):
                    if kind == "energy":
                        dve.wait_ge(pe_done, at("pe", "en", t))
                        VEs(v.tensor_reduce(m0[:, t:t + 1], bank(6)[:, 0, 0:S], AX.X, ALU.max, negate=True).then_inc(dve_done, 1), "m0", t)
                    elif kind == "scale":
                        dve.wait_ge(act_done, at("act", "en", t))
                        VEs(v.reciprocal(s0[:, t:t + 1], s0[:, t:t + 1]).then_inc(dve_done, 1))
                        dve.wait_ge(dve_done, VEs.n)
                        VEs(v.tensor_scalar(en, en, s0[:, t:t + 1], None, ALU.mult).then_inc(dve_done, 1), "enn", t)

            dve.wait_ge(dve_done, VEs.n)
            ln("B", 0, False, False)
            for b in range(B):
                if b + 1 < B:
                    ln("B", b + 1, False, False)

                def free(b=b):
                    dve.wait_ge(pe_done, at("pe", "B.xT", b - 2) if b >= 2 else at("pe", "A.rows", B - 1))
                ln_apply("B", b, False, False, free)
                for tt in range(TPB):
                    dve.wait_ge(pe_done, at("pe", "B.out", b))
                    add_to_x(TPB * b + tt, bank(2 + b % 2)[:, 0, tt * D:tt * D + D], "B.x", b, tt)
            book[("dve", "B.end")] = VEs.n

            dve.wait_ge(dve_done, VEs.n)
            dve.wait_ge(const_in, 16 * N_CONST)
            for b in range(B):
                ln("C", b, True, True)
            for b in range(B):
                def free(b=b):
                    if b < 2:
                        dve.wait_ge(pe_done, at("pe", "B.xT", b + 2))
                    else:
                        dve.wait_ge(pe_done, at("pe", "C.hT", TPB * (b - 2) + 1))
                        for i in range(TPB):
                            dve.wait_ge(h_stored[(TPB * b + i) % 4], 16)
                ln_apply("C", b, True, True, free)
                for t in range(TPB * b, TPB * b + TPB):
                    VEs(v.tensor_tensor(XS[:, t % 4, :], XS[:, t % 4, :], nwb, ALU.mult).then_inc(dve_done, 1), "C.h", t)
                for t in range(TPB * b, TPB * b + TPB):
                    dve.wait_ge(pe_done, at("pe", "C.logits", t))
                    L = bank(2 + t % 2)[:, 0, 0:E0]
                    VEs(v.max(top8[:, t, :], L).then_inc(dve_done, 1))
                    dve.wait_ge(dve_done, VEs.n)
                    VEs(v.max_index(idx8[:, t, :], top8[:, t, :], L).then_inc(dve_done, 1))
                    VEs(v.tensor_scalar(negm[:, t:t + 1], top8[:, t, 0:1], -1.0, None, ALU.mult).then_inc(dve_done, 1), "C.top", t)
                    dve.wait_ge(dve_done, VEs.n)
                    VEs(v.tensor_copy(idf, idx8[:, t, 0:K0]).then_inc(dve_done, 1))
                    dve.wait_ge(dve_done, VEs.n)
                    VEs(v.tensor_tensor(oh, iota32.rearrange("p (o e) -> p o e", o=1).broadcast_to((P, K0, E0)),
                                        idf.rearrange("p (k o) -> p k o", o=1).broadcast_to((P, K0, E0)), ALU.is_equal).then_inc(dve_done, 1))
                    VEs(v.tensor_scalar(base, idf, float(CAP), None, ALU.mult).then_inc(dve_done, 1))
                    dve.wait_ge(dve_done, VEs.n)
                    with nc.allow_low_precision(reason="0 and 1"):
                        VEs(v.tensor_reduce(sel_tile[:, t, :], oh.rearrange("p k e -> p e k"), AX.X, ALU.add).then_inc(dve_done, 1), "C.sel", t)
                    dve.wait_ge(pe_done, at("pe", "C.pos", t))
                    VEs(v.tensor_tensor(ohp, oh, bank(4 + t % 2)[:, 0, 0:E0].rearrange("p (o e) -> p o e", o=1).broadcast_to((P, K0, E0)),
                                        ALU.mult).then_inc(dve_done, 1), "C.ohp", t)
                    dve.wait_ge(dve_done, VEs.n)
                    VEs(v.tensor_reduce(posk, ohp, AX.X, ALU.add).then_inc(dve_done, 1))
                    dve.wait_ge(dve_done, VEs.n)
                    VEs(v.tensor_scalar(over, posk, float(CAP - 1), float(E0 * CAP), ALU.is_gt, ALU.mult).then_inc(dve_done, 1))
                    VEs(v.scalar_tensor_tensor(out=rowf, in0=posk, scalar=float(CAP - 1), in1=base, op0=ALU.min, op1=ALU.add).then_inc(dve_done, 1))
                    dve.wait_ge(dve_done, VEs.n)
                    VEs(v.tensor_tensor(slotf, rowf, over, ALU.add).then_inc(dve_done, 1))
                    VEs(v.tensor_copy(row[:, t, :], rowf).then_inc(dve_done, 1))
                    dve.wait_ge(dve_done, VEs.n)
                    VEs(v.tensor_copy(slot[:, t, :], slotf).then_inc(dve_done, 1), "C.slot", t)
                    dve.wait_ge(act_done, at("act", "C.ex4", t))
                    VEs(v.reciprocal(sm4[:, t:t + 1], sm4[:, t:t + 1]).then_inc(dve_done, 1))
                    dve.wait_ge(dve_done, VEs.n)
                    VEs(v.tensor_scalar(w4[:, t, :], ex4[:, t, :], sm4[:, t:t + 1], None, ALU.mult).then_inc(dve_done, 1), "C.w4", t)
            for hf in range(NHALF):
                dve.wait_ge(act_done, at("act", "C.sgs", hf))
                if hf:
                    dve.wait_ge(pe_done, at("pe", "C.sout", hf - 1))
                VEs(v.tensor_tensor(acs, sgs, bank(5)[:, 0, :], ALU.mult).then_inc(dve_done, 1), "C.sact", hf)
                dve.wait_ge(pe_done, at("pe", "C.sout", hf))
                for tt in range(HALF // P):
                    add_to_x(hf * 4 + tt, bank(6 + tt // 2)[:, 0, (tt % 2) * D:(tt % 2) * D + D], "C.xs", hf)
                dve.wait_ge(dve_done, VEs.n)
            dve.wait_ge(table_in, 16)
            VEs(v.tensor_copy(tabf[0:2 * E0, :], tab[0:2 * E0, :]).then_inc(dve_done, 1), "C.tabf")
            dve.wait_ge(pe_done, at("pe", "C.tabT"))
            VEs(v.tensor_copy(slot_tok, bank(6)[:, 0, 0:2 * E0]).then_inc(dve_done, 1), "C.slot_tok")

            def gated(e):
                dve.wait_ge(act_done, at("act", "C.sg", e))
                if e >= 2:
                    dve.wait_ge(pe_done, at("pe", "C.down", e - 2))
                VEs(v.tensor_tensor(ac[:, e % 2, :], sg[:, e % 2, :], bank(2 + e % 2)[:, 0, CAP:2 * CAP], ALU.mult).then_inc(dve_done, 1),
                    "C.act", e)

            for e in range(E0):
                dve.wait_ge(pe_done, at("pe", "C.xT", e))
                if e >= 2:
                    dve.wait_ge(pe_done, at("pe", "C.gu", e - 2))
                VEs(v.tensor_copy(XTc[:, e % 2], bank(e % 2)[:, 0, :].rearrange("p (k n) -> p k n", k=DB)).then_inc(dve_done, 1), "C.xT", e)
                if e:
                    gated(e - 1)
            gated(E0 - 1)
            for t in range(TILES):
                dve.wait_ge(y_in[t % 2], 16 * K0 * (t // 2 + 1))
                for k in range(K0):
                    VEs(v.scalar_tensor_tensor(out=X[:, t, :], in0=Y[:, t % 2, k, :], scalar=w4[:, t, k:k + 1], in1=X[:, t, :],
                                               op0=ALU.mult, op1=ALU.add).then_inc(dve_done, 1), "C.comb", t)
                    dve.wait_ge(dve_done, VEs.n)
            book[("dve", "C.end")] = VEs.n

            dve.wait_ge(act_done, at("act", "D.A"))
            VEs(v.tensor_scalar(Aneg, Aneg, -1.0, None, ALU.mult).then_inc(dve_done, 1), "D.A")
            dve.wait_ge(mamba_w_in, 16 * N_MAMBA)
            VEs(v.tensor_copy(wdt, wxp[:, :, 32:33].broadcast_to((P, IB, P))).then_inc(dve_done, 1), "D.wdt")
            for b in range(B):
                ln("D", b, True, True)
            for hf in range(NHALF):
                for b in range(BPH * hf, BPH * hf + BPH):
                    def free(b=b):
                        if b < 2:
                            dve.wait_ge(pe_done, at("pe", "C.hT", TILES - 1))
                            for i in range(4):
                                dve.wait_ge(h_stored[i], 16 * TILES // 4)
                        else:
                            dve.wait_ge(pe_done, at("pe", "D.xT", 0))
                    ln_apply("D", b, True, True, free)
                for m in range(IB):
                    dve.wait_ge(act_done, at("act", "D.xi", hf, m))
                    if hf:
                        dve.wait_ge(dve_done, VEs.n)
                        dve.wait_ge(pe_done, at("pe", "D.xs", hf - 1))
                    um = u[:, m, :].rearrange("p (b s) -> p b s", b=BPH)
                    VEs(v.tensor_scalar(um, xi[:, m, :, 0:S], cw[:, m, 0:1], cb[:, m:m + 1], ALU.mult, ALU.add).then_inc(dve_done, 1))
                    for k in range(1, KC):
                        dve.wait_ge(dve_done, VEs.n)
                        VEs(v.scalar_tensor_tensor(out=um, in0=xi[:, m, :, k:k + S], scalar=cw[:, m, k:k + 1], in1=um,
                                                   op0=ALU.mult, op1=ALU.add).then_inc(dve_done, 1), "D.conv", hf, m)
                dve.wait_ge(pe_done, at("pe", "D.xs", hf))
                NR = 2 * NST
                if hf:
                    dve.wait_ge(pe_done, at("pe", "D.C", hf * NST - 1))
                VEs(v.tensor_copy(xs3f[0:NR, :], bank(7)[0:NR, 0, :]).then_inc(dve_done, 1), "D.xsf", hf)
                dve.wait_ge(dve_done, VEs.n)
                VEs(v.tensor_copy(xs3[0:NR, :], xs3f[0:NR, :]).then_inc(dve_done, 1))
                for i in range(1, 3):
                    dve.wait_ge(dve_done, VEs.n)
                    VEs(v.tensor_tensor(xs3f[0:NR, :], xs3f[0:NR, :], xs3[0:NR, :] if i == 1 else xs3m[0:NR, :], ALU.subtract).then_inc(dve_done, 1))
                    dve.wait_ge(dve_done, VEs.n)
                    if i == 1:
                        VEs(v.tensor_copy(xs3m[0:NR, :], xs3f[0:NR, :]).then_inc(dve_done, 1))
                        dve.wait_ge(dve_done, VEs.n)
                    VEs(v.tensor_copy(xs3[NR * i:NR * i + NR, :], xs3f[0:NR, :]).then_inc(dve_done, 1), "D.xs3", hf)
                dve.wait_ge(pe_done, at("pe", "D.dt", hf))
                for m in range(IB):
                    if hf and m == 0:
                        dve.wait_ge(act_done, at("act", "D.dA", hf * NST - 1))
                    VEs(v.tensor_scalar(dt[:, m, :], bank(6)[:, 0, :], dtw[:, m:m + 1], dtb[:, m:m + 1], ALU.mult, ALU.add).then_inc(dve_done, 1), "D.v", hf, m)
                dve.wait_ge(act_done, at("act", "D.sp", hf))
                VEs(v.scalar_tensor_tensor(out=dt, in0=dt, scalar=0.0, in1=e1, op0=ALU.max, op1=ALU.add).then_inc(dve_done, 1))
                dve.wait_ge(dve_done, VEs.n)
                VEs(v.tensor_tensor(dtu, dt, u, ALU.mult).then_inc(dve_done, 1), "D.dtu", hf)
                flat = "p m n -> p (m n)"
                for n in range(NST):
                    s = hf * NST + n
                    dve.wait_ge(pool_done, at("pool", "D.Bu", s))
                    dve.wait_ge(act_done, at("act", "D.dA", s))
                    h = hbuf(s)
                    VEs(v.tensor_tensor_scan(h.rearrange(flat), dA[:, s % 2].rearrange(flat), h.rearrange(flat), 0.0,
                                             ALU.mult, ALU.add).then_inc(dve_done, 1), "D.scan", s)
                    dve.wait_ge(dve_done, VEs.n)
                    dve.wait_ge(pe_done, at("pe", "D.C", s))
                    VEs(v.tensor_tensor(h, h, bank(4 + s % 2).broadcast_to((P, IB, HALF)), ALU.mult).then_inc(dve_done, 1), "D.hC", s)
                dve.wait_ge(pe_done, at("pe", "D.sum", hf * NST + NST - 1))
                for m in range(IB):
                    VEs(v.scalar_tensor_tensor(out=u[:, m, :], in0=u[:, m, :], scalar=dpar[:, m:m + 1], in1=bank(m)[:, 0, :],
                                               op0=ALU.mult, op1=ALU.add).then_inc(dve_done, 1), "D.yu", hf)
                dve.wait_ge(dve_done, VEs.n)
                for m in range(IB):
                    dve.wait_ge(act_done, at("act", "D.sz", hf, m))
                    VEs(v.tensor_tensor(sz[:, m, :], sz[:, m, :], u[:, m, :], ALU.mult).then_inc(dve_done, 1), "D.yz", hf, m)
                dve.wait_ge(pe_done, at("pe", "D.out", hf))
                for tt in range(HALF // P):
                    add_to_x(hf * 4 + tt, bank(4 + tt // 2)[:, 0, (tt % 2) * D:(tt % 2) * D + D], "D.x", hf)
            book[("dve", "D.end")] = VEs.n

            dve.wait_ge(xattn1_w_in, 16 * N_XATTN1)
            VEs(v.tensor_scalar(mrowb[0:1, :], mrow[0:1].rearrange("p b s -> p (b s)"), 1.0, -NEG, ALU.subtract, ALU.mult).then_inc(dve_done, 1), "E.mrow")
            VEs(v.tensor_reduce(mflag, vfl, AX.X, ALU.max).then_inc(dve_done, 1))
            VEs(v.memset(one1, 1.0).then_inc(dve_done, 1), "E.one")
            dve.wait_ge(dve_done, VEs.n)
            for b in range(B):
                ln("E", b, False, False)

            def rows1(b):
                def free():
                    dve.wait_ge(pe_done, at("pe", "E.rows", b - 2) if b >= 2 else at("pe", "D.xT", NHALF - 1))
                ln_apply("E", b, False, False, free)

            rows1(0)
            side = side_work()
            for i in range(-1, LAST_STEP + 1):
                for kind, b, *w in side.get(i + 1, []):
                    if kind == "rows" and b:
                        rows1(b)
                if 0 <= i < UNITS:
                    dve.wait_ge(pe_done, at("pe", "E.S", i))
                    if i >= 3:
                        dve.wait_ge(act_done, at("act", "E.P", i - 3))
                    VEs(v.tensor_reduce(mxe[:, i % 3, :], bank(i % 3)[:, 0, :].rearrange("p (h s) -> p h s", h=GR), AX.X, ALU.max,
                                        negate=True).then_inc(dve_done, 1), "E.max", i)
                n = i - 1
                if 0 <= n < UNITS:
                    b = unit(n)[0]
                    dve.wait_ge(act_done, at("act", "E.P", n))
                    VEs(v.reciprocal(rie[:, n % 3, :], rse[:, n % 3, :]).then_inc(dve_done, 1))
                    dve.wait_ge(dve_done, VEs.n)
                    for j in range(GR):
                        VEs(v.tensor_scalar(Pe[:, n % 3, j, :], Pe[:, n % 3, j, :], rie[:, n % 3, j:j + 1], mflag[:, b:b + 1],
                                            ALU.mult, ALU.mult).then_inc(dve_done, 1), "E.Pn", n)
                n = i - 2
                if 0 <= n < UNITS:
                    dve.wait_ge(pe_done, at("pe", "E.PT", n))
                    VEs(v.tensor_copy(PTe[:, n % 2], bank(3 + n % 2)[:, 0, :].rearrange("p (i k q) -> p i k q", i=GR, k=2))
                        .then_inc(dve_done, 1), "E.PT", n)
                for kind, b, *w in side.get(i, []):
                    if kind == "values":
                        dve.wait_ge(pe_done, at("pe", "E.values", b, w[0]))
                        if b >= 2 and w[0] == 0:
                            dve.wait_ge(pe_done, at("pe", "E.av", (b - 1) * UPB - 1))
                        VEs(v.tensor_copy(V1[:, b % 2, w[0] // 2, 512 * (w[0] % 2):512 * (w[0] % 2) + 512], bank(7)[:, 0, :])
                            .then_inc(dve_done, 1), "E.values", b, w[0])
                    elif kind == "output":
                        dve.wait_ge(pe_done, at("pe", "E.output", b, w[0]))
                        add_to_x(TPB * b + w[0], bank(7)[:, 0, 0:D], "E.output", b, w[0])
            dve.wait_ge(dve_done, VEs.n)

            for b in range(B):
                ln("F", b, False, False)
            for b in range(B):
                def free(b=b):
                    dve.wait_ge(pe_done, at("pe", "F.xT", b - 2) if b >= 2 else at("pe", "E.rows", B - 1))
                ln_apply("F", b, False, False, free)
            dve.wait_ge(const_in, 16 * N_CONST)
            dve.wait_ge(ffn1_w_in, 16 * N_FFN1)
            for t in range(TILES):
                dve.wait_ge(pe_done, at("pe", "F.logits", t))
                VEs(v.tensor_copy(lg[:, t, :], bank(2 + t % 2)[:, 0, 0:E1 + 1]).then_inc(dve_done, 1), "F.lg", t)
                dve.wait_ge(dve_done, VEs.n)
                VEs(v.tensor_reduce(np8[:, t:t + 1], lg[:, t, 0:E1], AX.X, ALU.max, negate=True).then_inc(dve_done, 1), "F.max", t)
                dve.wait_ge(act_done, at("act", "F.pr", t))
                VEs(v.reciprocal(rp[:, t:t + 1], sp1[:, t:t + 1]).then_inc(dve_done, 1))
                VEs(v.tensor_scalar(cc[:, t, E1:], lg[:, t, E1:], 1.0, None, ALU.add).then_inc(dve_done, 1))
                dve.wait_ge(dve_done, VEs.n)
                VEs(v.tensor_scalar(pr[:, t, :], pr[:, t, :], rp[:, t:t + 1], None, ALU.mult).then_inc(dve_done, 1))
                VEs(v.reciprocal(cc[:, t, E1:], cc[:, t, E1:]).then_inc(dve_done, 1))
                dve.wait_ge(dve_done, VEs.n)
                VEs(v.max(tp8[:, t, :], pr[:, t, :]).then_inc(dve_done, 1))
                dve.wait_ge(dve_done, VEs.n)
                VEs(v.max_index(ti8[:, t, :], tp8[:, t, :], pr[:, t, :]).then_inc(dve_done, 1))
                dve.wait_ge(dve_done, VEs.n)
                VEs(v.tensor_copy(tif[:, t, :], ti8[:, t, 0:2]).then_inc(dve_done, 1))
                dve.wait_ge(dve_done, VEs.n)
                VEs(v.tensor_scalar(cc[:, t, 0:E1], iota8, tif[:, t, 0:1], tp8[:, t, 0:1], ALU.is_equal, ALU.mult).then_inc(dve_done, 1))
                VEs(v.tensor_scalar(c2[:, t, :], iota8, tif[:, t, 1:2], tp8[:, t, 1:2], ALU.is_equal, ALU.mult).then_inc(dve_done, 1))
                dve.wait_ge(dve_done, VEs.n)
                VEs(v.tensor_tensor(cc[:, t, 0:E1], cc[:, t, 0:E1], c2[:, t, :], ALU.add).then_inc(dve_done, 1))
                dve.wait_ge(dve_done, VEs.n)
                W = E1 + 1
                VEs(v.tensor_copy(chb[:, 0:W], cc[:, t, :]).then_inc(dve_done, 1))
                dve.wait_ge(dve_done, VEs.n)
                VEs(v.tensor_copy(c27[:, t, 0:W], chb[:, 0:W]).then_inc(dve_done, 1))
                VEs(v.tensor_tensor(r1c, cc[:, t, :], chb[:, 0:W], ALU.subtract).then_inc(dve_done, 1))
                dve.wait_ge(dve_done, VEs.n)
                VEs(v.tensor_copy(cmb[:, 0:W], r1c).then_inc(dve_done, 1))
                dve.wait_ge(dve_done, VEs.n)
                VEs(v.tensor_copy(c27[:, t, W:2 * W], cmb[:, 0:W]).then_inc(dve_done, 1))
                VEs(v.tensor_tensor(c27[:, t, 2 * W:], r1c, cmb[:, 0:W], ALU.subtract).then_inc(dve_done, 1), "F.c27", t)
                dve.wait_ge(dve_done, VEs.n)
            for hf in range(NHALF):
                for f in range(FB):
                    n = hf * FB + f
                    m = min(P, FT - f * P)
                    dve.wait_ge(act_done, at("act", "F.sg", n))
                    VEs(v.tensor_tensor(tf[0:m, n % 2, :], sgf[0:m, n % 2, :], bank(2 + n % 2)[0:m, 0, :], ALU.mult).then_inc(dve_done, 1))
                    dve.wait_ge(dve_done, VEs.n)
                    if n >= 3:
                        dve.wait_ge(pe_done, at("pe", "F.down", n - 3))
                    VEs(v.tensor_tensor(acf[0:m, n % 3, :], tf[0:m, n % 2, :], bank(4 + n % 2)[0:m, 0, :], ALU.mult).then_inc(dve_done, 1), "F.act", n)
                dve.wait_ge(pe_done, at("pe", "F.down", hf * FB + FB - 1))
                for tt in range(HALF // P):
                    add_to_x(hf * 4 + tt, bank(6 + tt // 2)[:, 0, (tt % 2) * D:(tt % 2) * D + D], "F.x", hf * 4 + tt)

        @block.tensor
        def _(pe):
            te = nc.tensor

            def mm(dst, lhsT, rhs, start=True, stop=True, **kw):
                return te.matmul(dst, lhsT, rhs, start=start, stop=stop, **kw)

            def transposes(dst, name, b, step):
                pe.wait_ge(dve_done, at("dve", name + ".xs", b))
                for tt in range(TPB):
                    for k in range(DB):
                        last = te.transpose(dst[:, k, tt * P:tt * P + P], XS[:, (TPB * b + tt) % 4, k * P:k * P + P], ident[:, :])
                PEs(last.then_inc(pe_done, 1), *step)

            pe.wait_ge(const_in, 16 * N_CONST)
            pe.wait_ge(ctx_in, 16)
            pe.wait_ge(xattn_w_in, 16 * N_XATTN)
            pe.wait_ge(attn_w_in, 16 * N_ATTN)
            side, maps = side_work0(), map_work()
            user = {6: None, 7: None}

            def emptied(n, by=None):
                if user[n]:
                    pe.wait_ge(act_done if user[n][0] == "act" else dve_done, at(*user[n]))
                user[n] = by

            for i in range(-1, LAST0 + 1):
                if 0 <= i < UNITS0:
                    b, tt, p = unit0(i)
                    if p == 0:
                        pe.wait_ge(act_done, at("act", "A.turn", b, TPB - 1, 0, 1))
                    if i >= 3:
                        pe.wait_ge(act_done, at("act", "A.P", i - 3))
                    for j in range(2):
                        h = 2 * p + j
                        last = mm(bank(i % 3)[:, 0, j * S:j * S + S], QT[0:KA, b % 2, 0, h, tt * P:tt * P + P], QT[0:KA, b % 2, 1, h, :])
                    PEs(last.then_inc(pe_done, 1), "A.S", i)
                n = i - 2
                if 0 <= n < UNITS0:
                    pe.wait_ge(dve_done, at("dve", "A.Pn", n))
                    if n >= 2:
                        pe.wait_ge(act_done, at("act", "A.PT", n - 2))
                    for j in range(2):
                        for k in range(2):
                            o = (j * 2 + k) * P
                            last = te.transpose(bank(3 + n % 2)[:, 0, o:o + P], Pa[:, n % 3, j, k * P:k * P + P], ident[:, :])
                    PEs(last.then_inc(pe_done, 1), "A.PT", n)
                n = i - 3
                if 0 <= n < UNITS0:
                    b, tt, p = unit0(n)
                    pe.wait_ge(act_done, at("act", "A.PT", n))
                    if p == 0 and n:
                        pe.wait_ge(act_done, at("act", "A.cT", n // UPT0 - 1))
                    for j in range(2):
                        h = 2 * p + j
                        r = 32 * (h % 4)
                        for k in range(2):
                            last = mm(bank(5)[r:r + 32, 0, (h // 4) * P:(h // 4) * P + P], Va[:, b % 2, k, h, :], PTa[:, n % 2, j, k, :], k == 0, k == 1)
                    PEs(last.then_inc(pe_done, 1), "A.av", n)
                for kind, b, *w in side.get(i, []):
                    emptied(7, ("dve" if kind in ("qk", "out") else "act", "A." + kind, b, *w))
                    if kind == "rows":
                        transposes(bank(7)[:, 0, :].rearrange("p (k n) -> p k n", k=DB), "A", b, ("A.rows", b))
                        continue
                    if kind in ("qk", "v"):
                        pe.wait_ge(act_done, at("act", "A.rows", b))
                        c0, c1 = (0, 2 * D) if kind == "qk" else (2 * D, 3 * D)
                        for k in range(DB):
                            last = mm(bank(7)[:, 0, 0:c1 - c0], xTa[:, b % 2, k, w[0] * P:w[0] * P + P], w_in[:, k, c0:c1], k == 0, k == DB - 1)
                    elif kind == "turn":
                        tt, qk, half = w
                        pe.wait_ge(pool_done, at("pool", "A.stack", b, tt))
                        pb = bank(7)[0:KA, 0, :].bitcast(BF16)
                        for h in range(8):
                            last = te.transpose(pb[:, h * P:h * P + P], stack[:, tt, qk, 8 * half + h, :], identb)
                    else:
                        pe.wait_ge(act_done, at("act", "A.cT", TPB * b + w[0]))
                        for g in range(4):
                            last = mm(bank(7)[:, 0, 0:D], CTa[:, g, :], w_out[:, g, :], g == 0, g == 3)
                    PEs(last.then_inc(pe_done, 1), "A." + kind, b, *w)
                for kind, t in maps.get(i, []):
                    if kind == "context":
                        emptied(6, ("act", "context", t))
                        for j in range(4):
                            last = te.transpose(bank(6)[:, 0, j * P:j * P + P], cx[:, 4 * t + j, :], ident[:, :])
                        PEs(last.then_inc(pe_done, 1), "context", t)
                    elif kind == "qk":
                        emptied(6, ("act", "map.qk", t))
                        PEs(mm(bank(6)[:, 0, :], (wq0, wk0)[t // 2], ctxT[:, 512 * (t % 2):512 * (t % 2) + 512]).then_inc(pe_done, 1), "map.qk", t)
                    elif kind == "energy":
                        emptied(6, ("act", "en", t))
                        b = t // 2
                        PEs(mm(bank(6)[:, 0, 0:S], q0[:, t * P:t * P + P], k0[:, b * S:b * S + S]).then_inc(pe_done, 1), "en", t)
                    elif kind == "turn":
                        emptied(6, ("act", "map", t))
                        pe.wait_ge(dve_done, at("dve", "enn", t))
                        for m in range(2):
                            last = te.transpose(bank(6)[:, 0, m * P:m * P + P], en[:, m * P:m * P + P], ident[:, :])
                        PEs(last.then_inc(pe_done, 1), "map", t)

            for b in range(B):
                if b >= 2:
                    pe.wait_ge(act_done, at("act", "B.xT", b - 2))
                transposes(bank(b % 2)[:, 0, :].rearrange("p (k n) -> p k n", k=DB), "B", b, ("B.xT", b))
                pe.wait_ge(act_done, at("act", "B.xT", b))
                if b >= 2:
                    pe.wait_ge(dve_done, at("dve", "B.x", b - 2, 1))
                for tt in range(TPB):
                    for k in range(DB):
                        last = mm(bank(2 + b % 2)[:, 0, tt * D:tt * D + D], xTb[:, b % 2, k, tt * P:tt * P + P], attT[:, b, k, :], k == 0, k == DB - 1)
                PEs(last.then_inc(pe_done, 1), "B.out", b)
            book[("pe", "B.end")] = PEs.n

            pe.wait_ge(moe_w_in, 16 * N_MOE)
            pe.wait_ge(pool_done, at("pool", "ones"))
            pe.wait_ge(dve_done, at("dve", "B.end"))
            for t in range(TILES):
                pe.wait_ge(dve_done, at("dve", "C.h", t))
                if t >= 2:
                    pe.wait_ge(act_done, at("act", "C.hT", t - 2))
                for k in range(DB):
                    last = te.transpose(bank(t % 2)[:, 0, k * P:k * P + P], XS[:, t % 4, k * P:k * P + P], ident[:, :])
                PEs(last.then_inc(pe_done, 1), "C.hT", t)
                pe.wait_ge(act_done, at("act", "C.hT", t))
                if t >= 2:
                    pe.wait_ge(dve_done, at("dve", "C.top", t - 2))
                for k in range(DB):
                    last = mm(bank(2 + t % 2)[:, 0, 0:E0], hT[:, k, t * P:t * P + P], gw[:, k, :], k == 0, k == DB - 1)
                PEs(last.then_inc(pe_done, 1), "C.logits", t)
                pe.wait_ge(dve_done, at("dve", "C.sel", t))
                if t >= 2:
                    pe.wait_ge(dve_done, at("dve", "C.ohp", t - 2))
                for i in range(t):
                    mm(bank(4 + t % 2)[:, 0, 0:E0], ones, sel_tile[:, i, :], i == 0, False)
                PEs(mm(bank(4 + t % 2)[:, 0, 0:E0], tri, sel_tile[:, t, :], t == 0, True).then_inc(pe_done, 1), "C.pos", t)
            pe.wait_ge(dve_done, at("dve", "C.slot", TILES - 1))
            for hf in range(NHALF):
                if hf:
                    pe.wait_ge(dve_done, at("dve", "C.xs", hf - 1))
                for w in range(2):
                    for k in range(DB):
                        last = mm(bank(4 + w)[:, 0, :], sgu[:, k, w * I0:w * I0 + I0], hT[:, k, hf * HALF:hf * HALF + HALF], k == 0, k == DB - 1)
                PEs(last.then_inc(pe_done, 1), "C.sgu", hf)
                pe.wait_ge(dve_done, at("dve", "C.sact", hf))
                for tt in range(HALF // P):
                    last = mm(bank(6 + tt // 2)[:, 0, (tt % 2) * D:(tt % 2) * D + D], acs[:, tt * P:tt * P + P], sdn)
                PEs(last.then_inc(pe_done, 1), "C.sout", hf)
            pe.wait_ge(dve_done, at("dve", "C.tabf"))
            PEs(te.transpose(bank(6)[:, 0, 0:2 * E0], tabf[0:2 * E0, :], ident[0:2 * E0, 0:2 * E0]).then_inc(pe_done, 1), "C.tabT")

            def expert_rows(e):
                pe.wait_ge(gathered[e % 4], 16 * 2 * (e // 4 + 1))
                if e >= 2:
                    pe.wait_ge(dve_done, at("dve", "C.xT", e - 2))
                for s in range(2):
                    for k in range(DB):
                        last = te.transpose(bank(e % 2)[:, 0, k * CAP + s * P:k * CAP + s * P + P], G[:, e % 4, s, k * P:k * P + P], ident[:, :])
                PEs(last.then_inc(pe_done, 1), "C.xT", e)

            def expert_up(e):
                pe.wait_ge(dve_done, at("dve", "C.xT", e))
                pe.wait_ge(expert_in[e % NW], 32 * (e // NW + 1))
                if e >= 2:
                    pe.wait_ge(dve_done, at("dve", "C.act", e - 2))
                for w in range(2):
                    for k in range(DB):
                        last = mm(bank(2 + e % 2)[:, 0, w * CAP:w * CAP + CAP], w13[:, e % NW, k, w * I0:w * I0 + I0], XTc[:, e % 2, k, :],
                                  k == 0, k == DB - 1)
                PEs(last.then_inc(pe_done, 1), "C.gu", e)

            def expert_down(e):
                pe.wait_ge(dve_done, at("dve", "C.act", e))
                if e >= 2:
                    pe.wait_ge(act_done, at("act", "C.eo", e - 2))
                for s in range(2):
                    last = mm(bank(4 + e % 2)[:, 0, s * D:s * D + D], ac[:, e % 2, s * P:s * P + P], w2[:, e % NW, :])
                PEs(last.then_inc(pe_done, 1), "C.down", e)

            expert_rows(0)
            expert_up(0)
            for e in range(E0):
                if e + 1 < E0:
                    expert_rows(e + 1)
                    expert_up(e + 1)
                expert_down(e)

            pe.wait_ge(mamba_w_in, 16 * N_MAMBA)
            pe.wait_ge(act_done, at("act", "C.eo", E0 - 1))
            pe.wait_ge(dve_done, at("dve", "D.wdt"))
            for hf in range(NHALF):
                if hf:
                    pe.wait_ge(act_done, at("act", "D.Bb", hf * NST - 1))
                    pe.wait_ge(dve_done, at("dve", "D.yu", hf - 1))
                for b in range(BPH * hf, BPH * hf + BPH):
                    pe.wait_ge(dve_done, at("dve", "D.xs", b))
                    for tt in range(TPB):
                        for k in range(DB):
                            o = (b % BPH) * S + tt * P
                            last = te.transpose(bank(6 + k)[:, 0, o:o + P], XS[:, (TPB * b + tt) % 4, k * P:k * P + P], ident[:, :])
                PEs(last.then_inc(pe_done, 1), "D.xT", hf)
                pe.wait_ge(act_done, at("act", "D.xT", hf))
                for m in range(2 * IB):
                    if m >= IB + 2:
                        pe.wait_ge(act_done, at("act", "D.sz", hf, m - IB - 2))
                    elif m >= IB and hf:
                        pe.wait_ge(dve_done, at("dve", "D.x", hf - 1))
                    dst = bank(m if m < IB else 4 + m % 2)[:, 0, :]
                    for k in range(DB):
                        last = mm(dst, wip[:, k, m * P:m * P + P], xTd[:, k, :], k == 0, k == DB - 1)
                    PEs(last.then_inc(pe_done, 1), *(("D.xi", hf, m) if m < IB else ("D.z", hf, m - IB)))
                pe.wait_ge(act_done, at("act", "D.u", hf, IB - 1))
                for m in range(IB):
                    last = mm(bank(7)[0:33, 0, :], wxp[:, m, :], u[:, m, :], m == 0, m == IB - 1)
                for m in range(IB):
                    last = mm(bank(6)[:, 0, :], wdt[:, m, :], u[:, m, :], m == 0, m == IB - 1)
                    if m == IB - 1:
                        PEs(last.then_inc(pe_done, 1), "D.xs", hf)
                        book[("pe", "D.dt", hf)] = PEs.n
                pe.wait_ge(dve_done, at("dve", "D.v", hf, IB - 1))
                pe.wait_ge(dve_done, at("dve", "D.xs3", hf))
                pe.wait_ge(act_done, at("act", "D.sz", hf, IB - 1))

                def spread(s):
                    n = s % NST
                    if n:
                        pe.wait_ge(act_done, at("act", "D.Bb", s - 1))
                    PEs(mm(bank(6)[:, 0, :], selbc[0:96, n, :], xs3[0:96, :]).then_inc(pe_done, 1), "D.B", s)
                    if n >= 2:
                        pe.wait_ge(dve_done, at("dve", "D.hC", s - 2))
                    PEs(mm(bank(4 + s % 2)[:, 0, :], selbc[0:96, NST + n, :], xs3[0:96, :]).then_inc(pe_done, 1), "D.C", s)

                s0_ = hf * NST
                spread(s0_)
                spread(s0_ + 1)
                for s in range(s0_, s0_ + NST):
                    pe.wait_ge(dve_done, at("dve", "D.hC", s))
                    for m in range(IB):
                        last = mm(bank(m)[:, 0, :], ident[:, :], hbuf(s)[:, m, :], s == s0_, s == s0_ + NST - 1)
                    PEs(last.then_inc(pe_done, 1), "D.sum", s)
                    if s + 2 < s0_ + NST:
                        spread(s + 2)
                for tt in range(HALF // P):
                    for m in range(IB):
                        pe.wait_ge(dve_done, at("dve", "D.yz", hf, m))
                        last = mm(bank(4 + tt // 2)[:, 0, (tt % 2) * D:(tt % 2) * D + D], sz[:, m, tt * P:tt * P + P], wop[:, m, :], m == 0, m == IB - 1)
                PEs(last.then_inc(pe_done, 1), "D.out", hf)
            book[("pe", "D.end")] = PEs.n

            pe.wait_ge(xattn1_w_in, 16 * N_XATTN1)
            pe.wait_ge(dve_done, at("dve", "E.one"))
            pe.wait_ge(dve_done, at("dve", "D.x", NHALF - 1))
            side = side_work()
            bank7 = [None]

            def item(kind, b, w=()):
                if bank7[0]:
                    pe.wait_ge(act_done if bank7[0][0] == "act" else dve_done, at(*bank7[0]))
                step = ("E." + kind, b, *w)
                if kind == "rows":
                    transposes(bank(7)[:, 0, :].rearrange("p (k n) -> p k n", k=DB), "E", b, step)
                elif kind == "keys":
                    for j in range(2):
                        h = 2 * w[0] + j
                        last = mm(bank(7)[:, 0, j * S:j * S + S], wk1[:, h * P:h * P + P], ctxT[:, b * S:b * S + S])
                    PEs(last.then_inc(pe_done, 1), *step)
                elif kind == "values":
                    o = b * S + (w[0] // 2) * P
                    PEs(mm(bank(7)[:, 0, :], ctxT[:, o:o + P], wv1[:, (w[0] % 2) * 512:(w[0] % 2) * 512 + 512]).then_inc(pe_done, 1), *step)
                elif kind == "queries":
                    pe.wait_ge(act_done, at("act", "E.rows", b))
                    for j in range(GR):
                        h = GR * w[0] + j
                        for k in range(DB):
                            last = mm(bank(7)[:, 0, j * S:j * S + S], wq1[:, k, h * P:h * P + P], xTe[:, b % 2, k, :], k == 0, k == DB - 1)
                    PEs(last.then_inc(pe_done, 1), *step)
                else:
                    pe.wait_ge(act_done, at("act", "E.OT", (b + 1) * HKV - 1))
                    for h in range(H1):
                        last = mm(bank(7)[:, 0, 0:D], OT[:, w[0], h, :], wo1[:, h, :], h == 0, h == H1 - 1)
                    PEs(last.then_inc(pe_done, 1), *step)
                bank7[0] = ("dve" if kind in ("values", "output") else "act", *step)

            for i in range(-1, LAST_STEP + 1):
                if 0 <= i < UNITS:
                    b, h, qt = unit(i)
                    pe.wait_ge(act_done, at("act", "E.queries", b, h))
                    if i % UPB == 0:
                        pe.wait_ge(act_done, at("act", "E.keys", b, 3))
                    if i >= 3:
                        pe.wait_ge(act_done, at("act", "E.P", i - 3))
                    dst = bank(i % 3)[:, 0, :]
                    for j in range(GR):
                        mm(dst[:, j * S:j * S + S], QE[:, (b * HKV + h) % 3, j, qt * P:qt * P + P], kT[:, b % 2, h, :], j == 0, False,
                           skip_group_check=True)
                    mr = mrowb[0:1, b * S:b * S + S].rearrange("p (o s) -> p o s", o=1).broadcast_to((1, GR, S))
                    last = mm(dst.rearrange("p (o s) -> p o s", o=GR), one1[0:1, :], mr, False, True, skip_group_check=True)
                    PEs(last.then_inc(pe_done, 1), "E.S", i)
                n = i - 2
                if 0 <= n < UNITS:
                    pe.wait_ge(dve_done, at("dve", "E.Pn", n))
                    if n >= 2:
                        pe.wait_ge(dve_done, at("dve", "E.PT", n - 2))
                    for j in range(GR):
                        for k in range(2):
                            o = (j * 2 + k) * P
                            last = te.transpose(bank(3 + n % 2)[:, 0, o:o + P], Pe[:, n % 3, j, k * P:k * P + P], ident[:, :])
                    PEs(last.then_inc(pe_done, 1), "E.PT", n)
                n = i - 3
                if 0 <= n < UNITS:
                    b, h, qt = unit(n)
                    pe.wait_ge(dve_done, at("dve", "E.PT", n))
                    if n % UPB == 0:
                        pe.wait_ge(dve_done, at("dve", "E.values", b, 3))
                    if n >= 4 and n % 2 == 0:
                        pe.wait_ge(act_done, at("act", "E.OT", n // 2 - 2))
                    o = qt * GR * P
                    for k in range(2):
                        last = mm(bank(5 + n // 2 % 2)[:, 0, o:o + GR * P].rearrange("p (g q) -> p g q", g=GR), V1[:, b % 2, k, h * P:h * P + P],
                                  PTe[:, n % 2, :, k, :], k == 0, k == 1)
                    PEs(last.then_inc(pe_done, 1), "E.av", n)
                for kind, b, *w in side.get(i, []):
                    item(kind, b, w)

            pe.wait_ge(ffn1_w_in, 16 * N_FFN1)
            pe.wait_ge(dve_done, at("dve", "E.output", B - 1, TPB - 1))
            for b in range(B):
                if b >= 2:
                    pe.wait_ge(act_done, at("act", "F.xT", b - 2))
                transposes(bank(b % 2)[:, 0, :].rearrange("p (k n) -> p k n", k=DB), "F", b, ("F.xT", b))

            def weights_turned(t):
                pe.wait_ge(dve_done, at("dve", "F.c27", t))
                if t >= 2:
                    pe.wait_ge(act_done, at("act", "F.cT", t - 2))
                PEs(te.transpose(bank(4 + t % 2)[0:27, 0, 0:P], c27[:, t, :], ident[:, :]).then_inc(pe_done, 1), "F.cT", t)

            for t in range(TILES):
                pe.wait_ge(act_done, at("act", "F.xT", t // TPB))
                if t >= 2:
                    pe.wait_ge(dve_done, at("dve", "F.lg", t - 2))
                o = (t % 4) * P
                for k in range(DB):
                    last = mm(bank(2 + t % 2)[:, 0, 0:E1 + 1], xTf[:, t // 4, k, o:o + P], wr[:, k, :], k == 0, k == DB - 1)
                PEs(last.then_inc(pe_done, 1), "F.logits", t)
                if t:
                    weights_turned(t - 1)
            weights_turned(TILES - 1)
            pe.wait_ge(act_done, at("act", "F.cT", TILES - 1))

            def up(n):
                hf, f = n // FB, n % FB
                m = min(P, FT - f * P)
                if n >= 2:
                    pe.wait_ge(dve_done, at("dve", "F.act", n - 2))
                for w_, bk in ((wg, n % 2), (wu, 2 + n % 2)):
                    for k in range(DB):
                        mm(bank(bk)[0:m, 0, :], w_[:, k, f * P:f * P + m], xTf[:, hf, k, :], k == 0, k == DB - 1)
                PEs(mm(bank(4 + n % 2)[0:m, 0, :], sel27[0:27, f * P:f * P + m], cT[0:27, hf * HALF:hf * HALF + HALF]).then_inc(pe_done, 1), "F.gu", n)

            up(0)
            for n in range(NHALF * FB):
                hf, f = n // FB, n % FB
                m = min(P, FT - f * P)
                if n + 1 < NHALF * FB:
                    up(n + 1)
                pe.wait_ge(dve_done, at("dve", "F.act", n))
                if f == 0 and hf:
                    pe.wait_ge(dve_done, at("dve", "F.x", hf * 4 - 1))
                for tt in range(HALF // P):
                    last = mm(bank(6 + tt // 2)[:, 0, (tt % 2) * D:(tt % 2) * D + D], acf[0:m, n % 3, tt * P:tt * P + P], wd[0:m, f, :],
                              f == 0 and tt % 2 == 0, f == FB - 1, skip_group_check=True)
                PEs(last.then_inc(pe_done, 1), "F.down", n)
    return book


def kernel(**inputs):
    import ml_dtypes
    from concourse import bacc
    from concourse.bass_utils import run_bass_kernel_spmd

    f = {k: np.asarray(v) for k, v in inputs.items()}
    bf = ml_dtypes.bfloat16

    def turned(name):
        return np.ascontiguousarray(f[name].T)

    def by_row(name):
        return f[name].reshape(IB, P).T

    inv = (1.0 / 10000.0 ** (np.arange(0, ROT, 2, dtype=np.float32) / ROT)).astype(np.float32)
    ang = np.repeat(np.arange(S, dtype=np.float32)[:, None] * inv[None, :], 2, axis=1)
    cos, sin = np.cos(ang), np.sin(ang) * np.tile(np.array([-1.0, 1.0], np.float32), ROT // 2)
    rope = np.stack([cos, sin], 1).astype(np.float32).reshape(TPB, P, 1, 2, ROT)
    rope = np.concatenate([rope * np.float32(DH0 ** -0.5), rope], axis=2).transpose(1, 0, 2, 3, 4)
    r = np.arange(96)[:, None, None] % (2 * NST) == np.arange(2 * NST)[None, :, None]
    selbc = np.broadcast_to(r, (96, 2 * NST, P)).astype(bf)
    which = np.minimum(np.arange(FB * P) // F1, E1)
    sel27 = (np.arange(27)[:, None] % (E1 + 1) == which[None, :]).astype(bf)
    tri = (np.arange(P)[:, None] < np.arange(P)[None, :]).astype(bf)
    wd = np.concatenate([f["L1_ffn_Wd"].reshape(E1 * F1, D), f["L1_ffn_Sd"], np.zeros((FB * P - FT, D), np.float32)])

    w_out = np.zeros((4, 32, 4, D), np.float32)
    w_out[:, :DH0] = f["L0_attn_W_out"].reshape(4, 4, DH0, D).transpose(1, 2, 0, 3)
    w_out = w_out.reshape(P, 4, D)

    def flat(e, shared):
        return np.concatenate([f[e].transpose(1, 0, 2).reshape(D, E1 * F1), f[shared]], axis=1)

    arrays = {
        "x": f["x"], "ctx": f["ctx_1024"], "mask": f["mask_BxS2_bf1"].view(np.uint8),
        "ident": np.eye(P, dtype=np.float32),
        "lnw": np.stack([f[n].reshape(DB, P).T for n in ("L0_attn_ln_w", "L0_attn_ln_b", "L0_ffn_norm_w", "L1_attn_norm_w")], 1),
        "wq0T": turned("L0_xattn_Wq"), "wk0T": turned("L0_xattn_Wk"),
        "bqk": np.stack([f["L0_xattn_bq"], f["L0_xattn_bk"]], 1),
        "w_in": f["L0_attn_W_in"], "w_out": w_out, "rope": rope,
        "iota32": np.broadcast_to(np.arange(E0, dtype=np.float32), (P, E0)), "tri": tri,
        "tokid": np.arange(T, dtype=np.uint32).reshape(TILES, P).T, "norm_w": f["L0_ffn_norm_w"],
        "gate_wT": turned("L0_ffn_gate_w"), "sgate": f["L0_ffn_shared_gate_w"], "sup": f["L0_ffn_shared_up_w"],
        "sdown": f["L0_ffn_shared_down_w"], "w13": f["L0_ffn_w13"], "w2": f["L0_ffn_w2"],
        "in_projT": turned("L1_attn_in_proj_w"), "x_projT": turned("L1_attn_x_proj_w"), "out_projT": turned("L1_attn_out_proj_w"),
        "conv_w": f["L1_attn_conv_w"].reshape(DI, KC), "conv_b": by_row("L1_attn_conv_b"), "dt_w": by_row("L1_attn_dt_w"),
        "dt_b": by_row("L1_attn_dt_b"), "D_param": by_row("L1_attn_D_param"), "A_log": f["L1_attn_A_log"], "selbc": selbc,
        "wq1": f["L1_xattn_Wq"], "wk1": f["L1_xattn_Wk"], "wv1": f["L1_xattn_Wv"], "wo1": f["L1_xattn_Wo"],
        "wg": flat("L1_ffn_Wg", "L1_ffn_Sg"), "wu": flat("L1_ffn_Wu", "L1_ffn_Su"),
        "wd": wd.reshape(FB, P, D).transpose(1, 0, 2), "wr": np.concatenate([f["L1_ffn_Wr"], f["L1_ffn_Wsg"]], axis=1),
        "sel27": sel27,
    }
    arrays = {k: np.ascontiguousarray(v) for k, v in arrays.items()}

    def emitted(known):
        nc = bacc.Bacc("TRN2", target_bir_lowering=False, num_devices=1)
        ins = {k: nc.dram_tensor("in_" + k, v.shape, mybir.dt.from_np(v.dtype), kind="ExternalInput").ap() for k, v in arrays.items()}
        out = nc.dram_tensor("out", (B, S, D), F32, kind="ExternalOutput").ap()
        return nc, decoder(nc, ins, out, known)

    _, steps = emitted(None)
    nc, again = emitted(steps)
    assert again == steps
    res = run_bass_kernel_spmd(nc, [{"in_" + k: v for k, v in arrays.items()}], core_ids=[0])
    return res.results[0]["out"]
```

```python
from contextlib import ExitStack

import numpy as np

import concourse.bass as bass
from concourse import mybir

F32 = mybir.dt.float32
BF16 = mybir.dt.bfloat16
U32 = mybir.dt.uint32
U8 = mybir.dt.uint8
ALU = mybir.AluOpType
ACT = mybir.ActivationFunctionType
AX = mybir.AxisListType
EXP_LN = "natural_log_exp_and_others"

P = 128
B, S, D = 4, 256, 256
T = B * S
TILES = T // P
TPB = S // P
DB = D // P
C = 128
LN_EPS = 1e-5
H0, DH0 = 16, D // 16
E0, K0, I0 = 32, 4, 128
CAP = 2 * T * K0 // E0
ROT = DH0 // 2
DI, NST, KC = 512, 16, 4
IB = DI // P
HALF = 512
NHALF = T // HALF
BPH = HALF // S
GT = HALF // P
H1, HKV = 16, 8
GR = H1 // HKV
E1, F1, FS = 8, 176, 704
FT = E1 * F1 + FS
FB = -(-FT // P)
NEG = -1e30


PIECES = 6
KA = PIECES * DH0
STACK_COPIES = ((0, 3, 0, 2), (0, 5, 0, 1), (1, 4, 0, 2), (1, 2, 0, 1))
UPT0 = H0 // 2
UNITS0 = TILES * UPT0
LAST0 = UNITS0 + 5


def unit0(n):
    return n // UPT0 // TPB, n // UPT0 % TPB, n % UPT0


def side_work0():
    items = {}
    for b in range(B):
        def turns(tt):
            return [("turn", b, tt, w, half) for w in (1, 0) for half in range(2)]

        def cuts(tt):
            return [("cut", b, tt, stage) for stage in range(3)]

        if b == 0:
            items[-1] = [("rows", b), ("qk", b, 0), *cuts(0), ("v", b, 0), ("v", b, 1), ("qk", b, 1), *cuts(1), *turns(0), *turns(1)]
            continue
        first = (b - 1) * TPB * UPT0
        prep = {0: [("rows", b)], 1: [("qk", b, 0)], 2: [("v", b, 0)], 3: [("v", b, 1)], 4: [("qk", b, 1)]}
        for n, item in enumerate(cuts(0) + cuts(1)):
            prep.setdefault(2 + n, []).append(item)
        for n, item in enumerate(turns(0) + turns(1)):
            prep.setdefault(7 + n, []).append(item)
        for n, some in prep.items():
            items.setdefault(first + n, []).extend(some)
    for t in range(TILES):
        step = 3 if t == TILES - 1 else (7, 5)[t % TPB]
        items.setdefault(UPT0 * t + UPT0 + step, []).append(("out", t // TPB, t % TPB))
    return items


def side_bank0(kind, b, w):
    if b or kind in ("rows", "out"):
        return 7
    if kind in ("qk", "v"):
        return w[0] + (2 if kind == "v" else 0)
    tt, qk, half = w
    return ((4, 5, 2, 3), (7, 0, 4, 5))[tt][2 * (1 - qk) + half]


def map_work():
    items = {}
    for i in range(2):
        items.setdefault(i, []).append(("context", i))
    for i in range(4):
        items.setdefault(2 + i, []).append(("qk", i))
    for t in range(TILES):
        for n, kind in ((0, "energy"), (2, "scale"), (3, "turn")):
            items.setdefault(6 + 4 * t + n, []).append((kind, t))
    return items


UPB = HKV * TPB
UNITS = B * UPB
LAST_STEP = UNITS + 3 + TPB


def unit(n):
    return n // UPB, n // TPB % HKV, n % TPB


def side_work():
    items = {}

    def put(step, *item):
        items.setdefault(max(step, -1), []).append(item)

    for b in range(B):
        u0 = b * UPB
        first = u0 - UPB + 2 if b else -1
        if b:
            put(first, "rows", b)
        for i in range(4):
            put(first + 1 + i if b else -1, "keys", b, i)
            put(first + 5 + i if b else -1, "values", b, i)
        if b == 0:
            put(first, "rows", b)
        for h in range(HKV):
            put(u0 + TPB * h - 3, "queries", b, h)
        for q in range(TPB):
            put(u0 + UPB + 3 + q, "output", b, q)
    return items


def side_bank(kind, b, w):
    if b == 0 and kind in ("keys", "values"):
        return w[0] if kind == "keys" else 6 + w[0] % 2
    if b == 0 and (kind == "rows" or (kind == "queries" and w[0] == 0)):
        return 4 if kind == "rows" else 5
    return 7 if kind in ("queries", "output") else 2


def ffn_ahead():
    return {0: [("rows", BPH)], 1: [("rows", BPH + 1)], 2: [("logits", 1)], 6: [("coefficients", 1)]}


def mamba_ahead():
    items = [("rows", k) for k in range(DB)] + [("inner", m) for m in range(IB)]
    return {2 + 2 * i: [item] for i, item in enumerate(items)}


class Steps:

    def __init__(self, engine, book):
        self.engine, self.book, self.n = engine, book, 0

    def __call__(self, instruction, *step):
        self.n += 1
        if step:
            self.book[(self.engine, *step)] = self.n
        return instruction


def decoder(nc, ins, out, known):
    book = {}

    def at(*step):
        return known[step] if known is not None else 1

    ctx = ExitStack()
    with ctx:
        def sb(name, shape, dt=F32):
            return ctx.enter_context(nc.sbuf_tensor(name, shape, dt))

        def sem(name):
            return ctx.enter_context(nc.semaphore(name))

        X = sb("X", [P, TILES, D])
        XS = sb("XS", [P, 2 * TPB, D])
        XN = sb("XN", [P, TPB, D])
        stats = sb("stats", [P, TILES, 6])
        mv = sb("mv", [P, TILES, 2])
        lnv = sb("lnv", [P, 2, TILES])
        rstd = sb("rstd", [P, 2, TILES])
        ident = sb("ident", [P, P])
        lnw = sb("lnw", [P, 4, DB])
        ctxT = sb("ctxT", [P, T])
        iota_e = sb("iota_e", [P, E0])
        iota32 = iota_e[:, :]
        attT = sb("attT", [P, B, 2, S])

        def arena(name, size):
            whole = sb(name, [P, size])
            used = {}

            def phase(tag, after=None):
                used[tag] = used[after] if after else 0

                def take(shape, dt=F32):
                    n = int(np.prod(shape))
                    words = n if dt in (F32, U32) else -(-n // (2 if dt == BF16 else 4))
                    a = used[tag]
                    used[tag] += words
                    assert used[tag] <= size, (name, tag, used[tag])
                    v = whole[:, a:a + words]
                    if dt != F32:
                        v = v.bitcast(dt)
                    if len(shape) == 1:
                        return v
                    names = "abcd"[:len(shape)]
                    return v.rearrange(f"p ({' '.join(names)}) -> p {' '.join(names)}",
                                       **dict(zip(names, shape)))
                return take
            return phase

        ping, pong = arena("ping", 26430), arena("pong", 19856)

        take = ping("A")
        w_in, w_out = take([DB, 3 * D]), take([4, D])
        rope = take([TPB, 2, 2, ROT])
        xTa = take([2, DB, S])
        t1, t2 = take([2, H0, ROT]), take([2, H0, ROT])
        R = take([2, H0, DH0])
        stack = take([TPB, 2 * H0 * KA], BF16).rearrange("p t (w h d) -> p t w h d", w=2, h=H0)
        QT = take([2, 2 * H0 * S], BF16).rearrange("p b (w h s) -> p b w h s", w=2, h=H0)
        Va = take([2, TPB, H0 * 32]).rearrange("p b t (h d) -> p b t h d", h=H0)
        Pa = take([3, 2, S])
        PTa = take([2, 2, 2, P])
        mxa, rsa, ria = take([3, 2]), take([3, 2]), take([3, 2])
        CTa = take([4, P])
        identb = take([P], BF16)
        wq0, wk0, bqk = take([P]), take([P]), take([2])
        cx = take([TILES, C])
        q0, k0 = take([T]), take([T])
        en = take([S])
        m0, s0 = take([TILES]), take([TILES])
        xTb = take([2, DB, S])
        XSb = take([TPB, D])

        take = pong("C")
        nwb = take([D])
        gw = take([DB, E0])
        sgu, sdn = take([DB, 2 * I0]), take([D])
        NW = 6
        NY = 4
        w13, w2 = take([NW, DB, 2 * I0]), take([NW, D])
        hT = take([DB, T])
        tokid = take([TILES], U32)
        tri, ones = take([P], BF16), take([P], BF16)
        top8, idx8 = take([TILES, 8]), take([TILES, 8], U32)
        negm, ex4, sm4 = take([TILES]), take([TILES, K0]), take([TILES])
        w4 = take([TILES, K0])
        idf = take([TPB * K0])
        oh, ohp = take([TPB, K0, E0]), take([TPB, K0, E0])
        sel_tile = take([TILES, E0], BF16)
        posk, over, base = take([TPB * K0]), take([TPB * K0]), take([TPB * K0])
        rowf, slotf = take([TPB * K0]), take([TPB * K0])
        row, slot = take([TILES, K0], U32), take([TILES, K0], U32)
        tab, tabf = take([P], U32), take([P])
        slot_tok = take([2 * E0], U32)
        G = take([4, 2, D])
        XTc = take([2, DB, CAP])
        sg, ac = take([2, CAP]), take([2, CAP])
        EO = take([2, 2, D])
        Y = take([NY, K0, D])
        sgs, acs = take([HALF]), take([HALF])
        zero1 = take([64], U32)

        take = ping("D")
        wip, wxp, wop = take([DB, 2 * DI]), take([IB, 33]), take([IB, D])
        cw, cb, dtw, dtb, dpar, alog, Aneg = (take([IB, KC]), take([IB]), take([IB]), take([IB]), take([IB]),
                                              take([IB, NST]), take([IB, NST]))
        selbc = take([2 * NST * P], BF16).rearrange("p (n m) -> p n m", m=P)
        xTd = take([DB, HALF])
        xi = take([IB, BPH, S + KC - 1])
        us = take([2, IB, HALF])
        sz, dt = take([IB, HALF]), take([IB, HALF])
        xs3f, xs3, xs3m = take([HALF]), take([HALF], BF16), take([HALF], BF16)
        wdt = take([IB, P])
        NB = 4
        dA = take([2, IB, HALF])
        NHB = 4
        hb_ = take([2, IB, HALF])
        e1 = dA[:, 1]
        a1 = dA[:, 0]

        take = pong("E")
        wq1, wk1, wv1, wo1 = take([DB, H1 * P]), take([HKV * P]), take([HKV * P]), take([H1, D])
        vfl, mflag, maskf = take([B, S], U8), take([B]), take([B, S])
        far = pong("D", after="E")
        hb_far = far([2, IB, HALF])
        Bb = far([NB, HALF])
        dtu = far([IB, HALF])
        xTe = take([2, DB, S])
        QE = take([3, GR, S])
        Pe = take([3, GR, S])
        mxe, rse, rie = take([3, GR]), take([3, GR]), take([3, GR])
        V1 = take([2, 2, HKV * P])

        def hbuf(s):
            return (hb_ if s % NHB < 2 else hb_far)[:, s % 2]

        take = ping("F")
        wg, wu, wd = take([DB, FT]), take([DB, FT]), take([FB, D])
        wr = take([DB, E1 + 1])
        sel27 = take([FB * P], BF16)
        kT = take([2, HKV, S])
        PTe = take([2, GR, 2, P])
        OT = take([TPB, H1, P])
        take = pong("F")
        xTf = take([NHALF, DB, HALF])
        lg, pr, sp1, rp = take([TILES, E1 + 1]), take([TILES, E1]), take([TILES]), take([TILES])
        np8, tp8, ti8, tif = take([TILES]), take([TILES, 8]), take([TILES, 8], U32), take([TILES, 2])
        cc, c2 = take([TILES, E1 + 1]), take([TILES, E1])
        chb, cmb = take([GT, E1 + 1], BF16), take([GT, E1 + 1], BF16)
        c27 = take([TILES, 27])
        r1c = take([GT, E1 + 1])
        cT = take([T], BF16)
        iota8 = iota_e[:, 0:E1]
        sgf, tf, acf = take([2, HALF]), take([2, HALF]), take([3, HALF])

        PS = ctx.enter_context(nc.psum_tensor("PS", [P, 8, 512], F32))

        def bank(i, n=1):
            return PS[:, i:i + n, :]

        h_dram = nc.dram_tensor("h_dram", (T, D), F32, kind="Internal").ap()
        eo_dram = nc.dram_tensor("eo_dram", (E0 * CAP, D), F32, kind="Internal").ap()
        slots_dram = nc.dram_tensor("slots_dram", (E0 * CAP, 1), U32, kind="Internal").ap()

        pe_done, act_done = sem("pe_done"), sem("act_done")
        dve_done, pool_done = sem("dve_done"), sem("pool_done")
        PEs, ACs, VEs, POs = Steps("pe", book), Steps("act", book), Steps("dve", book), Steps("pool", book)
        x_in = [sem(f"x_in{b}") for b in range(B)]
        norm_in, rope_in = sem("norm_in"), sem("rope_in")
        ctx_in, attn_w_in, xattn_w_in = sem("ctx_in"), sem("attn_w_in"), sem("xattn_w_in")
        moe_w_in, const_in, mamba_w_in, xattn1_w_in = sem("moe_w_in"), sem("const_in"), sem("mamba_w_in"), sem("xattn1_w_in")
        ffn1_w_in = sem("ffn1_w_in")
        expert_in = [sem(f"expert_in{i}") for i in range(NW)]
        h_stored = [sem(f"h_stored{i}") for i in range(2 * TPB)]
        table_clear, scattered, table_in = sem("table_clear"), sem("scattered"), sem("table_in")
        gathered = [sem(f"gathered{i}") for i in range(4)]
        eo_stored = [sem(f"eo_stored{i}") for i in range(2)]
        y_in = [sem(f"y_in{i}") for i in range(NY)]
        out_stored = sem("out_stored")

        N_NORM, N_CONST, N_ATTN, N_XATTN, N_MOE, N_MAMBA, N_XATTN1, N_FFN1 = 2, 4, 1, 4, 4, 10, 5, 5

        ahead, router = mamba_ahead(), ffn_ahead()
        block = ctx.enter_context(nc.Block())

        @block.sync
        def _(sp):
            xv = ins["x"].rearrange("b (t p) d -> p (b t) d", p=P)
            sp.dma_start(X[:, 0:TPB, :], xv[:, 0:TPB, :]).then_inc(x_in[0], 16)
            sp.dma_start(ident[:, :], ins["ident"]).then_inc(norm_in, 16)
            sp.dma_start(lnw[:, :, :], ins["lnw"]).then_inc(norm_in, 16)
            sp.dma_start(w_in, ins["w_in"].rearrange("(k p) n -> p k n", p=P)).then_inc(attn_w_in, 16)
            sp.dma_start(rope, ins["rope"]).then_inc(rope_in, 16)
            for b in range(1, B):
                sp.dma_start(X[:, TPB * b:TPB * b + TPB, :], xv[:, TPB * b:TPB * b + TPB, :]).then_inc(x_in[b], 16)
            sp.dma_start(cx, ins["ctx"].rearrange("b (t p) d -> p (b t) d", p=P)).then_inc(ctx_in, 16)
            sp.dma_start(wq0, ins["wq0T"]).then_inc(xattn_w_in, 16)
            sp.dma_start(wk0, ins["wk0T"]).then_inc(xattn_w_in, 16)
            sp.dma_start(bqk, ins["bqk"]).then_inc(xattn_w_in, 16)
            sp.dma_start(w_out, ins["w_out"]).then_inc(xattn_w_in, 16)
            sp.dma_start(iota32, ins["iota32"]).then_inc(const_in, 16)
            sp.dma_start(tri, ins["tri"]).then_inc(const_in, 16)
            sp.dma_start(tokid, ins["tokid"]).then_inc(const_in, 16)
            sp.dma_start(nwb, ins["norm_w"].partition_broadcast(P)).then_inc(const_in, 16)
            sp.dma_start(gw, ins["gate_wT"].rearrange("(k p) n -> p k n", p=P)).then_inc(moe_w_in, 16)
            sp.dma_start(sgu[:, :, 0:I0], ins["sgate"].rearrange("(k p) n -> p k n", p=P)).then_inc(moe_w_in, 16)
            sp.dma_start(sgu[:, :, I0:2 * I0], ins["sup"].rearrange("(k p) n -> p k n", p=P)).then_inc(moe_w_in, 16)
            sp.dma_start(sdn, ins["sdown"]).then_inc(moe_w_in, 16)
            sp.wait_ge(pool_done, at("pool", "zeros"))
            sp.dma_start(slots_dram.rearrange("(p n) o -> p (n o)", p=P), zero1).then_inc(table_clear, 16)

            def load_expert(e):
                sp.dma_start(w13[:, e % NW], ins["w13"][e].rearrange("(k p) n -> p k n", p=P)).then_inc(expert_in[e % NW], 16)
                sp.dma_start(w2[:, e % NW], ins["w2"][e]).then_inc(expert_in[e % NW], 16)

            for e in range(NW):
                load_expert(e)
            for t in range(TILES):
                sp.wait_ge(dve_done, at("dve", "C.h", t))
                sp.dma_start(h_dram[t * P:(t + 1) * P, :], XS[:, t % (2 * TPB), :]).then_inc(h_stored[t % 4], 16)
            sp.wait_ge(scattered, 16 * TILES * K0)
            sp.dma_start(tab[0:2 * E0, :], slots_dram.rearrange("(j p) o -> j (p o)", p=P)).then_inc(table_in, 16)
            sp.wait_ge(pe_done, at("pe", "B.end"))
            sp.wait_ge(act_done, at("act", "B.end"))
            sp.wait_ge(dve_done, at("dve", "B.end"))
            sp.dma_start(wip, ins["in_projT"].rearrange("(k p) n -> p k n", p=P)).then_inc(mamba_w_in, 16)
            for dst, name in ((wxp, "x_projT"), (wop, "out_projT"), (cw, "conv_w"), (cb, "conv_b"), (dtw, "dt_w"),
                              (dtb, "dt_b"), (dpar, "D_param"), (alog, "A_log")):
                src = ins[name]
                if src.shape[0] == DI:
                    src = src.rearrange("(k p) n -> p k n", p=P)
                sp.dma_start(dst, src).then_inc(mamba_w_in, 16)
            sp.dma_start(selbc[0:96], ins["selbc"]).then_inc(mamba_w_in, 16)
            for e in range(E0):
                sp.wait_ge(act_done, at("act", "C.eo", e))
                sp.dma_start(eo_dram[e * CAP:(e + 1) * CAP, :].rearrange("(s p) d -> p s d", p=P),
                             EO[:, e % 2]).then_inc(eo_stored[e % 2], 16)
                if e + NW < E0:
                    sp.wait_ge(pe_done, at("pe", "C.down", e))
                    load_expert(e + NW)
            sp.wait_ge(dve_done, at("dve", "C.end"))
            for i in range(2):
                sp.wait_ge(eo_stored[i], 16 * E0 // 2)
            sp.dma_start(wq1, ins["wq1"].rearrange("(k p) n -> p k n", p=P)).then_inc(xattn1_w_in, 16)
            sp.dma_start(wk1, ins["wk1"]).then_inc(xattn1_w_in, 16)
            sp.dma_start(wv1, ins["wv1"]).then_inc(xattn1_w_in, 16)
            sp.dma_start(wo1, ins["wo1"].rearrange("(h p) n -> p h n", p=P)).then_inc(xattn1_w_in, 16)
            sp.dma_start(vfl, ins["mask"].partition_broadcast(P)).then_inc(xattn1_w_in, 16)
            sp.wait_ge(pe_done, at("pe", "D.end"))
            sp.wait_ge(act_done, at("act", "D.end"))
            sp.wait_ge(dve_done, at("dve", "D.end"))
            sp.wait_ge(pool_done, at("pool", "D.end"))
            sp.dma_start(wg, ins["wg"].rearrange("(k p) n -> p k n", p=P)).then_inc(ffn1_w_in, 16)
            sp.dma_start(wu, ins["wu"].rearrange("(k p) n -> p k n", p=P)).then_inc(ffn1_w_in, 16)
            sp.dma_start(wd, ins["wd"]).then_inc(ffn1_w_in, 16)
            sp.dma_start(wr, ins["wr"].rearrange("(k p) n -> p k n", p=P)).then_inc(ffn1_w_in, 16)
            sp.dma_start(sel27[0:27], ins["sel27"]).then_inc(ffn1_w_in, 16)
            ov = out.rearrange("b (t p) d -> p (b t) d", p=P)
            for t in range(0, TILES, 4):
                sp.wait_ge(dve_done, at("dve", "F.x", t + 3))
                sp.dma_start(ov[:, t:t + 4, :], X[:, t:t + 4, :]).then_inc(out_stored, 16)
            sp.wait_ge(out_stored, 16 * 2)

        @block.gpsimd
        def _(pool):
            POs(nc.gpsimd.memset(zero1, 0).then_inc(pool_done, 1), "zeros")
            POs(nc.gpsimd.memset(Va, 0.0).then_inc(pool_done, 1), "A.V")
            POs(nc.gpsimd.memset(ones, 1.0).then_inc(pool_done, 1), "ones")

            for b in range(1, B):
                for tt in range(TPB):
                    pool.wait_ge(dve_done, at("dve", "A.pieces", b, tt))
                    st = stack[:, tt]
                    for w, to, frm, n in STACK_COPIES:
                        POs(nc.gpsimd.tensor_copy(st[:, w, :, to * DH0:(to + n) * DH0], st[:, w, :, frm * DH0:(frm + n) * DH0])
                            .then_inc(pool_done, 1), "A.stack", b, tt)

            pool.wait_ge(table_clear, 16)
            pool.wait_ge(const_in, 16 * N_CONST)
            for t in range(TILES):
                pool.wait_ge(dve_done, at("dve", "C.slot", t // TPB))
                for k in range(K0):
                    nc.gpsimd.indirect_dma_start(
                        out=slots_dram, out_offset=bass.IndirectOffsetOnAxis(ap=slot[:, t, k:k + 1], axis=0),
                        in_=tokid[:, t:t + 1], in_offset=None,
                        bounds_check=E0 * CAP - 1, oob_is_err=False).then_inc(scattered, 16)
            for i in range(4):
                pool.wait_ge(h_stored[i], 16 * TILES // 4)
            pool.wait_ge(dve_done, at("dve", "C.slot_tok"))
            for j in range(2 * E0):
                if j >= 8:
                    pool.wait_ge(pe_done, at("pe", "C.xT", j // 2 - 4))
                nc.gpsimd.indirect_dma_start(
                    out=G[:, (j // 2) % 4, j % 2, :], out_offset=None, in_=h_dram,
                    in_offset=bass.IndirectOffsetOnAxis(ap=slot_tok[:, j:j + 1], axis=0),
                    bounds_check=T - 1, oob_is_err=False).then_inc(gathered[(j // 2) % 4], 16)
            pool.wait_ge(pe_done, at("pe", "B.end"))
            pool.wait_ge(dve_done, at("dve", "B.end"))
            pool.wait_ge(act_done, at("act", "B.end"))
            POs(nc.gpsimd.memset(xi[:, :, :, 0:KC - 1], 0.0).then_inc(pool_done, 1), "D.pad")
            for i in range(2):
                pool.wait_ge(eo_stored[i], 16 * E0 // 2)
            for t in range(TILES):
                if t >= NY:
                    pool.wait_ge(dve_done, at("dve", "C.comb", t - NY))
                for k in range(K0):
                    nc.gpsimd.indirect_dma_start(
                        out=Y[:, t % NY, k, :], out_offset=None, in_=eo_dram,
                        in_offset=bass.IndirectOffsetOnAxis(ap=row[:, t, k:k + 1], axis=0),
                        bounds_check=E0 * CAP - 1, oob_is_err=False).then_inc(y_in[t % NY], 16)

            for hf in range(NHALF):
                pool.wait_ge(dve_done, at("dve", "D.dtu", hf, IB - 1))
                for r in range(2):
                    POs(nc.gpsimd.memset(dA[:, r, :, 0:HALF:S], 0.0).then_inc(pool_done, 1), "D.zero", hf, r)
                for n in range(NST):
                    s = hf * NST + n
                    pool.wait_ge(act_done, at("act", "D.Bb", s))
                    if s >= NHB:
                        pool.wait_ge(pe_done, at("pe", "D.sum", s - NHB))
                    bn = Bb[:, s % NB, :]
                    POs(nc.gpsimd.tensor_tensor(
                        hbuf(s), dtu, bn.rearrange("p (o n) -> p o n", o=1).broadcast_to((P, IB, HALF)),
                        ALU.mult).then_inc(pool_done, 1), "D.Bu", s)
            book[("pool", "D.end")] = POs.n

        @block.scalar
        def _(act):
            a = nc.scalar

            def ln(name, b, second):
                act.wait_ge(dve_done, at("dve", name + ".mv", b))
                t0 = TPB * b
                var = mv[:, t0:t0 + TPB, 1]
                ACs(a.activation(lnv[:, 0, t0:t0 + TPB], var, ACT.Ln, bias=LN_EPS).then_inc(act_done, 1))
                if second:
                    ACs(a.activation(lnv[:, 1, t0:t0 + TPB], var, ACT.Ln, bias=LN_EPS * second, scale=1.0 + second).then_inc(act_done, 1))
                act.wait_ge(act_done, ACs.n)
                k = 2 if second else 1
                ACs(a.activation(rstd[:, 0:k, t0:t0 + TPB], lnv[:, 0:k, t0:t0 + TPB], ACT.Exp, scale=-0.5).then_inc(act_done, 1),
                    name + ".rstd", b)

            a.preload_act_table_set(EXP_LN)
            side, maps = side_work0(), map_work()
            for b in range(B):
                ln("A", b, LN_EPS)
            act.wait_ge(norm_in, 16 * N_NORM)
            act.wait_ge(xattn_w_in, 16 * N_XATTN)
            for i in range(-1, LAST0 + 1):
                if 0 <= i < UNITS0:
                    act.wait_ge(dve_done, at("dve", "A.max", i))
                    if i >= 3:
                        act.wait_ge(pe_done, at("pe", "A.PT", i - 3))
                    for j in range(2):
                        ACs(a.activation(Pa[:, i % 3, j, :], bank(i % 3)[:, 0, j * S:j * S + S], ACT.Exp, bias=mxa[:, i % 3, j:j + 1],
                                         accum_out=rsa[:, i % 3, j:j + 1]).then_inc(act_done, 1), "A.P", i)
                n = i - 2
                if 0 <= n < UNITS0:
                    act.wait_ge(pe_done, at("pe", "A.PT", n))
                    if n >= 2:
                        act.wait_ge(pe_done, at("pe", "A.av", n - 2))
                    ACs(a.activation(PTa[:, n % 2], bank(3 + n % 2)[:, 0, :].rearrange("p (i k q) -> p i k q", i=2, k=2), ACT.Copy)
                        .then_inc(act_done, 1), "A.PT", n)
                n = i - 3
                if 0 <= n < UNITS0 and n % UPT0 == UPT0 - 1:
                    t = n // UPT0
                    act.wait_ge(pe_done, at("pe", "A.av", n))
                    if t:
                        act.wait_ge(pe_done, at("pe", "A.out", (t - 1) // TPB, (t - 1) % TPB))
                    ACs(a.activation(CTa, bank(5)[:, 0, :].rearrange("p (g q) -> p g q", g=4), ACT.Copy).then_inc(act_done, 1), "A.cT", t)
                for kind, b, *w in side.get(i, []):
                    n = side_bank0(kind, b, w) if kind != "cut" else None
                    if kind == "rows":
                        act.wait_ge(pe_done, at("pe", "A.rows", b))
                        if b >= 2:
                            act.wait_ge(pe_done, at("pe", "A.v", b - 2, TPB - 1))
                        for k in range(DB):
                            ACs(a.activation(xTa[:, b % 2, k, :], bank(n)[:, 0, k * S:k * S + S], ACT.Identity, scale=lnw[:, 0, k:k + 1],
                                             bias=lnw[:, 1, k:k + 1]).then_inc(act_done, 1), "A.rows", b)
                    elif kind == "v":
                        act.wait_ge(pe_done, at("pe", "A.v", b, w[0]))
                        act.wait_ge(pool_done, at("pool", "A.V"))
                        if b >= 2 and w[0] == 0:
                            act.wait_ge(pe_done, at("pe", "A.av", (b - 1) * TPB * UPT0 - 1))
                        ACs(a.activation(Va[:, b % 2, w[0], :, 0:DH0], bank(n)[:, 0, 0:D].rearrange("p (h d) -> p h d", h=H0), ACT.Copy)
                            .then_inc(act_done, 1), "A.v", b, w[0])
                    elif kind == "turn":
                        tt, qk, half = w
                        act.wait_ge(pe_done, at("pe", "A.turn", b, *w))
                        if b >= 2 and (tt, qk, half) == (0, 1, 0):
                            act.wait_ge(pe_done, at("pe", "A.S", (b - 1) * TPB * UPT0 - 1))
                        ACs(a.activation(QT[0:KA, b % 2, qk, 8 * half:8 * half + 8, tt * P:tt * P + P],
                                         bank(n)[0:KA, 0, :].bitcast(BF16).rearrange("p (h s) -> p h s", h=8), ACT.Copy)
                            .then_inc(act_done, 1), "A.turn", b, *w)
                for kind, t in maps.get(i, []):
                    if kind == "context":
                        act.wait_ge(pe_done, at("pe", "context", t))
                        ACs(a.activation(ctxT[:, 512 * t:512 * t + 512], bank(6)[:, 0, :], ACT.Copy).then_inc(act_done, 1), "context", t)
                    elif kind == "qk":
                        act.wait_ge(pe_done, at("pe", "map.qk", t))
                        ACs(a.activation((q0, k0)[t // 2][:, 512 * (t % 2):512 * (t % 2) + 512], bank(6)[:, 0, :], ACT.Identity,
                                         bias=bqk[:, t // 2:t // 2 + 1]).then_inc(act_done, 1), "map.qk", t)
                    elif kind == "energy":
                        act.wait_ge(dve_done, at("dve", "m0", t))
                        if t:
                            act.wait_ge(pe_done, at("pe", "map", t - 1))
                        ACs(a.activation(en, bank(6)[:, 0, 0:S], ACT.Exp, bias=m0[:, t:t + 1], accum_out=s0[:, t:t + 1])
                            .then_inc(act_done, 1), "en", t)
                    elif kind == "turn":
                        act.wait_ge(pe_done, at("pe", "map", t))
                        ACs(a.activation(attT[:, t // 2, :, (t % 2) * P:(t % 2) * P + P],
                                         bank(6)[:, 0, 0:2 * P].rearrange("p (m n) -> p m n", m=2), ACT.Copy).then_inc(act_done, 1), "map", t)

            def rows_b(b):
                ln("B", b, None)
                act.wait_ge(pe_done, at("pe", "B.xT", b))
                if b >= 2:
                    act.wait_ge(pe_done, at("pe", "B.out", b - 2, 1))
                ACs(a.activation(xTb[:, b % 2], bank(6)[:, 0, :].rearrange("p (k n) -> p k n", k=DB), ACT.Copy).then_inc(act_done, 1), "B.xT", b)

            rows_b(0)
            for b in range(B):
                ln("C", b, 1e-6)
                for t in range(TPB * b, TPB * b + TPB):
                    act.wait_ge(pe_done, at("pe", "C.hT", t))
                    ACs(a.activation(hT[:, :, t * P:t * P + P], bank(t % 2)[:, 0, 0:2 * P].rearrange("p (k n) -> p k n", k=DB),
                                     ACT.Copy).then_inc(act_done, 1), "C.hT", t)
                if b + 1 < B:
                    rows_b(b + 1)
                    if b + 2 == B:
                        book[("act", "B.end")] = ACs.n
                act.wait_ge(dve_done, at("dve", "C.top", b))
                for t in range(TPB * b, TPB * b + TPB):
                    ACs(a.activation(ex4[:, t, :], top8[:, t, 0:K0], ACT.Exp, bias=negm[:, t:t + 1],
                                     accum_out=sm4[:, t:t + 1]).then_inc(act_done, 1), "C.ex4", t)
            for hf in range(NHALF):
                act.wait_ge(pe_done, at("pe", "C.sgu", hf))
                if hf:
                    act.wait_ge(dve_done, at("dve", "C.sact", hf - 1))
                ACs(a.activation(sgs, bank(4)[:, 0, :], ACT.Silu).then_inc(act_done, 1), "C.sgs", hf)
            for e in range(E0):
                act.wait_ge(pe_done, at("pe", "C.gu", e))
                if e >= 2:
                    act.wait_ge(dve_done, at("dve", "C.act", e - 2))
                ACs(a.activation(sg[:, e % 2, :], bank(2 + e % 2)[:, 0, 0:CAP], ACT.Silu).then_inc(act_done, 1), "C.sg", e)
                act.wait_ge(pe_done, at("pe", "C.down", e))
                if e >= 2:
                    act.wait_ge(eo_stored[e % 2], 16 * (e // 2))
                ACs(a.activation(EO[:, e % 2], bank(4 + e % 2)[:, 0, :].rearrange("p (s d) -> p s d", s=2), ACT.Copy).then_inc(act_done, 1), "C.eo", e)

            a.preload_act_table_set(EXP_LN)
            act.wait_ge(mamba_w_in, 16 * N_MAMBA)
            ACs(a.activation(Aneg, alog, ACT.Exp).then_inc(act_done, 1), "D.A")
            for b in range(BPH):
                ln("D", b, LN_EPS)

            def d_rows(hf, k):
                act.wait_ge(pe_done, at("pe", "D.xT", hf, k))
                if hf:
                    act.wait_ge(pe_done, at("pe", "D.z", hf - 1, IB - 1))
                ACs(a.activation(xTd[:, k, :], bank(7 if hf else 6 + k)[:, 0, :], ACT.Copy, scale=lnw[:, 3, k:k + 1]).then_inc(act_done, 1),
                    "D.xT", hf, k)

            def d_inner(hf, m):
                act.wait_ge(pe_done, at("pe", "D.xi", hf, m))
                act.wait_ge(pool_done, at("pool", "D.pad"))
                if hf:
                    act.wait_ge(dve_done, at("dve", "D.conv", hf - 1, m))
                src = bank(7 if hf else m)[:, 0, :]
                ACs(a.activation(xi[:, m, :, KC - 1:], src.rearrange("p (b s) -> p b s", b=BPH), ACT.Copy).then_inc(act_done, 1))
                ACs(a.activation(us[:, hf, m, :], src, ACT.Identity, bias=cb[:, m:m + 1], scale=cw[:, m, KC - 1:KC]).then_inc(act_done, 1),
                    "D.xi", hf, m)

            for k in range(DB):
                d_rows(0, k)
            for m in range(IB):
                d_inner(0, m)
            for hf in range(NHALF):
                for m in range(IB):
                    act.wait_ge(dve_done, at("dve", "D.conv", hf, m))
                    ACs(a.activation(us[:, hf, m, :], us[:, hf, m, :], ACT.Silu).then_inc(act_done, 1), "D.u", hf, m)
                a.preload_act_table_set(EXP_LN)
                if hf == 0:
                    for b in range(BPH, B):
                        ln("D", b, LN_EPS)
                for m in range(IB):
                    act.wait_ge(dve_done, at("dve", "D.v", hf, m))
                    ACs(a.activation(a1[:, m, :], dt[:, m, :], ACT.Abs).then_inc(act_done, 1))
                    act.wait_ge(act_done, ACs.n)
                    ACs(a.activation(e1[:, m, :], a1[:, m, :], ACT.Exp, scale=-1.0).then_inc(act_done, 1))
                    act.wait_ge(act_done, ACs.n)
                    ACs(a.activation(e1[:, m, :], e1[:, m, :], ACT.Ln, bias=1.0).then_inc(act_done, 1), "D.sp", hf, m)

                def b_row(s):
                    act.wait_ge(pe_done, at("pe", "D.B", s))
                    if s >= NB:
                        act.wait_ge(pool_done, at("pool", "D.Bu", s - NB))
                    ACs(a.activation(Bb[:, s % NB, :], bank(6)[:, 0, :], ACT.Copy).then_inc(act_done, 1), "D.Bb", s)

                b_row(hf * NST)
                b_row(hf * NST + 1)
                for n in range(NST):
                    s = hf * NST + n
                    if n == 1:
                        act.wait_ge(dve_done, at("dve", "D.dtu", hf, IB - 1))
                    elif n >= 2:
                        act.wait_ge(dve_done, at("dve", "D.scan", s - 2))
                    for m in range(IB):
                        if n == 0:
                            act.wait_ge(dve_done, at("dve", "D.dtu", hf, m))
                        step = dA[:, s % 2, m, :].rearrange("p (b s) -> p b s", b=BPH)[:, :, 1:]
                        ACs(a.activation(step, dt[:, m, :].rearrange("p (b s) -> p b s", b=BPH)[:, :, 1:], ACT.Exp,
                                         scale=Aneg[:, m, n:n + 1]).then_inc(act_done, 1), "D.dA", s)
                    if n == 1:
                        if hf:
                            act.wait_ge(pe_done, at("pe", "D.out", hf - 1))
                        for m in range(IB):
                            act.wait_ge(pe_done, at("pe", "D.z", hf, m))
                            ACs(a.activation(sz[:, m, :], bank(m)[:, 0, :], ACT.Silu).then_inc(act_done, 1), "D.sz", hf, m)
                        a.preload_act_table_set(EXP_LN)
                    if n + 2 < NST:
                        b_row(s + 2)
                    if hf == 0:
                        for kind, i in ahead.get(n - 2, []):
                            (d_rows if kind == "rows" else d_inner)(1, i)
            book[("act", "D.end")] = ACs.n

            def f_rows(b, n):
                act.wait_ge(pe_done, at("pe", "F.xT", b))
                ACs(a.activation(xTf[:, b // BPH, :, (b % BPH) * S:(b % BPH) * S + S],
                                 bank(n)[:, 0, :].rearrange("p (k n) -> p k n", k=DB), ACT.Copy).then_inc(act_done, 1), "F.xT", b)

            def f_exp(g):
                act.wait_ge(dve_done, at("dve", "F.max", g))
                for t in range(GT * g, GT * g + GT):
                    ACs(a.activation(pr[:, t, :], lg[:, t, 0:E1], ACT.Exp, bias=np8[:, t:t + 1], accum_out=sp1[:, t:t + 1]).then_inc(act_done, 1))
                gate = lg[:, GT * g:GT * g + GT, E1:]
                ACs(a.activation(gate, gate, ACT.Exp, scale=-1.0).then_inc(act_done, 1), "F.pr", g)

            def f_turned(g, n):
                act.wait_ge(pe_done, at("pe", "F.cT", g))
                ACs(a.activation(cT[0:27, g * HALF:g * HALF + HALF], bank(n)[0:27, 0, :], ACT.Copy).then_inc(act_done, 1), "F.cT", g)

            side = side_work()
            for i in range(-1, LAST_STEP + 1):
                if i == UNITS + 3:
                    for b in range(BPH):
                        ln("F", b, None)
                    for b in range(BPH):
                        f_rows(b, b)
                elif i == UNITS + 4:
                    f_exp(0)
                if 0 <= i < UNITS:
                    act.wait_ge(dve_done, at("dve", "E.max", i))
                    for j in range(GR):
                        ACs(a.activation(Pe[:, i % 3, j, :], Pe[:, i % 3, j, :], ACT.Exp, bias=mxe[:, i % 3, j:j + 1],
                                         accum_out=rse[:, i % 3, j:j + 1]).then_inc(act_done, 1), "E.P", i)
                n = i - 2
                if 0 <= n < UNITS:
                    act.wait_ge(pe_done, at("pe", "E.PT", n))
                    if n >= 2:
                        act.wait_ge(pe_done, at("pe", "E.av", n - 2))
                    ACs(a.activation(PTe[:, n % 2], bank(3 + n % 2)[:, 0, :].rearrange("p (i k q) -> p i k q", i=GR, k=2), ACT.Copy)
                        .then_inc(act_done, 1), "E.PT", n)
                n = i - 3
                if 0 <= n < UNITS and n % 2 == 1:
                    b, h, _ = unit(n)
                    act.wait_ge(pe_done, at("pe", "E.av", n))
                    if b and h == 0:
                        act.wait_ge(pe_done, at("pe", "E.output", b - 1, TPB - 1))
                    ACs(a.activation(OT[:, :, GR * h:GR * h + GR, :], bank(5 + n // 2 % 2)[:, 0, :].rearrange("p (t g q) -> p t g q", t=TPB, g=GR),
                                     ACT.Copy).then_inc(act_done, 1), "E.OT", n // 2)
                for kind, b, *w in side.get(i, []):
                    src = bank(side_bank(kind, b, w))[:, 0, :]
                    if kind == "keys" and b == 0 and w[0] == 1:
                        for r in range(B):
                            ln("E", r, None)
                    if kind == "rows":
                        act.wait_ge(pe_done, at("pe", "E.rows", b))
                        if b >= 2:
                            act.wait_ge(pe_done, at("pe", "E.queries", b - 2, HKV - 1))
                        ACs(a.activation(xTe[:, b % 2], src.rearrange("p (k n) -> p k n", k=DB), ACT.Copy).then_inc(act_done, 1),
                            "E.rows", b)
                    elif kind == "keys":
                        act.wait_ge(pe_done, at("pe", "E.keys", b, w[0]))
                        if b >= 2 and w[0] == 0:
                            act.wait_ge(pe_done, at("pe", "E.S", (b - 1) * UPB - 1))
                        ACs(a.activation(kT[:, b % 2, 2 * w[0]:2 * w[0] + 2, :], src.rearrange("p (h s) -> p h s", h=2),
                                         ACT.Copy).then_inc(act_done, 1), "E.keys", b, w[0])
                    elif kind == "queries":
                        act.wait_ge(pe_done, at("pe", "E.queries", b, w[0]))
                        c = b * HKV + w[0]
                        if c >= 3:
                            act.wait_ge(pe_done, at("pe", "E.S", (c - 2) * TPB - 1))
                        ACs(a.activation(QE[:, c % 3], src.rearrange("p (h s) -> p h s", h=GR), ACT.Copy,
                                         scale=float(P) ** -0.5).then_inc(act_done, 1), "E.queries", b, w[0])
                    elif kind == "values" and b == 0:
                        act.wait_ge(pe_done, at("pe", "E.values", b, w[0]))
                        ACs(a.activation(V1[:, 0, w[0] // 2, 512 * (w[0] % 2):512 * (w[0] % 2) + 512], src, ACT.Copy).then_inc(act_done, 1),
                            "E.values", b, w[0])

            f_turned(0, 3)
            for b in range(BPH, B):
                ln("F", b, None)
            for hf in range(NHALF):
                for f in range(FB):
                    n = hf * FB + f
                    act.wait_ge(pe_done, at("pe", "F.gu", n))
                    if n >= 2:
                        act.wait_ge(dve_done, at("dve", "F.act", n - 2))
                    m = min(P, FT - f * P)
                    ACs(a.activation(sgf[0:m, n % 2, :], bank(n % 2)[0:m, 0, :], ACT.Silu).then_inc(act_done, 1), "F.sg", n)
                    for kind, i in router.get(n - 1, []):
                        if kind == "rows":
                            f_rows(i, 5)
                        elif kind == "coefficients":
                            f_turned(i, 5)
                    if n == 4:
                        f_exp(1)

        @block.vector
        def _(dve):
            v = nc.vector

            def ln(name, b, second, residual):
                t0 = TPB * b
                for t in range(t0, t0 + TPB):
                    VEs(v.bn_stats(stats[:, t, :], X[:, t, :]).then_inc(dve_done, 1))
                dve.wait_ge(dve_done, VEs.n)
                for t in range(t0, t0 + TPB):
                    VEs(v.bn_aggr(mv[:, t, :], stats[:, t, :]).then_inc(dve_done, 1), name + ".mv", b)

            def ln_apply(name, b, second, residual, free, rows=XS):
                t0 = TPB * b
                dve.wait_ge(act_done, at("act", name + ".rstd", b))
                dve.wait_ge(dve_done, VEs.n)
                free()
                for t in range(t0, t0 + TPB):
                    VEs(v.tensor_scalar(rows[:, t % rows.shape[1], :], X[:, t, :], mv[:, t, 0:1], rstd[:, 1 if second else 0, t:t + 1],
                                        ALU.subtract, ALU.mult).then_inc(dve_done, 1), name + ".xs", b)
                if residual:
                    ln_residual(name, b)

            def ln_residual(name, b):
                t0 = TPB * b
                for t in range(t0, t0 + TPB):
                    VEs(v.tensor_scalar(XN[:, t % TPB, :], X[:, t, :], mv[:, t, 0:1], rstd[:, 0, t:t + 1],
                                        ALU.subtract, ALU.mult).then_inc(dve_done, 1))
                dve.wait_ge(dve_done, VEs.n)
                for t in range(t0, t0 + TPB):
                    VEs(v.tensor_tensor(X[:, t, :], X[:, t, :], XN[:, t % TPB, :], ALU.add).then_inc(dve_done, 1), name + ".res", b)

            def add_to_x(t, psum, *step):
                VEs(v.tensor_tensor(X[:, t, :], X[:, t, :], psum, ALU.add).then_inc(dve_done, 1), *step)

            side, maps = side_work0(), map_work()
            dve.wait_ge(x_in[0], 16)
            ln("A", 0, True, True)

            def rows0(b):
                def free():
                    if b >= 2:
                        dve.wait_ge(pe_done, at("pe", "A.rows", b - 2))
                ln_apply("A", b, True, True, free)

            def rotate(b, tt):
                dve.wait_ge(pe_done, at("pe", "A.qk", b, tt))
                dve.wait_ge(dve_done, VEs.n)
                qk = bank(side_bank0("qk", b, (tt,)))[:, 0, :].rearrange("p (w h d) -> p w h d", w=2, h=H0)

                def table(i, a0, n):
                    return rope[:, tt, :, i, a0:ROT:ROT // n].rearrange("p w (o d) -> p w o d", o=1).broadcast_to((P, 2, H0, n))
                VEs(v.tensor_tensor(t1, qk[:, :, :, 0:ROT], table(0, 0, ROT), ALU.mult).then_inc(dve_done, 1))
                VEs(v.tensor_tensor(t2[:, :, :, 0:ROT:2], qk[:, :, :, 1:ROT:2], table(1, 0, ROT // 2), ALU.mult).then_inc(dve_done, 1))
                VEs(v.tensor_tensor(t2[:, :, :, 1:ROT:2], qk[:, :, :, 0:ROT:2], table(1, 1, ROT // 2), ALU.mult).then_inc(dve_done, 1))
                VEs(v.tensor_scalar(R[:, 0, :, ROT:], qk[:, 0, :, ROT:], DH0 ** -0.5, None, ALU.mult).then_inc(dve_done, 1))
                VEs(v.tensor_copy(R[:, 1, :, ROT:], qk[:, 1, :, ROT:]).then_inc(dve_done, 1), "A.qk", b, tt)

            def cut_pieces(b, tt, stage):
                dve.wait_ge(dve_done, VEs.n)
                st = stack[:, tt]
                if stage == 0:
                    VEs(v.tensor_tensor(R[:, :, :, 0:ROT], t1, t2, ALU.add).then_inc(dve_done, 1))
                    if b:
                        dve.wait_ge(pe_done, at("pe", "A.turn", b - 1, tt, 0, 1))
                        if b > 1:
                            dve.wait_ge(pool_done, at("pool", "A.stack", b - 1, tt))
                else:
                    VEs(v.tensor_tensor(R, R, st[:, :, :, (stage - 1) * DH0:stage * DH0], ALU.subtract).then_inc(dve_done, 1))
                dve.wait_ge(dve_done, VEs.n)
                if stage < 2:
                    VEs(v.tensor_copy(st[:, :, :, stage * DH0:(stage + 1) * DH0], R).then_inc(dve_done, 1))
                else:
                    VEs(v.tensor_copy(st[:, 0, :, 2 * DH0:3 * DH0], R[:, 0]).then_inc(dve_done, 1))
                    VEs(v.tensor_copy(st[:, 1, :, 3 * DH0:4 * DH0], R[:, 1]).then_inc(dve_done, 1), "A.pieces", b, tt)
                if stage == 2 and b == 0:
                    dve.wait_ge(dve_done, VEs.n)
                    for w, to, frm, n in STACK_COPIES:
                        VEs(v.tensor_copy(st[:, w, :, to * DH0:(to + n) * DH0], st[:, w, :, frm * DH0:(frm + n) * DH0])
                            .then_inc(dve_done, 1), "A.stack", b, tt)

            rows0(0)
            dve.wait_ge(norm_in, 16 * N_NORM)
            VEs(v.tensor_copy(identb, ident[:, :]).then_inc(dve_done, 1), "identb")
            for b in range(1, B):
                dve.wait_ge(x_in[b], 16)
                ln("A", b, True, True)
            dve.wait_ge(rope_in, 16)
            for i in range(-1, LAST0 + 1):
                for kind, b, *w in side.get(i + 1, []):
                    if kind == "rows" and b:
                        rows0(b)
                if 0 <= i < UNITS0:
                    dve.wait_ge(pe_done, at("pe", "A.S", i))
                    if i >= 3:
                        dve.wait_ge(act_done, at("act", "A.P", i - 3))
                    VEs(v.tensor_reduce(mxa[:, i % 3, :], bank(i % 3)[:, 0, :].rearrange("p (h s) -> p h s", h=2), AX.X, ALU.max,
                                        negate=True).then_inc(dve_done, 1), "A.max", i)
                n = i - 1
                if 0 <= n < UNITS0:
                    dve.wait_ge(act_done, at("act", "A.P", n))
                    VEs(v.reciprocal(ria[:, n % 3, :], rsa[:, n % 3, :]).then_inc(dve_done, 1))
                    dve.wait_ge(dve_done, VEs.n)
                    for j in range(2):
                        VEs(v.tensor_scalar(Pa[:, n % 3, j, :], Pa[:, n % 3, j, :], ria[:, n % 3, j:j + 1], None, ALU.mult)
                            .then_inc(dve_done, 1), "A.Pn", n)
                for kind, b, *w in side.get(i, []):
                    if kind == "cut" and i >= 0:
                        cut_pieces(b, *w)
                for kind, b, *w in side.get(i, []):
                    if kind == "qk":
                        rotate(b, w[0])
                    elif kind == "cut" and i < 0:
                        cut_pieces(b, *w)
                    elif kind == "out":
                        dve.wait_ge(pe_done, at("pe", "A.out", b, w[0]))
                        add_to_x(TPB * b + w[0], bank(7)[:, 0, 0:D], "A.out", b, w[0])
                for kind, t in maps.get(i, []):
                    if kind == "energy":
                        dve.wait_ge(pe_done, at("pe", "en", t))
                        VEs(v.tensor_reduce(m0[:, t:t + 1], bank(6)[:, 0, 0:S], AX.X, ALU.max, negate=True).then_inc(dve_done, 1), "m0", t)
                for kind, t in maps.get(i, []):
                    if kind == "scale":
                        dve.wait_ge(act_done, at("act", "en", t))
                        VEs(v.reciprocal(s0[:, t:t + 1], s0[:, t:t + 1]).then_inc(dve_done, 1))
                        dve.wait_ge(dve_done, VEs.n)
                        VEs(v.tensor_scalar(en, en, s0[:, t:t + 1], None, ALU.mult).then_inc(dve_done, 1), "enn", t)

            def rows_b(b):
                ln("B", b, False, False)

                def free():
                    if b:
                        dve.wait_ge(pe_done, at("pe", "B.xT", b - 1))
                ln_apply("B", b, False, False, free, rows=XSb)

            dve.wait_ge(dve_done, VEs.n)
            dve.wait_ge(const_in, 16 * N_CONST)
            rows_b(0)
            for b in range(B):
                for tt in range(TPB):
                    dve.wait_ge(pe_done, at("pe", "B.out", b, TPB - 1))
                    add_to_x(TPB * b + tt, bank(7)[:, 0, tt * D:tt * D + D], "B.x", b, tt)
                if b == B - 1:
                    book[("dve", "B.end")] = VEs.n
                dve.wait_ge(dve_done, VEs.n)
                ln("C", b, True, True)

                def free(b=b):
                    if b < 2:
                        dve.wait_ge(pe_done, at("pe", "A.rows", B - 1))
                    else:
                        dve.wait_ge(pe_done, at("pe", "C.hT", TPB * (b - 2) + 1))
                        for i in range(TPB):
                            dve.wait_ge(h_stored[(TPB * b + i) % 4], 16)
                ln_apply("C", b, True, False, free)
                dve.wait_ge(dve_done, VEs.n)
                for t in range(TPB * b, TPB * b + TPB):
                    VEs(v.tensor_tensor(XS[:, t % 4, :], XS[:, t % 4, :], nwb, ALU.mult).then_inc(dve_done, 1), "C.h", t)
                ln_residual("C", b)
                if b + 1 < B:
                    rows_b(b + 1)
                t0, tend = TPB * b, TPB * b + TPB
                dve.wait_ge(pe_done, at("pe", "C.logits", b))
                for t in range(t0, tend):
                    VEs(v.max(top8[:, t, :], bank(2)[:, 0, (t % 2) * E0:(t % 2) * E0 + E0]).then_inc(dve_done, 1))
                dve.wait_ge(dve_done, VEs.n)
                for t in range(t0, tend):
                    VEs(v.max_index(idx8[:, t, :], top8[:, t, :], bank(2)[:, 0, (t % 2) * E0:(t % 2) * E0 + E0]).then_inc(dve_done, 1))
                VEs(v.tensor_scalar(negm[:, t0:tend].rearrange("p (t o) -> p t o", o=1), top8[:, t0:tend, 0:1], -1.0, None, ALU.mult)
                    .then_inc(dve_done, 1), "C.top", b)
                dve.wait_ge(dve_done, VEs.n)
                VEs(v.tensor_copy(idf.rearrange("p (t k) -> p t k", t=TPB), idx8[:, t0:tend, 0:K0]).then_inc(dve_done, 1))
                dve.wait_ge(dve_done, VEs.n)
                VEs(v.tensor_tensor(oh.rearrange("p t k e -> p (t k) e"), iota32.rearrange("p (o e) -> p o e", o=1).broadcast_to((P, TPB * K0, E0)),
                                    idf.rearrange("p (k o) -> p k o", o=1).broadcast_to((P, TPB * K0, E0)), ALU.is_equal).then_inc(dve_done, 1))
                VEs(v.tensor_scalar(base, idf, float(CAP), None, ALU.mult).then_inc(dve_done, 1))
                dve.wait_ge(dve_done, VEs.n)
                with nc.allow_low_precision(reason="0 and 1"):
                    VEs(v.tensor_reduce(sel_tile[:, t0:tend, :], oh.rearrange("p t k e -> p t e k"), AX.X, ALU.add).then_inc(dve_done, 1), "C.sel", b)
                dve.wait_ge(act_done, at("act", "C.ex4", tend - 1))
                VEs(v.reciprocal(sm4[:, t0:tend], sm4[:, t0:tend]).then_inc(dve_done, 1))
                dve.wait_ge(dve_done, VEs.n)
                for t in range(t0, tend):
                    VEs(v.tensor_scalar(w4[:, t, :], ex4[:, t, :], sm4[:, t:t + 1], None, ALU.mult).then_inc(dve_done, 1), "C.w4", t)
                dve.wait_ge(pe_done, at("pe", "C.pos", b))
                for tt in range(TPB):
                    VEs(v.tensor_tensor(ohp[:, tt], oh[:, tt], bank(3)[:, 0, tt * E0:tt * E0 + E0].rearrange("p (o e) -> p o e", o=1)
                                        .broadcast_to((P, K0, E0)), ALU.mult).then_inc(dve_done, 1), "C.ohp", b)
                dve.wait_ge(dve_done, VEs.n)
                VEs(v.tensor_reduce(posk, ohp.rearrange("p t k e -> p (t k) e"), AX.X, ALU.add).then_inc(dve_done, 1))
                dve.wait_ge(dve_done, VEs.n)
                VEs(v.tensor_scalar(over, posk, float(CAP - 1), float(E0 * CAP), ALU.is_gt, ALU.mult).then_inc(dve_done, 1))
                VEs(v.scalar_tensor_tensor(out=rowf, in0=posk, scalar=float(CAP - 1), in1=base, op0=ALU.min, op1=ALU.add).then_inc(dve_done, 1))
                dve.wait_ge(dve_done, VEs.n)
                VEs(v.tensor_tensor(slotf, rowf, over, ALU.add).then_inc(dve_done, 1))
                VEs(v.tensor_copy(row[:, t0:tend, :], rowf.rearrange("p (t k) -> p t k", t=TPB)).then_inc(dve_done, 1))
                dve.wait_ge(dve_done, VEs.n)
                VEs(v.tensor_copy(slot[:, t0:tend, :], slotf.rearrange("p (t k) -> p t k", t=TPB)).then_inc(dve_done, 1), "C.slot", b)
            for hf in range(NHALF):
                dve.wait_ge(act_done, at("act", "C.sgs", hf))
                if hf:
                    dve.wait_ge(pe_done, at("pe", "C.sout", hf - 1))
                VEs(v.tensor_tensor(acs, sgs, bank(5)[:, 0, :], ALU.mult).then_inc(dve_done, 1), "C.sact", hf)
                dve.wait_ge(pe_done, at("pe", "C.sout", hf))
                for tt in range(HALF // P):
                    add_to_x(hf * 4 + tt, bank(6 + tt // 2)[:, 0, (tt % 2) * D:(tt % 2) * D + D], "C.xs", hf)
                dve.wait_ge(dve_done, VEs.n)
            dve.wait_ge(table_in, 16)
            VEs(v.tensor_copy(tabf[0:2 * E0, :], tab[0:2 * E0, :]).then_inc(dve_done, 1), "C.tabf")
            dve.wait_ge(pe_done, at("pe", "C.tabT"))
            VEs(v.tensor_copy(slot_tok, bank(0)[:, 0, 0:2 * E0]).then_inc(dve_done, 1), "C.slot_tok")

            def gated(e):
                dve.wait_ge(act_done, at("act", "C.sg", e))
                if e >= 2:
                    dve.wait_ge(pe_done, at("pe", "C.down", e - 2))
                VEs(v.tensor_tensor(ac[:, e % 2, :], sg[:, e % 2, :], bank(2 + e % 2)[:, 0, CAP:2 * CAP], ALU.mult).then_inc(dve_done, 1),
                    "C.act", e)

            def turned(e):
                dve.wait_ge(pe_done, at("pe", "C.xT", e))
                if e >= 2:
                    dve.wait_ge(pe_done, at("pe", "C.gu", e - 2))
                VEs(v.tensor_copy(XTc[:, e % 2], bank(e % 2)[:, 0, :].rearrange("p (k n) -> p k n", k=DB)).then_inc(dve_done, 1), "C.xT", e)

            turned(0)
            turned(1)
            for e in range(E0):
                gated(e)
                if e + 2 < E0:
                    turned(e + 2)

            def combine(t):
                dve.wait_ge(y_in[t % NY], 16 * K0 * (t // NY + 1))
                for k in range(K0):
                    VEs(v.scalar_tensor_tensor(out=X[:, t, :], in0=Y[:, t % NY, k, :], scalar=w4[:, t, k:k + 1], in1=X[:, t, :],
                                               op0=ALU.mult, op1=ALU.add).then_inc(dve_done, 1), "C.comb", t)
                    dve.wait_ge(dve_done, VEs.n)

            def mask_rows():
                dve.wait_ge(xattn1_w_in, 16 * N_XATTN1)
                VEs(v.tensor_scalar(maskf, vfl, 1.0, -NEG, ALU.subtract, ALU.mult).then_inc(dve_done, 1))
                VEs(v.tensor_reduce(mflag, vfl, AX.X, ALU.max).then_inc(dve_done, 1), "E.mask")

            def rows_d(b):
                def free():
                    if b < BPH:
                        dve.wait_ge(pe_done, at("pe", "C.hT", TILES - 1))
                        for i in range(4):
                            dve.wait_ge(h_stored[i], 16 * TILES // 4)
                    else:
                        dve.wait_ge(pe_done, at("pe", "D.xT", 0, DB - 1))
                ln_apply("D", b, True, True, free)

            def conv(hf, m):
                dve.wait_ge(act_done, at("act", "D.xi", hf, m))
                um = us[:, hf, m, :].rearrange("p (b s) -> p b s", b=BPH)
                for k in range(KC - 1):
                    if k:
                        dve.wait_ge(dve_done, VEs.n)
                    VEs(v.scalar_tensor_tensor(out=um, in0=xi[:, m, :, k:k + S], scalar=cw[:, m, k:k + 1], in1=um,
                                               op0=ALU.mult, op1=ALU.add).then_inc(dve_done, 1), "D.conv", hf, m)

            dve.wait_ge(act_done, at("act", "D.A"))
            VEs(v.tensor_scalar(Aneg, Aneg, -1.0, None, ALU.mult).then_inc(dve_done, 1), "D.A")
            dve.wait_ge(mamba_w_in, 16 * N_MAMBA)
            VEs(v.tensor_copy(wdt, wxp[:, :, 32:33].broadcast_to((P, IB, P))).then_inc(dve_done, 1), "D.wdt")
            for b in range(BPH):
                for t in range(TPB * b, TPB * b + TPB):
                    combine(t)
                ln("D", b, True, True)
                rows_d(b)
            combine(GT)
            combine(GT + 1)
            for m in range(IB):
                conv(0, m)
                if m % 2:
                    combine(GT + 2 + m // 2)
            book[("dve", "C.end")] = VEs.n
            for b in range(BPH, B):
                ln("D", b, True, True)
            for hf in range(NHALF):
                u = us[:, hf]
                dve.wait_ge(pe_done, at("pe", "D.dt", hf))
                for m in range(IB):
                    if hf and m == 0:
                        dve.wait_ge(act_done, at("act", "D.dA", hf * NST - 1))
                    VEs(v.tensor_scalar(dt[:, m, :], bank(6)[:, 0, :], dtw[:, m:m + 1], dtb[:, m:m + 1], ALU.mult, ALU.add).then_inc(dve_done, 1), "D.v", hf, m)
                dve.wait_ge(pe_done, at("pe", "D.xs", hf))
                NR = 2 * NST
                if hf:
                    dve.wait_ge(pe_done, at("pe", "D.C", hf * NST - 1))
                VEs(v.tensor_copy(xs3f[0:NR, :], bank(7)[0:NR, 0, :]).then_inc(dve_done, 1), "D.xsf", hf)
                dve.wait_ge(dve_done, VEs.n)
                VEs(v.tensor_copy(xs3[0:NR, :], xs3f[0:NR, :]).then_inc(dve_done, 1))
                for i in range(1, 3):
                    dve.wait_ge(dve_done, VEs.n)
                    VEs(v.tensor_tensor(xs3f[0:NR, :], xs3f[0:NR, :], xs3[0:NR, :] if i == 1 else xs3m[0:NR, :], ALU.subtract).then_inc(dve_done, 1))
                    dve.wait_ge(dve_done, VEs.n)
                    if i == 1:
                        VEs(v.tensor_copy(xs3m[0:NR, :], xs3f[0:NR, :]).then_inc(dve_done, 1))
                        dve.wait_ge(dve_done, VEs.n)
                    VEs(v.tensor_copy(xs3[NR * i:NR * i + NR, :], xs3f[0:NR, :]).then_inc(dve_done, 1), "D.xs3", hf)
                for m in range(IB):
                    dve.wait_ge(act_done, at("act", "D.sp", hf, m))
                    VEs(v.scalar_tensor_tensor(out=dt[:, m, :], in0=dt[:, m, :], scalar=0.0, in1=e1[:, m, :], op0=ALU.max, op1=ALU.add).then_inc(dve_done, 1))
                    dve.wait_ge(dve_done, VEs.n)
                    VEs(v.tensor_tensor(dtu[:, m, :], dt[:, m, :], u[:, m, :], ALU.mult).then_inc(dve_done, 1), "D.dtu", hf, m)
                if hf == 0:
                    for b in range(BPH, B):
                        rows_d(b)
                flat = "p m n -> p (m n)"
                for n in range(NST):
                    s = hf * NST + n
                    dve.wait_ge(pool_done, at("pool", "D.Bu", s))
                    dve.wait_ge(act_done, at("act", "D.dA", s))
                    h = hbuf(s)
                    VEs(v.tensor_tensor_scan(h.rearrange(flat), dA[:, s % 2].rearrange(flat), h.rearrange(flat), 0.0,
                                             ALU.mult, ALU.add).then_inc(dve_done, 1), "D.scan", s)
                    dve.wait_ge(dve_done, VEs.n)
                    dve.wait_ge(pe_done, at("pe", "D.C", s))
                    VEs(v.tensor_tensor(h, h, bank(4 + s % 2).broadcast_to((P, IB, HALF)), ALU.mult).then_inc(dve_done, 1), "D.hC", s)
                if hf + 1 < NHALF:
                    conv(hf + 1, 0)
                    conv(hf + 1, 1)

                def skip(m):
                    dve.wait_ge(pe_done, at("pe", "D.y", hf, m))
                    VEs(v.scalar_tensor_tensor(out=u[:, m, :], in0=u[:, m, :], scalar=dpar[:, m:m + 1], in1=bank(m)[:, 0, :],
                                               op0=ALU.mult, op1=ALU.add).then_inc(dve_done, 1), "D.yu", hf, m)

                def gate(m):
                    dve.wait_ge(dve_done, at("dve", "D.yu", hf, m))
                    dve.wait_ge(act_done, at("act", "D.sz", hf, m))
                    VEs(v.tensor_tensor(sz[:, m, :], sz[:, m, :], u[:, m, :], ALU.mult).then_inc(dve_done, 1), "D.yz", hf, m)

                skip(0)
                for m in range(1, IB):
                    skip(m)
                    gate(m - 1)
                gate(IB - 1)
                if hf + 1 < NHALF:
                    conv(hf + 1, 2)
                    conv(hf + 1, 3)
                if hf == NHALF - 1:
                    mask_rows()
                dve.wait_ge(pe_done, at("pe", "D.out", hf))
                for tt in range(HALF // P):
                    add_to_x(hf * 4 + tt, bank(4 + tt // 2)[:, 0, (tt % 2) * D:(tt % 2) * D + D], "D.x", hf)
            book[("dve", "D.end")] = VEs.n

            dve.wait_ge(dve_done, VEs.n)
            for b in range(B):
                ln("E", b, False, False)

            def rows1(b):
                def free():
                    dve.wait_ge(pe_done, at("pe", "E.rows", b - 2) if b >= 2 else at("pe", "D.xT", NHALF - 1, DB - 1))
                ln_apply("E", b, False, False, free)

            def f_rows(b):
                def free():
                    dve.wait_ge(pe_done, at("pe", "F.xT", b - 2) if b >= 2 else at("pe", "E.rows", B - 1))
                ln_apply("F", b, False, False, free)

            W = E1 + 1

            def per_tile(x, n):
                return x.rearrange("p (t o) -> p t o", o=1).broadcast_to((P, GT, n))

            def route(g, stage):
                ts = slice(GT * g, GT * g + GT)
                if stage == 0:
                    dve.wait_ge(pe_done, at("pe", "F.logits", g))
                    VEs(v.tensor_copy(lg[:, ts, :], bank(5 if g else 2)[:, 0, 0:GT * W].rearrange("p (t e) -> p t e", t=GT)).then_inc(dve_done, 1), "F.lg", g)
                    dve.wait_ge(dve_done, VEs.n)
                    VEs(v.tensor_reduce(np8[:, ts], lg[:, ts, 0:E1], AX.X, ALU.max, negate=True).then_inc(dve_done, 1), "F.max", g)
                elif stage == 1:
                    dve.wait_ge(act_done, at("act", "F.pr", g))
                    VEs(v.reciprocal(rp[:, ts], sp1[:, ts]).then_inc(dve_done, 1))
                    VEs(v.tensor_scalar(cc[:, ts, E1:], lg[:, ts, E1:], 1.0, None, ALU.add).then_inc(dve_done, 1))
                    dve.wait_ge(dve_done, VEs.n)
                    VEs(v.tensor_tensor(pr[:, ts, :], pr[:, ts, :], per_tile(rp[:, ts], E1), ALU.mult).then_inc(dve_done, 1))
                    VEs(v.reciprocal(cc[:, ts, E1:], cc[:, ts, E1:]).then_inc(dve_done, 1))
                    dve.wait_ge(dve_done, VEs.n)
                    for t in range(GT * g, GT * g + GT):
                        VEs(v.max(tp8[:, t, :], pr[:, t, :]).then_inc(dve_done, 1))
                    dve.wait_ge(dve_done, VEs.n)
                    for t in range(GT * g, GT * g + GT):
                        VEs(v.max_index(ti8[:, t, :], tp8[:, t, :], pr[:, t, :]).then_inc(dve_done, 1))
                    dve.wait_ge(dve_done, VEs.n)
                    VEs(v.tensor_copy(tif[:, ts, :], ti8[:, ts, 0:2]).then_inc(dve_done, 1))
                else:
                    dve.wait_ge(dve_done, VEs.n)
                    for t in range(GT * g, GT * g + GT):
                        VEs(v.tensor_scalar(cc[:, t, 0:E1], iota8, tif[:, t, 0:1], tp8[:, t, 0:1], ALU.is_equal, ALU.mult).then_inc(dve_done, 1))
                        VEs(v.tensor_scalar(c2[:, t, :], iota8, tif[:, t, 1:2], tp8[:, t, 1:2], ALU.is_equal, ALU.mult).then_inc(dve_done, 1))
                    dve.wait_ge(dve_done, VEs.n)
                    VEs(v.tensor_tensor(cc[:, ts, 0:E1], cc[:, ts, 0:E1], c2[:, ts, :], ALU.add).then_inc(dve_done, 1))
                    dve.wait_ge(dve_done, VEs.n)
                    VEs(v.tensor_copy(chb, cc[:, ts, :]).then_inc(dve_done, 1))
                    dve.wait_ge(dve_done, VEs.n)
                    VEs(v.tensor_copy(c27[:, ts, 0:W], chb).then_inc(dve_done, 1))
                    VEs(v.tensor_tensor(r1c, cc[:, ts, :], chb, ALU.subtract).then_inc(dve_done, 1))
                    dve.wait_ge(dve_done, VEs.n)
                    VEs(v.tensor_copy(cmb, r1c).then_inc(dve_done, 1))
                    dve.wait_ge(dve_done, VEs.n)
                    VEs(v.tensor_copy(c27[:, ts, W:2 * W], cmb).then_inc(dve_done, 1))
                    VEs(v.tensor_tensor(c27[:, ts, 2 * W:], r1c, cmb, ALU.subtract).then_inc(dve_done, 1), "F.c27", g)
                    dve.wait_ge(dve_done, VEs.n)

            rows1(0)
            side = side_work()
            for i in range(-1, LAST_STEP + 1):
                if i == UNITS + 3:
                    dve.wait_ge(dve_done, VEs.n)
                    for b in range(BPH):
                        ln("F", b, False, False)
                    for b in range(BPH):
                        f_rows(b)
                elif i == UNITS + 4:
                    for stage in range(3):
                        route(0, stage)
                for kind, b, *w in side.get(i + 1, []):
                    if kind == "rows" and b:
                        rows1(b)
                if 0 <= i < UNITS:
                    dve.wait_ge(pe_done, at("pe", "E.S", i))
                    if i >= 3:
                        dve.wait_ge(pe_done, at("pe", "E.PT", i - 3))
                    mask = maskf[:, unit(i)[0], :].rearrange("p (o s) -> p o s", o=1).broadcast_to((P, GR, S))
                    VEs(v.tensor_tensor(Pe[:, i % 3], bank(i % 2)[:, 0, :].rearrange("p (h s) -> p h s", h=GR), mask, ALU.add)
                        .then_inc(dve_done, 1), "E.masked", i)
                    dve.wait_ge(dve_done, VEs.n)
                    VEs(v.tensor_reduce(mxe[:, i % 3, :], Pe[:, i % 3], AX.X, ALU.max,
                                        negate=True).then_inc(dve_done, 1), "E.max", i)
                n = i - 1
                if 0 <= n < UNITS:
                    b = unit(n)[0]
                    dve.wait_ge(act_done, at("act", "E.P", n))
                    VEs(v.reciprocal(rie[:, n % 3, :], rse[:, n % 3, :]).then_inc(dve_done, 1))
                    dve.wait_ge(dve_done, VEs.n)
                    for j in range(GR):
                        VEs(v.tensor_scalar(Pe[:, n % 3, j, :], Pe[:, n % 3, j, :], rie[:, n % 3, j:j + 1], mflag[:, b:b + 1],
                                            ALU.mult, ALU.mult).then_inc(dve_done, 1), "E.Pn", n)
                for kind, b, *w in side.get(i, []):
                    if kind == "values" and b:
                        dve.wait_ge(pe_done, at("pe", "E.values", b, w[0]))
                        if b >= 2 and w[0] == 0:
                            dve.wait_ge(pe_done, at("pe", "E.av", (b - 1) * UPB - 1))
                        VEs(v.tensor_copy(V1[:, b % 2, w[0] // 2, 512 * (w[0] % 2):512 * (w[0] % 2) + 512], bank(side_bank(kind, b, w))[:, 0, :])
                            .then_inc(dve_done, 1), "E.values", b, w[0])
                    elif kind == "output":
                        dve.wait_ge(pe_done, at("pe", "E.output", b, w[0]))
                        add_to_x(TPB * b + w[0], bank(side_bank(kind, b, w))[:, 0, 0:D], "E.output", b, w[0])
            dve.wait_ge(dve_done, VEs.n)

            for b in range(BPH, B):
                ln("F", b, False, False)
            for b in range(BPH, B):
                f_rows(b)
            for hf in range(NHALF):
                for f in range(FB):
                    n = hf * FB + f
                    m = min(P, FT - f * P)
                    dve.wait_ge(act_done, at("act", "F.sg", n))
                    dve.wait_ge(pe_done, at("pe", "F.gu", n))
                    VEs(v.tensor_tensor(tf[0:m, n % 2, :], sgf[0:m, n % 2, :], bank(2 + n % 2)[0:m, 0, :], ALU.mult).then_inc(dve_done, 1))
                    dve.wait_ge(dve_done, VEs.n)
                    dve.wait_ge(pe_done, at("pe", "F.spread", n))
                    if n >= 3:
                        dve.wait_ge(pe_done, at("pe", "F.down", n - 3))
                    VEs(v.tensor_tensor(acf[0:m, n % 3, :], tf[0:m, n % 2, :], bank(4)[0:m, 0, :], ALU.mult).then_inc(dve_done, 1), "F.act", n)
                    if n in (3, 4, 5):
                        route(1, n - 3)
                dve.wait_ge(pe_done, at("pe", "F.down", hf * FB + FB - 1))
                for tt in range(HALF // P):
                    add_to_x(hf * 4 + tt, bank(6 + tt // 2)[:, 0, (tt % 2) * D:(tt % 2) * D + D], "F.x", hf * 4 + tt)

        @block.tensor
        def _(pe):
            te = nc.tensor

            def mm(dst, lhsT, rhs, start=True, stop=True, **kw):
                return te.matmul(dst, lhsT, rhs, start=start, stop=stop, **kw)

            def transposes(dst, name, b, step, rows=XS):
                pe.wait_ge(dve_done, at("dve", name + ".xs", b))
                for tt in range(TPB):
                    for k in range(DB):
                        last = te.transpose(dst[:, k, tt * P:tt * P + P], rows[:, (TPB * b + tt) % rows.shape[1], k * P:k * P + P], ident[:, :])
                PEs(last.then_inc(pe_done, 1), *step)

            pe.wait_ge(norm_in, 16 * N_NORM)
            side, maps = side_work0(), map_work()
            user = {}

            def emptied(n, by=None):
                if n in user:
                    pe.wait_ge(act_done if user[n][0] == "act" else dve_done, at(*user[n]))
                user[n] = by

            for i in range(-1, LAST0 + 1):
                if 0 <= i < UNITS0:
                    b, tt, p = unit0(i)
                    if p == 0:
                        pe.wait_ge(act_done, at("act", "A.turn", b, TPB - 1, 0, 1))
                    if i >= 3:
                        pe.wait_ge(act_done, at("act", "A.P", i - 3))
                    for j in range(2):
                        h = 2 * p + j
                        last = mm(bank(i % 3)[:, 0, j * S:j * S + S], QT[0:KA, b % 2, 0, h, tt * P:tt * P + P], QT[0:KA, b % 2, 1, h, :])
                    PEs(last.then_inc(pe_done, 1), "A.S", i)
                n = i - 2
                if 0 <= n < UNITS0:
                    pe.wait_ge(dve_done, at("dve", "A.Pn", n))
                    if n >= 2:
                        pe.wait_ge(act_done, at("act", "A.PT", n - 2))
                    for j in range(2):
                        for k in range(2):
                            o = (j * 2 + k) * P
                            last = te.transpose(bank(3 + n % 2)[:, 0, o:o + P], Pa[:, n % 3, j, k * P:k * P + P], ident[:, :])
                    PEs(last.then_inc(pe_done, 1), "A.PT", n)
                n = i - 3
                if 0 <= n < UNITS0:
                    b, tt, p = unit0(n)
                    pe.wait_ge(act_done, at("act", "A.PT", n))
                    if p == 0 and n:
                        pe.wait_ge(act_done, at("act", "A.cT", n // UPT0 - 1))
                    for j in range(2):
                        h = 2 * p + j
                        r = 32 * (h % 4)
                        for k in range(2):
                            last = mm(bank(5)[r:r + 32, 0, (h // 4) * P:(h // 4) * P + P], Va[:, b % 2, k, h, :], PTa[:, n % 2, j, k, :], k == 0, k == 1)
                    PEs(last.then_inc(pe_done, 1), "A.av", n)
                for kind, b, *w in side.get(i, []):
                    if kind == "cut":
                        continue
                    n = side_bank0(kind, b, w)
                    emptied(n, ("dve" if kind in ("qk", "out") else "act", "A." + kind, b, *w))
                    if kind == "rows":
                        transposes(bank(n)[:, 0, :].rearrange("p (k n) -> p k n", k=DB), "A", b, ("A.rows", b))
                        continue
                    if kind in ("qk", "v"):
                        pe.wait_ge(act_done, at("act", "A.rows", b))
                        if b == 0:
                            pe.wait_ge(attn_w_in, 16 * N_ATTN)
                        c0, c1 = (0, 2 * D) if kind == "qk" else (2 * D, 3 * D)
                        for k in range(DB):
                            last = mm(bank(n)[:, 0, 0:c1 - c0], xTa[:, b % 2, k, w[0] * P:w[0] * P + P], w_in[:, k, c0:c1], k == 0, k == DB - 1)
                    elif kind == "turn":
                        tt, qk, half = w
                        if b:
                            pe.wait_ge(pool_done, at("pool", "A.stack", b, tt))
                        else:
                            pe.wait_ge(dve_done, at("dve", "A.stack", b, tt))
                        pb = bank(n)[0:KA, 0, :].bitcast(BF16)
                        for h in range(8):
                            last = te.transpose(pb[:, h * P:h * P + P], stack[:, tt, qk, 8 * half + h, :], identb)
                    else:
                        pe.wait_ge(act_done, at("act", "A.cT", TPB * b + w[0]))
                        for g in range(4):
                            last = mm(bank(n)[:, 0, 0:D], CTa[:, g, :], w_out[:, g, :], g == 0, g == 3)
                    PEs(last.then_inc(pe_done, 1), "A." + kind, b, *w)
                if i == 0:
                    pe.wait_ge(ctx_in, 16)
                    pe.wait_ge(xattn_w_in, 16 * N_XATTN)
                for kind, t in maps.get(i, []):
                    if kind == "context":
                        emptied(6, ("act", "context", t))
                        for j in range(4):
                            last = te.transpose(bank(6)[:, 0, j * P:j * P + P], cx[:, 4 * t + j, :], ident[:, :])
                        PEs(last.then_inc(pe_done, 1), "context", t)
                    elif kind == "qk":
                        emptied(6, ("act", "map.qk", t))
                        PEs(mm(bank(6)[:, 0, :], (wq0, wk0)[t // 2], ctxT[:, 512 * (t % 2):512 * (t % 2) + 512]).then_inc(pe_done, 1), "map.qk", t)
                    elif kind == "energy":
                        emptied(6, ("act", "en", t))
                        b = t // 2
                        PEs(mm(bank(6)[:, 0, 0:S], q0[:, t * P:t * P + P], k0[:, b * S:b * S + S]).then_inc(pe_done, 1), "en", t)
                    elif kind == "turn":
                        emptied(6, ("act", "map", t))
                        pe.wait_ge(dve_done, at("dve", "enn", t))
                        for m in range(2):
                            last = te.transpose(bank(6)[:, 0, m * P:m * P + P], en[:, m * P:m * P + P], ident[:, :])
                        PEs(last.then_inc(pe_done, 1), "map", t)

            def rows_b(b):
                if b:
                    pe.wait_ge(act_done, at("act", "B.xT", b - 1))
                transposes(bank(6)[:, 0, :].rearrange("p (k n) -> p k n", k=DB), "B", b, ("B.xT", b), rows=XSb)

            def out_b(b):
                pe.wait_ge(act_done, at("act", "B.xT", b))
                if b:
                    pe.wait_ge(dve_done, at("dve", "B.x", b - 1, 1))
                for tt in range(TPB):
                    for k in range(DB):
                        last = mm(bank(7)[:, 0, tt * D:tt * D + D], xTb[:, b % 2, k, tt * P:tt * P + P], attT[:, b, k, :], k == 0, k == DB - 1)
                    PEs(last.then_inc(pe_done, 1), "B.out", b, tt)

            def shared_up(hf):
                for w in range(2):
                    for k in range(DB):
                        last = mm(bank(4 + w)[:, 0, :], sgu[:, k, w * I0:w * I0 + I0], hT[:, k, hf * HALF:hf * HALF + HALF], k == 0, k == DB - 1)
                PEs(last.then_inc(pe_done, 1), "C.sgu", hf)

            pe.wait_ge(act_done, at("act", "map", TILES - 1))
            pe.wait_ge(moe_w_in, 16 * N_MOE)
            pe.wait_ge(pool_done, at("pool", "ones"))
            rows_b(0)
            out_b(0)
            for b in range(B):
                for t in range(TPB * b, TPB * b + TPB):
                    pe.wait_ge(dve_done, at("dve", "C.h", t))
                    if b:
                        pe.wait_ge(act_done, at("act", "C.hT", t - 2))
                    for k in range(DB):
                        last = te.transpose(bank(t % 2)[:, 0, k * P:k * P + P], XS[:, t % 4, k * P:k * P + P], ident[:, :])
                    PEs(last.then_inc(pe_done, 1), "C.hT", t)
                for t in range(TPB * b, TPB * b + TPB):
                    pe.wait_ge(act_done, at("act", "C.hT", t))
                    if b:
                        pe.wait_ge(dve_done, at("dve", "C.top", b - 1))
                    for k in range(DB):
                        last = mm(bank(2)[:, 0, (t % 2) * E0:(t % 2) * E0 + E0], hT[:, k, t * P:t * P + P], gw[:, k, :], k == 0, k == DB - 1)
                PEs(last.then_inc(pe_done, 1), "C.logits", b)
                if b + 1 < B:
                    rows_b(b + 1)
                pe.wait_ge(dve_done, at("dve", "C.sel", b))
                if b:
                    pe.wait_ge(dve_done, at("dve", "C.ohp", b - 1))
                for tt in range(TPB):
                    t = TPB * b + tt
                    dst = bank(3)[:, 0, tt * E0:tt * E0 + E0]
                    for i in range(t):
                        mm(dst, ones, sel_tile[:, i, :], i == 0, False)
                    last = mm(dst, tri, sel_tile[:, t, :], t == 0, True)
                PEs(last.then_inc(pe_done, 1), "C.pos", b)
                if b + 1 < B:
                    out_b(b + 1)
                if b + 2 == B:
                    book[("pe", "B.end")] = PEs.n
                    shared_up(0)
            pe.wait_ge(dve_done, at("dve", "C.slot", B - 1))
            for hf in range(NHALF):
                if hf:
                    pe.wait_ge(dve_done, at("dve", "C.xs", hf - 1))
                    shared_up(hf)
                pe.wait_ge(dve_done, at("dve", "C.sact", hf))
                for tt in range(HALF // P):
                    last = mm(bank(6 + tt // 2)[:, 0, (tt % 2) * D:(tt % 2) * D + D], acs[:, tt * P:tt * P + P], sdn)
                PEs(last.then_inc(pe_done, 1), "C.sout", hf)
            pe.wait_ge(dve_done, at("dve", "C.tabf"))
            PEs(te.transpose(bank(0)[:, 0, 0:2 * E0], tabf[0:2 * E0, :], ident[0:2 * E0, 0:2 * E0]).then_inc(pe_done, 1), "C.tabT")

            def expert_rows(e):
                pe.wait_ge(gathered[e % 4], 16 * 2 * (e // 4 + 1))
                if e >= 2:
                    pe.wait_ge(dve_done, at("dve", "C.xT", e - 2))
                for s in range(2):
                    for k in range(DB):
                        last = te.transpose(bank(e % 2)[:, 0, k * CAP + s * P:k * CAP + s * P + P], G[:, e % 4, s, k * P:k * P + P], ident[:, :])
                PEs(last.then_inc(pe_done, 1), "C.xT", e)

            def expert_up(e):
                pe.wait_ge(dve_done, at("dve", "C.xT", e))
                pe.wait_ge(expert_in[e % NW], 32 * (e // NW + 1))
                if e >= 2:
                    pe.wait_ge(dve_done, at("dve", "C.act", e - 2))
                for w in range(2):
                    for k in range(DB):
                        last = mm(bank(2 + e % 2)[:, 0, w * CAP:w * CAP + CAP], w13[:, e % NW, k, w * I0:w * I0 + I0], XTc[:, e % 2, k, :],
                                  k == 0, k == DB - 1)
                PEs(last.then_inc(pe_done, 1), "C.gu", e)

            def expert_down(e):
                pe.wait_ge(dve_done, at("dve", "C.act", e))
                if e >= 2:
                    pe.wait_ge(act_done, at("act", "C.eo", e - 2))
                for s in range(2):
                    last = mm(bank(4 + e % 2)[:, 0, s * D:s * D + D], ac[:, e % 2, s * P:s * P + P], w2[:, e % NW, :])
                PEs(last.then_inc(pe_done, 1), "C.down", e)

            expert_rows(0)
            expert_rows(1)
            expert_up(0)
            for e in range(E0):
                if e + 2 < E0:
                    expert_rows(e + 2)
                if e + 1 < E0:
                    expert_up(e + 1)
                expert_down(e)

            pe.wait_ge(mamba_w_in, 16 * N_MAMBA)
            pe.wait_ge(act_done, at("act", "C.eo", E0 - 1))
            pe.wait_ge(dve_done, at("dve", "D.wdt"))

            def d_rows(hf, k):
                for b in range(BPH * hf, BPH * hf + BPH):
                    pe.wait_ge(dve_done, at("dve", "D.xs", b))
                    for tt in range(TPB):
                        o = (b % BPH) * S + tt * P
                        last = te.transpose(bank(7 if hf else 6 + k)[:, 0, o:o + P], XS[:, (TPB * b + tt) % 4, k * P:k * P + P], ident[:, :])
                PEs(last.then_inc(pe_done, 1), "D.xT", hf, k)

            def product_in(dst, m, *step):
                for k in range(DB):
                    last = mm(dst, wip[:, k, m * P:m * P + P], xTd[:, k, :], k == 0, k == DB - 1)
                PEs(last.then_inc(pe_done, 1), *step)

            for k in range(DB):
                d_rows(0, k)
            for k in range(DB):
                pe.wait_ge(act_done, at("act", "D.xT", 0, k))
            for m in range(IB):
                product_in(bank(m)[:, 0, :], m, "D.xi", 0, m)
            for hf in range(NHALF):
                for m in range(IB):
                    pe.wait_ge(act_done, at("act", "D.u", hf, m))
                    mm(bank(7)[0:33, 0, :], wxp[:, m, :], us[:, hf, m, :], m == 0, m == IB - 1)
                    last = mm(bank(6)[:, 0, :], wdt[:, m, :], us[:, hf, m, :], m == 0, m == IB - 1)
                PEs(last.then_inc(pe_done, 1), "D.xs", hf)
                book[("pe", "D.dt", hf)] = PEs.n
                for m in range(IB):
                    if hf:
                        pe.wait_ge(dve_done, at("dve", "D.yu", hf - 1, m))
                    product_in(bank(m)[:, 0, :], IB + m, "D.z", hf, m)
                pe.wait_ge(dve_done, at("dve", "D.v", hf, IB - 1))
                pe.wait_ge(dve_done, at("dve", "D.xs3", hf))
                end = hf * NST + NST

                def spread_b(s):
                    if s % NST and s < end:
                        pe.wait_ge(act_done, at("act", "D.Bb", s - 1))
                    if s < end:
                        PEs(mm(bank(6)[:, 0, :], selbc[0:96, s % NST, :], xs3[0:96, :]).then_inc(pe_done, 1), "D.B", s)

                def spread_c(s):
                    if s < end:
                        PEs(mm(bank(4 + s % 2)[:, 0, :], selbc[0:96, NST + s % NST, :], xs3[0:96, :]).then_inc(pe_done, 1), "D.C", s)

                first = hf * NST
                for i in range(2):
                    spread_b(first + i)
                    spread_c(first + i)
                spread_b(first + 2)
                for s in range(first, end):
                    spread_b(s + 3)
                    pe.wait_ge(dve_done, at("dve", "D.hC", s))
                    spread_c(s + 2)
                    if s == first:
                        pe.wait_ge(act_done, at("act", "D.sz", hf, IB - 1))
                    for m in range(IB):
                        last = mm(bank(m)[:, 0, :], ident[:, :], hbuf(s)[:, m, :], s == first, s == end - 1)
                        if s == end - 1:
                            PEs(last.then_inc(pe_done, 1), "D.y", hf, m)
                    if s < end - 1:
                        PEs(last.then_inc(pe_done, 1), "D.sum", s)
                    else:
                        book[("pe", "D.sum", s)] = PEs.n
                    if hf == 0:
                        for kind, i in ahead.get(s, []):
                            before = {("rows", 1): ("D.xT", 1, 0), ("inner", 0): ("D.xT", 1, 1)}.get((kind, i), ("D.xi", 1, i - 1))
                            if (kind, i) == ("rows", 0):
                                pe.wait_ge(dve_done, at("dve", "D.xsf", 0))
                            else:
                                pe.wait_ge(act_done, at("act", *before))
                            if kind == "rows":
                                d_rows(1, i)
                            else:
                                product_in(bank(7)[:, 0, :], i, "D.xi", 1, i)
                for m in range(IB):
                    pe.wait_ge(dve_done, at("dve", "D.yz", hf, m))
                    for tt in range(HALF // P):
                        last = mm(bank(4 + tt // 2)[:, 0, (tt % 2) * D:(tt % 2) * D + D], sz[:, m, tt * P:tt * P + P], wop[:, m, :],
                                  m == 0 and tt % 2 == 0, m == IB - 1, skip_group_check=True)
                PEs(last.then_inc(pe_done, 1), "D.out", hf)
            book[("pe", "D.end")] = PEs.n

            pe.wait_ge(xattn1_w_in, 16 * N_XATTN1)
            pe.wait_ge(dve_done, at("dve", "E.mask"))
            side = side_work()
            last_item = {}

            def item(kind, b, w=()):
                n = side_bank(kind, b, w)
                dst = bank(n)[:, 0, :]
                if n in last_item:
                    pe.wait_ge(act_done if last_item[n][0] == "act" else dve_done, at(*last_item[n]))
                step = ("E." + kind, b, *w)
                if kind == "rows":
                    if b == 0:
                        pe.wait_ge(dve_done, at("dve", "D.x", NHALF - 1))
                    transposes(dst.rearrange("p (k n) -> p k n", k=DB), "E", b, step)
                elif kind == "keys":
                    for j in range(2):
                        h = 2 * w[0] + j
                        last = mm(dst[:, j * S:j * S + S], wk1[:, h * P:h * P + P], ctxT[:, b * S:b * S + S])
                    PEs(last.then_inc(pe_done, 1), *step)
                elif kind == "values":
                    o = b * S + (w[0] // 2) * P
                    PEs(mm(dst, ctxT[:, o:o + P], wv1[:, (w[0] % 2) * 512:(w[0] % 2) * 512 + 512]).then_inc(pe_done, 1), *step)
                elif kind == "queries":
                    pe.wait_ge(act_done, at("act", "E.rows", b))
                    for j in range(GR):
                        h = GR * w[0] + j
                        for k in range(DB):
                            last = mm(dst[:, j * S:j * S + S], wq1[:, k, h * P:h * P + P], xTe[:, b % 2, k, :], k == 0, k == DB - 1)
                    PEs(last.then_inc(pe_done, 1), *step)
                else:
                    pe.wait_ge(act_done, at("act", "E.OT", (b + 1) * HKV - 1))
                    for h in range(H1):
                        last = mm(dst[:, 0:D], OT[:, w[0], h, :], wo1[:, h, :], h == 0, h == H1 - 1)
                    PEs(last.then_inc(pe_done, 1), *step)
                last_item[n] = ("dve" if kind == "output" or (kind == "values" and b) else "act", *step)

            def f_rows(b, n):
                transposes(bank(n)[:, 0, :].rearrange("p (k n) -> p k n", k=DB), "F", b, ("F.xT", b))

            def f_logits(g, n):
                pe.wait_ge(ffn1_w_in, 16 * N_FFN1)
                pe.wait_ge(act_done, at("act", "F.xT", g * BPH + BPH - 1))
                for t in range(GT * g, GT * g + GT):
                    o = (t % GT) * P
                    for k in range(DB):
                        last = mm(bank(n)[:, 0, (t % GT) * (E1 + 1):(t % GT + 1) * (E1 + 1)], xTf[:, g, k, o:o + P], wr[:, k, :], k == 0, k == DB - 1)
                PEs(last.then_inc(pe_done, 1), "F.logits", g)

            def f_turned(g, n):
                pe.wait_ge(dve_done, at("dve", "F.c27", g))
                for tt in range(GT):
                    last = te.transpose(bank(n)[0:27, 0, tt * P:tt * P + P], c27[:, GT * g + tt, :], ident[:, :])
                PEs(last.then_inc(pe_done, 1), "F.cT", g)

            for i in range(-1, LAST_STEP + 1):
                if 0 <= i < UNITS:
                    b, h, qt = unit(i)
                    pe.wait_ge(act_done, at("act", "E.queries", b, h))
                    if i % UPB == 0:
                        pe.wait_ge(act_done, at("act", "E.keys", b, 3))
                    if i == 0:
                        pe.wait_ge(act_done, at("act", "E.values", 0, 3))
                    if i >= 2:
                        pe.wait_ge(dve_done, at("dve", "E.masked", i - 2))
                    dst = bank(i % 2)[:, 0, :]
                    for j in range(GR):
                        last = mm(dst[:, j * S:j * S + S], QE[:, (b * HKV + h) % 3, j, qt * P:qt * P + P], kT[:, b % 2, h, :])
                    PEs(last.then_inc(pe_done, 1), "E.S", i)
                n = i - 2
                if 0 <= n < UNITS:
                    pe.wait_ge(dve_done, at("dve", "E.Pn", n))
                    if n >= 2:
                        pe.wait_ge(act_done, at("act", "E.PT", n - 2))
                    for j in range(GR):
                        for k in range(2):
                            o = (j * 2 + k) * P
                            last = te.transpose(bank(3 + n % 2)[:, 0, o:o + P], Pe[:, n % 3, j, k * P:k * P + P], ident[:, :])
                    PEs(last.then_inc(pe_done, 1), "E.PT", n)
                n = i - 3
                if 0 <= n < UNITS:
                    b, h, qt = unit(n)
                    pe.wait_ge(act_done, at("act", "E.PT", n))
                    if n % UPB == 0 and b:
                        pe.wait_ge(dve_done, at("dve", "E.values", b, 3))
                    if n >= 4 and n % 2 == 0:
                        pe.wait_ge(act_done, at("act", "E.OT", n // 2 - 2))
                    o = qt * GR * P
                    for k in range(2):
                        last = mm(bank(5 + n // 2 % 2)[:, 0, o:o + GR * P].rearrange("p (g q) -> p g q", g=GR), V1[:, b % 2, k, h * P:h * P + P],
                                  PTe[:, n % 2, :, k, :], k == 0, k == 1)
                    PEs(last.then_inc(pe_done, 1), "E.av", n)
                if i == UNITS + 4:
                    f_logits(0, 2)
                for kind, b, *w in side.get(i, []):
                    item(kind, b, w)
                if i == UNITS + 3:
                    pe.wait_ge(act_done, at("act", "E.P", UNITS - 1))
                    for b in range(BPH):
                        f_rows(b, b)

            f_turned(0, 3)

            def up(n):
                hf, f = n // FB, n % FB
                m = min(P, FT - f * P)
                if n == 0:
                    pe.wait_ge(act_done, at("act", "F.cT", 0))
                elif n >= 2:
                    pe.wait_ge(dve_done, at("dve", "F.act", n - 2))
                for w_, bk in ((wg, n % 2), (wu, 2 + n % 2)):
                    for k in range(DB):
                        last = mm(bank(bk)[0:m, 0, :], w_[:, k, f * P:f * P + m], xTf[:, hf, k, :], k == 0, k == DB - 1)
                PEs(last.then_inc(pe_done, 1), "F.gu", n)
                if n:
                    pe.wait_ge(dve_done, at("dve", "F.act", n - 1))
                if n == FB:
                    pe.wait_ge(act_done, at("act", "F.cT", 1))
                PEs(mm(bank(4)[0:m, 0, :], sel27[0:27, f * P:f * P + m], cT[0:27, hf * HALF:hf * HALF + HALF]).then_inc(pe_done, 1), "F.spread", n)

            up(0)
            for n in range(NHALF * FB):
                hf, f = n // FB, n % FB
                m = min(P, FT - f * P)
                if n + 1 < NHALF * FB:
                    up(n + 1)
                pe.wait_ge(dve_done, at("dve", "F.act", n))
                if f == 0:
                    pe.wait_ge(dve_done, at("dve", "F.x", hf * GT - 1) if hf else at("dve", "E.output", B - 1, TPB - 1))
                for tt in range(HALF // P):
                    last = mm(bank(6 + tt // 2)[:, 0, (tt % 2) * D:(tt % 2) * D + D], acf[0:m, n % 3, tt * P:tt * P + P], wd[0:m, f, :],
                              f == 0 and tt % 2 == 0, f == FB - 1, skip_group_check=True)
                PEs(last.then_inc(pe_done, 1), "F.down", n)
                for kind, i in router.get(n, []):
                    if kind == "rows":
                        if i > BPH:
                            pe.wait_ge(act_done, at("act", "F.xT", i - 1))
                        f_rows(i, 5)
                    elif kind == "logits":
                        f_logits(i, 5)
                    else:
                        f_turned(i, 5)
    return book


def kernel(**inputs):
    import ml_dtypes
    from concourse import bacc
    from concourse.bass_utils import run_bass_kernel_spmd

    f = {k: np.asarray(v) for k, v in inputs.items()}
    bf = ml_dtypes.bfloat16

    def turned(name):
        return np.ascontiguousarray(f[name].T)

    def by_row(name):
        return f[name].reshape(IB, P).T

    inv = (1.0 / 10000.0 ** (np.arange(0, ROT, 2, dtype=np.float32) / ROT)).astype(np.float32)
    ang = np.repeat(np.arange(S, dtype=np.float32)[:, None] * inv[None, :], 2, axis=1)
    cos, sin = np.cos(ang), np.sin(ang) * np.tile(np.array([-1.0, 1.0], np.float32), ROT // 2)
    rope = np.stack([cos, sin], 1).astype(np.float32).reshape(TPB, P, 1, 2, ROT)
    rope = np.concatenate([rope * np.float32(DH0 ** -0.5), rope], axis=2).transpose(1, 0, 2, 3, 4)
    r = np.arange(96)[:, None, None] % (2 * NST) == np.arange(2 * NST)[None, :, None]
    selbc = np.broadcast_to(r, (96, 2 * NST, P)).astype(bf)
    which = np.minimum(np.arange(FB * P) // F1, E1)
    sel27 = (np.arange(27)[:, None] % (E1 + 1) == which[None, :]).astype(bf)
    tri = (np.arange(P)[:, None] < np.arange(P)[None, :]).astype(bf)
    wd = np.concatenate([f["L1_ffn_Wd"].reshape(E1 * F1, D), f["L1_ffn_Sd"], np.zeros((FB * P - FT, D), np.float32)])

    w_out = np.zeros((4, 32, 4, D), np.float32)
    w_out[:, :DH0] = f["L0_attn_W_out"].reshape(4, 4, DH0, D).transpose(1, 2, 0, 3)
    w_out = w_out.reshape(P, 4, D)

    def flat(e, shared):
        return np.concatenate([f[e].transpose(1, 0, 2).reshape(D, E1 * F1), f[shared]], axis=1)

    arrays = {
        "x": f["x"], "ctx": f["ctx_1024"], "mask": f["mask_BxS2_bf1"].view(np.uint8),
        "ident": np.eye(P, dtype=np.float32),
        "lnw": np.stack([f[n].reshape(DB, P).T for n in ("L0_attn_ln_w", "L0_attn_ln_b", "L0_ffn_norm_w", "L1_attn_norm_w")], 1),
        "wq0T": turned("L0_xattn_Wq"), "wk0T": turned("L0_xattn_Wk"),
        "bqk": np.stack([f["L0_xattn_bq"], f["L0_xattn_bk"]], 1),
        "w_in": f["L0_attn_W_in"], "w_out": w_out, "rope": rope,
        "iota32": np.broadcast_to(np.arange(E0, dtype=np.float32), (P, E0)), "tri": tri,
        "tokid": np.arange(T, dtype=np.uint32).reshape(TILES, P).T, "norm_w": f["L0_ffn_norm_w"],
        "gate_wT": turned("L0_ffn_gate_w"), "sgate": f["L0_ffn_shared_gate_w"], "sup": f["L0_ffn_shared_up_w"],
        "sdown": f["L0_ffn_shared_down_w"], "w13": f["L0_ffn_w13"], "w2": f["L0_ffn_w2"],
        "in_projT": turned("L1_attn_in_proj_w"), "x_projT": turned("L1_attn_x_proj_w"), "out_projT": turned("L1_attn_out_proj_w"),
        "conv_w": f["L1_attn_conv_w"].reshape(DI, KC), "conv_b": by_row("L1_attn_conv_b"), "dt_w": by_row("L1_attn_dt_w"),
        "dt_b": by_row("L1_attn_dt_b"), "D_param": by_row("L1_attn_D_param"), "A_log": f["L1_attn_A_log"], "selbc": selbc,
        "wq1": f["L1_xattn_Wq"], "wk1": f["L1_xattn_Wk"], "wv1": f["L1_xattn_Wv"], "wo1": f["L1_xattn_Wo"],
        "wg": flat("L1_ffn_Wg", "L1_ffn_Sg"), "wu": flat("L1_ffn_Wu", "L1_ffn_Su"),
        "wd": wd.reshape(FB, P, D).transpose(1, 0, 2), "wr": np.concatenate([f["L1_ffn_Wr"], f["L1_ffn_Wsg"]], axis=1),
        "sel27": sel27,
    }
    arrays = {k: np.ascontiguousarray(v) for k, v in arrays.items()}

    def emitted(known):
        nc = bacc.Bacc("TRN2", target_bir_lowering=False, num_devices=1)
        ins = {k: nc.dram_tensor("in_" + k, v.shape, mybir.dt.from_np(v.dtype), kind="ExternalInput").ap() for k, v in arrays.items()}
        out = nc.dram_tensor("out", (B, S, D), F32, kind="ExternalOutput").ap()
        return nc, decoder(nc, ins, out, known)

    _, steps = emitted(None)
    nc, again = emitted(steps)
    assert again == steps
    res = run_bass_kernel_spmd(nc, [{"in_" + k: v for k, v in arrays.items()}], core_ids=[0])
    return res.results[0]["out"]
```
